# Optimizing a Trainium2 kernel written in Bass

```python
import numpy as np
import jax
import jax.numpy as jnp

def _softmax(x, axis=-1):
    return jax.nn.softmax(x, axis=axis)

def _gelu(x):
    return jax.nn.gelu(x, approximate=True)

def _silu(x):
    return jax.nn.silu(x)

def _sigmoid(x):
    return jax.nn.sigmoid(x)

def _layernorm(x, axis=-1, eps=1e-05):
    m = jnp.mean(x, axis=axis, keepdims=True)
    v = jnp.var(x, axis=axis, keepdims=True)
    return (x - m) / jnp.sqrt(v + eps)

def _scatter_add(tgt, idx, src, axis=0):
    return tgt.at[idx].add(src)

def _segment_sum(src, seg, n):
    return jax.ops.segment_sum(src, seg, n)
kernel_name = 'mk_flamingo_gated_d1_seqx_r4_fa72eb'

def setup_inputs(seed: int=0):
    np.random.seed(seed)
    _w = jnp.asarray

    def _rec_inputs():
        import jax
        import jax.numpy as jnp
        _rk = jax.random.key(seed)
        x = 7.22e-05 + 1 * jax.random.normal(jax.random.fold_in(_rk, 1), (8, 512, 256), jnp.float32)
        _lenS = 512 - jax.random.randint(jax.random.fold_in(_rk, 7), (8,), 0, max(1, 512 // 4) + 1, jnp.int32)
        _lenS2 = 512 - jax.random.randint(jax.random.fold_in(_rk, 8), (8,), 0, max(1, 512 // 4) + 1, jnp.int32)
        _ctx_768P = jax.random.normal(jax.random.fold_in(_rk, 11), (8, 16, 192), jnp.float32)
        _ctx_768c = jax.random.dirichlet(jax.random.fold_in(_rk, 511), 0.3 * jnp.ones((16,), jnp.float32), (8, 512))
        _ctx_768t = jnp.einsum('bsk,bkd->bsd', _ctx_768c, _ctx_768P)
        _ctx_768t = _ctx_768t * jax.lax.rsqrt(jnp.mean(jnp.square(_ctx_768t)) + 1e-12) * 0.953939
        ctx_768 = -0.000191848 + 0.999787 * (_ctx_768t + 0.3 * jax.random.normal(jax.random.fold_in(_rk, 611), (8, 512, 192), jnp.float32))
        _g = jax.random.normal(jax.random.fold_in(_rk, 9001), (2, 1), jnp.float32)
        _g = jnp.sign(_g) * jnp.maximum(jnp.abs(_g), 1.0) + (_g == 0) * 1.0
        g_xattn = _g[0]
        g_ffn = _g[1]
        return (x, ctx_768, g_xattn, g_ffn)
    x, ctx_768, g_xattn, g_ffn = _rec_inputs()

    def _L0_xattn_setup():
        import jax, jax.numpy as jnp
        import numpy as np
        NUM_HEADS = 16
        CLAMP = 10000.0
        key = jax.random.key(seed)
        ks = jax.random.split(key, 8)
        B, Nq, Nkv, Cq, Ckv = (4, 512, 512, 256, 192)
        s_q = 1.0 / np.sqrt(Cq)
        s_kv = 1.0 / np.sqrt(Ckv)
        return {'query': jax.random.normal(ks[0], (B, Nq, Cq), jnp.float32), 'key_value': jax.random.normal(ks[1], (B, Nkv, Ckv), jnp.float32), 'Wq': jax.random.normal(ks[2], (Cq, Cq), jnp.float32) * s_q, 'bq': jnp.zeros((Cq,), jnp.float32), 'Wk': jax.random.normal(ks[3], (Ckv, Cq), jnp.float32) * s_kv, 'bk': jnp.zeros((Cq,), jnp.float32), 'Wv': jax.random.normal(ks[4], (Ckv, Cq), jnp.float32) * s_kv, 'bv': jnp.zeros((Cq,), jnp.float32), 'Wo': jax.random.normal(ks[5], (Cq, Cq), jnp.float32) * s_q, 'bo': jnp.zeros((Cq,), jnp.float32)}
    _L0_xattn_all = _L0_xattn_setup()
    _L0_xattn_in = {k: v for k, v in _L0_xattn_all.items() if k in ('Wq', 'bq', 'Wk', 'bk', 'Wv', 'bv', 'Wo', 'bo')}
    del _L0_xattn_all

    def _L0_ffn_setup():
        import jax, jax.numpy as jnp
        import numpy as np
        B, L, D = (4, 256, 256)
        E, H = (8, 1024)
        CAPACITY = 6
        key = jax.random.key(seed)
        ks = jax.random.split(key, 6)
        x = jax.random.normal(ks[0], (B, L, D), dtype=jnp.float32)
        gate_weight = jax.random.normal(ks[1], (E, D), dtype=jnp.float32) * 0.006
        w1 = jax.random.normal(ks[2], (E, H, D), dtype=jnp.float32) * 0.02
        b1 = jnp.zeros((E, H), dtype=jnp.float32)
        w2 = jax.random.normal(ks[3], (E, D, H), dtype=jnp.float32) * 0.02
        b2 = jnp.zeros((E, D), dtype=jnp.float32)
        return {'x': x, 'gate_weight': gate_weight, 'w1': w1, 'b1': b1, 'w2': w2, 'b2': b2}
    _L0_ffn_all = _L0_ffn_setup()
    _L0_ffn_in = {k: v for k, v in _L0_ffn_all.items() if k in ('gate_weight', 'w1', 'b1', 'w2', 'b2')}
    del _L0_ffn_all
    return {'x': x, 'ctx_768': ctx_768, 'g_xattn': g_xattn, 'g_ffn': g_ffn, 'L0_xattn_Wq': _L0_xattn_in['Wq'], 'L0_xattn_bq': _L0_xattn_in['bq'], 'L0_xattn_Wk': _L0_xattn_in['Wk'], 'L0_xattn_bk': _L0_xattn_in['bk'], 'L0_xattn_Wv': _L0_xattn_in['Wv'], 'L0_xattn_bv': _L0_xattn_in['bv'], 'L0_xattn_Wo': _L0_xattn_in['Wo'], 'L0_xattn_bo': _L0_xattn_in['bo'], 'L0_ffn_gate_weight': _L0_ffn_in['gate_weight'], 'L0_ffn_w1': _L0_ffn_in['w1'], 'L0_ffn_b1': _L0_ffn_in['b1'], 'L0_ffn_w2': _L0_ffn_in['w2'], 'L0_ffn_b2': _L0_ffn_in['b2']}

def reference(x, ctx_768, g_xattn, g_ffn, L0_xattn_Wq, L0_xattn_bq, L0_xattn_Wk, L0_xattn_bk, L0_xattn_Wv, L0_xattn_bv, L0_xattn_Wo, L0_xattn_bo, L0_ffn_gate_weight, L0_ffn_w1, L0_ffn_b1, L0_ffn_w2, L0_ffn_b2):
    import jax
    import jax.numpy as jnp

    def _L0_xattn_ref(query, key_value, Wq, bq, Wk, bk, Wv, bv, Wo, bo):
        import jax, jax.numpy as jnp
        import numpy as np
        NUM_HEADS = 16
        CLAMP = 10000.0
        B, Nq, Cq = query.shape
        Nkv = key_value.shape[1]
        H = NUM_HEADS
        D = Cq // H
        scale = D ** (-0.5)
        q = (query @ Wq + bq).reshape(B, Nq, H, D).transpose(0, 2, 1, 3)
        k = (key_value @ Wk + bk).reshape(B, Nkv, H, D).transpose(0, 2, 1, 3)
        v = (key_value @ Wv + bv).reshape(B, Nkv, H, D).transpose(0, 2, 1, 3)
        attn = jnp.einsum('bhqd,bhkd->bhqk', q, k) * scale
        attn = jnp.clip(attn, -CLAMP, CLAMP)
        attn = jax.nn.softmax(attn, axis=-1)
        attn = jnp.where(jnp.any(jnp.isnan(attn)), jnp.asarray(1.0 / Nkv, attn.dtype), attn)
        x = jnp.einsum('bhqk,bhkd->bqhd', attn, v).reshape(B, Nq, Cq)
        return x @ Wo + bo

    def _L0_ffn_ref(x, gate_weight, w1, b1, w2, b2):
        import jax, jax.numpy as jnp
        import numpy as np
        B, L, D = (4, 256, 256)
        E, H = (8, 1024)
        CAPACITY = 6
        logits = jnp.einsum('bld,ed->ble', x, gate_weight)
        expert_k = B * L * CAPACITY
        kth_val = jnp.sort(logits.reshape(-1))[expert_k - 1]
        mask = (logits >= kth_val).astype(x.dtype)
        gates = logits * mask
        h = jax.nn.gelu(jnp.einsum('bld,ehd->bleh', x, w1) + b1, approximate=True)
        y = jnp.einsum('bleh,edh->blde', h, w2) + b2.T[None, None]
        out = jnp.einsum('blde,ble->bld', y, gates)
        return out
    x = x + jnp.tanh(g_xattn[0]) * _L0_xattn_ref(_layernorm(x, axis=-1), ctx_768, L0_xattn_Wq, L0_xattn_bq, L0_xattn_Wk, L0_xattn_bk, L0_xattn_Wv, L0_xattn_bv, L0_xattn_Wo, L0_xattn_bo)
    x = x + jnp.tanh(g_ffn[0]) * _L0_ffn_ref(_layernorm(x, axis=-1), L0_ffn_gate_weight, L0_ffn_w1, L0_ffn_b1, L0_ffn_w2, L0_ffn_b2)
    return x

_drawn_inputs = setup_inputs


def setup_inputs(seed=0):
    import zlib

    import numpy as np

    out = dict(_drawn_inputs(seed))
    spreads = {'L0_xattn_bq': (0.0, 0.511),
     'L0_xattn_bk': (0.0, 0.8),
     'L0_xattn_bv': (0.0, 0.1),
     'L0_xattn_bo': (0.0, 0.1),
     'L0_ffn_b1': (0.0, 0.8),
     'L0_ffn_b2': (0.0, 0.387)}
    factors = {}
    for name, (base, spread) in spreads.items():
        noise = np.random.default_rng([zlib.crc32(name.encode()), seed]).standard_normal(out[name].shape)
        drawn = base * np.exp(spread * noise) if base else spread * noise
        out[name] = jnp.asarray(drawn.astype(out[name].dtype))
    for name, factor in factors.items():
        out[name] = (out[name] * factor).astype(out[name].dtype)
    return out
```

```python
from contextlib import ExitStack

import concourse.bass as bass
from concourse import mybir

F32 = mybir.dt.float32
F32R = mybir.dt.float32r
I32 = mybir.dt.int32
ALU = mybir.AluOpType
ACT = mybir.ActivationFunctionType
AX_X = mybir.AxisListType.X

P = 128
BATCH, SEQ, DIM = 8, 512, 256
CTX = 192
TOKENS = BATCH * SEQ
HEADS, HDIM = 16, 16
CLAMP = 10000.0
EXPERTS, HIDDEN = 8, 1024
EPS = 1e-5
KEPT_FROM = 4 * 256 * 6 - 1
KT = DIM // P
TT = SEQ // P
GROUP = 4
GROUPS = HEADS // GROUP
VW = 32
ROWS = 1 + 3 * HDIM
FITS = CLAMP - 104.0
SUM_LEAST = 0.01
HT = HIDDEN // P


def wait(eng, sem, value):
    if isinstance(value, int) and value <= 0:
        return
    eng.wait_ge(sem, value)


class Names:

    def __init__(self, nc, ctx):
        self.nc, self.ctx = nc, ctx

    def sb(self, name, shape, dt=F32):
        return self.ctx.enter_context(self.nc.sbuf_tensor(name, shape, dt))

    def ps(self, name, shape):
        return self.ctx.enter_context(self.nc.psum_tensor(name, shape, F32))

    def sem(self, name):
        return self.ctx.enter_context(self.nc.semaphore(name))


def build_project(nc, io, scratch, keep):
    with ExitStack() as ctx:
        n = Names(nc, ctx)
        wq = n.sb("wq", [P, KT, DIM])
        wk = n.sb("wk", [P, KT, DIM])
        wv = n.sb("wv", [P, KT, DIM])
        bq = n.sb("bq_col", [P, KT])
        bq_scaled = n.sb("bq_scaled", [P, KT])
        gates_in = n.sb("gates_in", [P, 2])
        eps = n.sb("eps_a", [P, 1])
        x_t = [n.sb(f"x_t{i}", [P, TT, DIM]) for i in range(2)]
        ctx_t = [n.sb(f"ctx_t{i}", [P, KT, SEQ]) for i in range(2)]
        stats = n.sb("stats_a", [P, TT, 6])
        meanvar = n.sb("meanvar_a", [P, 4, TT])
        std = n.sb("std_a", [P, TT])
        newton = n.sb("newton_a", [P, 4, TT])
        xn = [n.sb(f"xn_a{i}", [P, TT, DIM]) for i in range(2)]
        xn_T = n.sb("xn_T_a", [P, KT, SEQ])
        q_full = n.sb("q_full", [P, KT, SEQ])
        k_full = n.sb("k_full", [P, KT, SEQ])
        q_hl = [n.sb(f"q_hl{i}", [P, 2, KT, SEQ], F32R) for i in range(2)]
        k_hl = [n.sb(f"k_hl{i}", [P, 2, KT, SEQ], F32R) for i in range(2)]
        v_out = [n.sb(f"v_out{i}", [P, TT, HEADS, VW]) for i in range(2)]
        const_rows = n.sb("const_rows", [P, 2, SEQ])
        ps_x = n.ps("ps_x", [P, KT, SEQ])
        ps_q = n.ps("ps_q", [P, KT, SEQ])
        ps_k = n.ps("ps_k", [P, KT, SEQ])
        ps_v = n.ps("ps_v", [P, TT, DIM])

        zeroed = n.sem("a_zeroed")
        const_rows_set = n.sem("a_const_rows_set")
        consts_moved = n.sem("a_consts_moved")
        ones_set = n.sem("a_ones_set")
        ident_set = n.sem("a_ident_set")
        w_loaded = n.sem("a_w_loaded")
        small_loaded = n.sem("a_small_loaded")
        x_loaded = [n.sem(f"a_x_loaded{i}") for i in range(2)]
        ctx_loaded = [n.sem(f"a_ctx_loaded{i}") for i in range(2)]
        bq_ready = n.sem("a_bq_ready")
        eps_set = n.sem("a_eps_set")
        stats_done = n.sem("a_stats_done")
        std_done = n.sem("a_std_done")
        newton_done = n.sem("a_newton_done")
        xn_ready = n.sem("a_xn_ready")
        xT_in_psum = n.sem("a_xT_in_psum")
        xT_ready = n.sem("a_xT_ready")
        q_in_psum = n.sem("a_q_in_psum")
        k_in_psum = n.sem("a_k_in_psum")
        v_in_psum = n.sem("a_v_in_psum")
        q_full_ready = n.sem("a_q_full_ready")
        k_full_ready = n.sem("a_k_full_ready")
        hi_done = n.sem("a_hi_done")
        q_split = n.sem("a_q_split")
        k_split = n.sem("a_k_split")
        v_ready = n.sem("a_v_ready")
        stored = [n.sem(f"a_stored{i}") for i in range(2)]
        block = ctx.enter_context(nc.Block())
        rest = CTX - P
        STORES = 16 * (2 * 3 * KT + 1)

        @block.sync
        def _(sp):
            sp.dma_start(gates_in[:, 0:1], io["g_xattn"].rearrange("(a b) -> a b", a=1).to_broadcast([P, 1])).then_inc(small_loaded, 16)
            sp.dma_start(gates_in[:, 1:2], io["g_ffn"].rearrange("(a b) -> a b", a=1).to_broadcast([P, 1])).then_inc(small_loaded, 16)
            sp.dma_start(bq[:], io["bq"]).then_inc(small_loaded, 16)
            sp.dma_start(wq[:], io["Wq"].rearrange("(k p) n -> p k n", p=P)).then_inc(w_loaded, 16)
            sp.dma_start(keep["wo"][:], io["Wo"].rearrange("(k p) n -> p k n", p=P)).then_inc(consts_moved, 16)
            sp.wait_ge(zeroed, 2)
            for w, w_in, b_in in ((wk, "Wk", "bk"), (wv, "Wv", "bv")):
                sp.dma_start(w[:, 0, :], io[w_in][0:P, :]).then_inc(w_loaded, 16)
                sp.dma_start(w[0:rest, 1, :], io[w_in][P:CTX, :]).then_inc(w_loaded, 16)
                sp.dma_start(w[rest:rest + 1, 1, :], io[b_in].rearrange("(a n) -> a n", a=1)).then_inc(w_loaded, 16)

            def load(bb, p):
                b = bb * 2 + p
                wait(sp, xn_ready, b - 1)
                sp.dma_start(x_t[p][:], io["x"][bass.ds(b * SEQ, SEQ), :].rearrange("(t p) d -> p t d", p=P)).then_inc(x_loaded[p], 16)
                wait(sp, v_in_psum, b - 1)
                sp.dma_start(ctx_t[p][:, 0, :], io["ctxT"][bass.ds(b, 1), 0:P, :].rearrange("a c t -> (a c) t")).then_inc(ctx_loaded[p], 16)
                sp.dma_start(ctx_t[p][0:rest, 1, :], io["ctxT"][bass.ds(b, 1), P:CTX, :].rearrange("a c t -> (a c) t")).then_inc(ctx_loaded[p], 16)

            def store(bb, p):
                b = bb * 2 + p
                for name, tile, ready, parts in (("k", k_hl[p], k_split, (0, 0, 1)), ("q", q_hl[p], q_split, (0, 1, 0))):
                    sp.wait_ge(ready, b + 1)
                    rows = scratch[name][bass.ds(b, 1)].rearrange("a (k h r) t -> h r (a k) t", k=KT, r=ROWS)
                    for c, part in enumerate(parts):
                        for k in range(KT):
                            sp.dma_start(rows[:, 1 + c * HDIM:1 + (c + 1) * HDIM, k], tile[:, part, k].bitcast(F32)).then_inc(stored[p], 16)
                sp.wait_ge(v_ready, b + 1)
                sp.dma_start(scratch["v"][bass.ds(b, 1), :, :].rearrange("a p n -> p (a n)"),
                             v_out[p][:].rearrange("p t h w -> p (t h w)")).then_inc(stored[p], 16)

            for p in range(2):
                load(0, p)
            sp.wait_ge(const_rows_set, 2)
            for i, name in enumerate(("q", "k")):
                sp.dma_start(scratch[name].rearrange("b (h r) t -> (b h) r t", r=ROWS)[:, 0, :], const_rows[:, i, :]).then_inc(consts_moved, 16)
            with sp.Fori(0, BATCH // 2 - 1) as bb:
                for p in range(2):
                    store(bb, p)
                    load(bb + 1, p)
            for p in range(2):
                store(BATCH // 2 - 1, p)
            for p in range(2):
                sp.wait_ge(stored[p], STORES * BATCH // 2)
            sp.wait_ge(consts_moved, 48)

        @block.gpsimd
        def _(pool):
            pool.memset(wk[rest:P, 1, :], 0.0).then_inc(zeroed, 1)
            pool.memset(wv[rest:P, 1, :], 0.0).then_inc(zeroed, 1)
            for p in range(2):
                pool.memset(ctx_t[p][rest:P, 1, :], 0.0).then_inc(zeroed, 1)
            pool.wait_ge(zeroed, 4)
            for p in range(2):
                pool.memset(ctx_t[p][rest:rest + 1, 1, :], 1.0).then_inc(ones_set, 1)
            pool.wait_ge(ones_set, 2)
            pool.memset(keep["ident"][:], 0.0).then_inc(ident_set, 1)
            pool.wait_ge(ident_set, 1)
            pool.affine_select(out=keep["ident"][:], in_=keep["ident"][:], compare_op=ALU.not_equal, fill=1.0,
                               base=0, pattern=[[-1, P]], channel_multiplier=1).then_inc(ident_set, 1)
            pool.wait_ge(ident_set, 2)
            for p in range(2):
                pool.memset(v_out[p][:], 1.0).then_inc(ones_set, 1)
            for i in range(2):
                pool.memset(const_rows[:, i, :], float(i)).then_inc(const_rows_set, 1)
            for s in range(GROUPS):
                pool.memset(keep["q_st"][s][:].bitcast(F32), 0.0)
                pool.memset(keep["k_st"][s][:].bitcast(F32), 0.0)

        @block.tensor
        def _(pe):
            pe.wait_ge(ident_set, 2)
            pe.wait_ge(ones_set, 2)
            pe.wait_ge(w_loaded, 16 * 7)

            def batch(bb, p):
                b = bb * 2 + p
                pe.wait_ge(ctx_loaded[p], bb * 32 + 32)
                wait(pe, k_full_ready, b)
                for m in range(KT):
                    for k in range(KT):
                        mm = pe.matmul(ps_k[:, m, :], wk[:, k, m * P:(m + 1) * P], ctx_t[p][:, k, :],
                                       start=(k == 0), stop=(k == KT - 1))
                mm.then_inc(k_in_psum, 1)
                wait(pe, v_ready, b)
                for t in range(TT):
                    for k in range(KT):
                        mm = pe.matmul(ps_v[:, t, :], ctx_t[p][:, k, t * P:(t + 1) * P], wv[:, k, :],
                                       start=(k == 0), stop=(k == KT - 1))
                mm.then_inc(v_in_psum, 1)
                pe.wait_ge(xn_ready, b + 1)
                wait(pe, xT_ready, b)
                for k in range(KT):
                    for t in range(TT):
                        mm = pe.transpose(ps_x[:, k, t * P:(t + 1) * P], xn[p][:, t, k * P:(k + 1) * P], keep["ident"][:])
                mm.then_inc(xT_in_psum, 1)
                pe.wait_ge(xT_ready, b + 1)
                wait(pe, q_full_ready, b * 2)
                for m in range(KT):
                    for k in range(KT):
                        mm = pe.matmul(ps_q[:, m, :], wq[:, k, m * P:(m + 1) * P], xn_T[:, k, :],
                                       start=(k == 0), stop=(k == KT - 1))
                mm.then_inc(q_in_psum, 1)

            for p in range(2):
                batch(0, p)
            with pe.Fori(1, BATCH // 2) as bb:
                for p in range(2):
                    batch(bb, p)

        @block.scalar
        def _(act):
            act.wait_ge(small_loaded, 48)
            act.activation(keep["tanh_g"][:], gates_in[:], ACT.Tanh)
            act.activation(bq_scaled[:], bq[:], ACT.Copy, scale=-(HDIM ** -0.5)).then_inc(bq_ready, 1)
            act.wait_ge(bq_ready, 1)
            act.wait_ge(eps_set, 1)

            def batch(bb, p):
                b = bb * 2 + p
                act.wait_ge(k_in_psum, b + 1)
                wait(act, k_split, b)
                act.activation(k_full[:], ps_k[:], ACT.Copy).then_inc(k_full_ready, 1)
                act.wait_ge(stats_done, b * 4 + 4)
                act.activation(std[:], meanvar[:, 1, :], ACT.Sqrt, bias=eps[:, 0:1]).then_inc(std_done, 1)
                act.wait_ge(xT_in_psum, b + 1)
                wait(act, q_in_psum, b)
                act.activation(xn_T[:], ps_x[:], ACT.Copy).then_inc(xT_ready, 1)
                act.wait_ge(q_in_psum, b + 1)
                wait(act, q_split, b)
                for m in range(KT):
                    act.activation(q_full[:, m, :], ps_q[:, m, :], ACT.Identity, bias=bq_scaled[:, m:m + 1],
                                   scale=-(HDIM ** -0.5)).then_inc(q_full_ready, 1)

            for p in range(2):
                batch(0, p)
            with act.Fori(1, BATCH // 2) as bb:
                for p in range(2):
                    batch(bb, p)

        @block.vector
        def _(dve):
            dve.memset(eps[:], EPS).then_inc(eps_set, 1)
            dve.wait_ge(eps_set, 1)
            dve.wait_ge(ones_set, 4)

            def split(full, hl, done, count):
                dve.tensor_copy(hl[:, 0], full[:]).then_inc(hi_done, 1)
                dve.wait_ge(hi_done, count)
                dve.tensor_tensor(hl[:, 1], full[:], hl[:, 0].bitcast(F32), ALU.subtract).then_inc(done, 1)

            def batch(bb, p):
                b = bb * 2 + p
                dve.wait_ge(x_loaded[p], bb * 16 + 16)
                wait(dve, xn_ready, b)
                mean_variance(dve, [x_t[p][:, t, :] for t in range(TT)], stats, meanvar, stats_done, b)
                dve.wait_ge(std_done, b + 1)
                rstd = reciprocal_root(dve, std[:], meanvar[:, 1, :], newton, newton_done, b)
                wait(dve, xT_in_psum, b - 1)
                for t in range(TT):
                    ins = dve.tensor_scalar(xn[p][:, t, :], x_t[p][:, t, :], meanvar[:, 0, t:t + 1], rstd[:, t:t + 1],
                                            ALU.subtract, ALU.mult)
                ins.then_inc(xn_ready, 1)
                wait(dve, stored[p], bb * STORES)
                dve.wait_ge(k_full_ready, b + 1)
                split(k_full, k_hl[p], k_split, b * 2 + 1)
                dve.wait_ge(v_in_psum, b + 1)
                dve.tensor_copy(v_out[p][:, :, :, 0:HDIM],
                                ps_v[:].rearrange("p t (h d) -> p t h d", h=HEADS)).then_inc(v_ready, 1)
                dve.wait_ge(q_full_ready, b * 2 + 2)
                split(q_full, q_hl[p], q_split, b * 2 + 2)

            for p in range(2):
                batch(0, p)
            with dve.Fori(1, BATCH // 2) as bb:
                for p in range(2):
                    batch(bb, p)


def mean_variance(dve, tiles, stats, meanvar, done, b):
    size = tiles[0].shape[-1]
    for t, tile in enumerate(tiles):
        ins = dve.bn_stats(stats[:, t, :], tile)
    ins.then_inc(done, 1)
    dve.wait_ge(done, b * 4 + 1)
    mean, var, diff, dev = (meanvar[:, i, :] for i in range(4))
    dve.tensor_tensor(mean, stats[:, :, 1], stats[:, :, 4], ALU.add)
    dve.tensor_tensor(diff, stats[:, :, 1], stats[:, :, 4], ALU.subtract)
    dve.tensor_tensor(dev, stats[:, :, 2], stats[:, :, 5], ALU.add).then_inc(done, 1)
    dve.wait_ge(done, b * 4 + 2)
    dve.tensor_scalar(mean, mean, 0.5, None, ALU.mult)
    dve.tensor_scalar(dev, dev, 1.0 / size, None, ALU.mult)
    dve.scalar_tensor_tensor(out=diff, in0=diff, scalar=0.25, in1=diff, op0=ALU.mult, op1=ALU.mult).then_inc(done, 1)
    dve.wait_ge(done, b * 4 + 3)
    dve.tensor_tensor(var, dev, diff, ALU.add).then_inc(done, 1)


def reciprocal_root(dve, std, var, newton, done, b):
    first, square, scaled, result = (newton[:, i, :] for i in range(4))
    dve.reciprocal(first, std).then_inc(done, 1)
    dve.wait_ge(done, b * 5 + 1)
    dve.tensor_tensor(square, first, first, ALU.mult).then_inc(done, 1)
    dve.wait_ge(done, b * 5 + 2)
    dve.scalar_tensor_tensor(out=scaled, in0=var, scalar=EPS, in1=square, op0=ALU.add, op1=ALU.mult).then_inc(done, 1)
    dve.wait_ge(done, b * 5 + 3)
    dve.tensor_scalar(square, scaled, -0.5, 1.5, ALU.mult, ALU.add).then_inc(done, 1)
    dve.wait_ge(done, b * 5 + 4)
    dve.tensor_tensor(result, first, square, ALU.mult).then_inc(done, 1)
    dve.wait_ge(done, b * 5 + 5)
    return result


SHARED = {
    (0, 0): ("low", 0, 1), (0, 2): ("out", -1, 3),
    (1, 0): ("rows", -1, 0), (1, 1): ("low", 0, 2), (1, 2): ("rows", -1, 1), (1, 3): ("out", 0, 0),
    (2, 0): ("low", 0, 3), (2, 1): ("y", -1, 0), (2, 2): ("out", 0, 1), (2, 3): ("y", -1, 1),
    (3, 0): ("low", 1, 0), (3, 2): ("out", 0, 2),
}
SHARED_ORDER = [SHARED[at] for at in sorted(SHARED)]
UNITS_OF = {"low": GROUPS, "out": GROUPS, "rows": KT, "y": 2}


def exists(b):
    return not isinstance(b, int) or 0 <= b < BATCH


def unit_no(kind, b, i):
    return b * UNITS_OF[kind] + i


def unit_before(b, unit):
    at = SHARED_ORDER.index(unit)
    for back in range(1, 2 * len(SHARED_ORDER) + 1):
        kind, off, i = SHARED_ORDER[(at - back) % len(SHARED_ORDER)]
        owner = b + (at - back) // len(SHARED_ORDER) + off
        if exists(owner):
            return kind, unit_no(kind, owner, i)


def group_after(b, g, steps):
    return b + (g + steps) // GROUPS, (g + steps) % GROUPS


def build_attend(nc, io, scratch, keep):
    with ExitStack() as ctx:
        n_ = Names(nc, ctx)
        ident = keep["ident"]
        q_st, k_st, wo = keep["q_st"], keep["k_st"], keep["wo"]
        v_st = [n_.sb(f"v_st{i}", [P, TT, GROUP, VW]) for i in range(GROUPS)]
        bo_gated = n_.sb("bo_gated", [P, DIM])
        low = n_.sb("low", [P, 2, GROUP * TT])
        low_rows = n_.sb("low_rows", [GROUP * TT, P], F32R)
        probs_T = n_.sb("probs_T", [P, TT, GROUP, SEQ])
        o_sb = n_.sb("o_sb", [P, SEQ])
        recip = n_.sb("recip", [P, TT, GROUP])
        attn = n_.sb("attn", [P, TT, DIM])
        attn_T = n_.sb("attn_T", [P, KT, SEQ])
        x_res = n_.sb("x_res", [P, TT, DIM])
        fits = n_.sb("fits", [P, 3, GROUP * TT])
        fits_sum = n_.sb("fits_sum", [P, 1])
        ones = n_.sb("ones_b", [P, P])
        ps_s = [n_.ps(f"ps_s{i}", [P, 2, SEQ]) for i in range(2)]
        ps_t = [n_.ps(f"ps_t{i}", [P, SEQ]) for i in range(2)]
        ps_o = n_.ps("ps_o", [P, SEQ])
        ps_m = n_.ps("ps_m", [P, SEQ])

        consts_set = n_.sem("b_consts_set")
        bo_loaded = n_.sem("b_bo_loaded")
        bo_ready = n_.sem("b_bo_ready")
        qk_loaded = [n_.sem(f"b_qk_loaded{i}") for i in range(GROUPS)]
        v_loaded = [n_.sem(f"b_v_loaded{i}") for i in range(GROUPS)]
        scores_in_psum = n_.sem("b_scores_in_psum")
        low_done = n_.sem("b_low_done")
        rows_sent = n_.sem("b_rows_sent")
        t_in_psum = n_.sem("b_t_in_psum")
        exp_done = n_.sem("b_exp_done")
        pv_done = n_.sem("b_pv_done")
        o_copied = n_.sem("b_o_copied")
        in_psum = {kind: n_.sem(f"b_{kind}_in_psum") for kind in UNITS_OF}
        taken = {kind: n_.sem(f"b_{kind}_taken") for kind in UNITS_OF}
        recip_done = n_.sem("b_recip_done")
        lows_checked = n_.sem("b_lows_checked")
        x_loaded = n_.sem("b_x_loaded")
        x_biased = n_.sem("b_x_biased")
        x2_stored = n_.sem("b_x2_stored")
        fits_summed = n_.sem("b_fits_summed")
        fits_in_psum = n_.sem("b_fits_in_psum")
        block = ctx.enter_context(nc.Block())

        def head_no(b, g, j):
            return b * HEADS + g * GROUP + j

        def quad_no(b, g, k):
            return b * (GROUPS * TT) + g * TT + k

        def group_no(b, g):
            return b * GROUPS + g

        def batches(eng, batch):
            batch(0)
            with eng.Fori(1, BATCH - 1) as b:
                batch(b)
            batch(BATCH - 1)
            batch(BATCH)

        @block.sync
        def _(sp):
            def load_group(b, g):
                done = group_no(b, g) - GROUPS
                wait(sp, t_in_psum, (done + 1) * TT * GROUP)
                for name, dst in (("q", q_st[g]), ("k", k_st[g])):
                    src = scratch[name][bass.ds(b, 1)].rearrange("a (g k h r) t -> (a g) h r k t", g=GROUPS, k=2, h=2)
                    for half in range(2):
                        rows = slice(half * 64 + 64 - ROWS, half * 64 + 64)
                        to = dst[rows, :, :] if name == "q" else dst[rows, half:GROUP:2, :]
                        sp.dma_start(to.bitcast(F32), src[g, half]).then_inc(qk_loaded[g], 16)
                wait(sp, pv_done, (done + 1) * TT)
                src = scratch["v"][bass.ds(b, 1), :, :].rearrange("a p (t h w) -> (a p) t (h w)", t=TT, h=HEADS)
                sp.dma_start(v_st[g][:].rearrange("p t h w -> p t (h w)"),
                             src[:, :, g * GROUP * VW:(g + 1) * GROUP * VW]).then_inc(v_loaded[g], 16)

            def send_lows(b, g):
                sp.wait_ge(taken["low"], group_no(b, g) + 1)
                for half in range(2):
                    row = half * 64 + 64 - ROWS
                    sp.dma_start(q_st[g][row:row + 1].rearrange("a k (t q) -> a (k t) q", q=P).bitcast(F32),
                                 low_rows[half * 8:half * 8 + 8, :].bitcast(F32)).then_inc(rows_sent, 16)

            def batch(b):
                for g in range(GROUPS):
                    ahead = group_after(b, g, 3)
                    if exists(ahead[0]) and exists(b):
                        load_group(*ahead)
                    ahead = group_after(b, g, 1)
                    if exists(ahead[0]) and exists(b):
                        send_lows(*ahead)
                if exists(b - 1):
                    sp.wait_ge(taken["y"], b * 2)
                    sp.dma_start(scratch["x2"][bass.ds((b - 1) * SEQ, SEQ), :].rearrange("(t p) d -> p t d", p=P), x_res[:]).then_inc(x2_stored, 16)
                if exists(b):
                    wait(sp, x2_stored, b * 16)
                    sp.dma_start(x_res[:], io["x"][bass.ds(b * SEQ, SEQ), :].rearrange("(t p) d -> p t d", p=P)).then_inc(x_loaded, 16)

            load_group(0, 0)
            sp.dma_start(bo_gated[:], io["bo"].rearrange("(a n) -> a n", a=1).to_broadcast([P, DIM])).then_inc(bo_loaded, 16)
            for g in (1, 2):
                load_group(0, g)
            send_lows(0, 0)
            batches(sp, batch)
            sp.wait_ge(x2_stored, 16 * BATCH)

        @block.gpsimd
        def _(pool):
            pool.memset(ones[:], 1.0).then_inc(consts_set, 1)
            pool.memset(fits[:], 0.0).then_inc(consts_set, 1)
            pool.wait_ge(bo_ready, 1)
            with pool.Fori(0, BATCH) as b:
                pool.wait_ge(x_loaded, b * 16 + 16)
                pool.tensor_tensor(x_res[:], x_res[:], bo_gated[:].rearrange("p (a d) -> p a d", a=1)
                                   .to_broadcast([P, TT, DIM]), ALU.add).then_inc(x_biased, 1)

        @block.tensor
        def _(pe):
            def scores(b, g, j, u):
                n = head_no(b, g, j)
                if j == 0 and u == 0:
                    pe.wait_ge(qk_loaded[g], b * 64 + 64)
                wait(pe, low_done, 2 * n - 1 + u)
                for t in range(2):
                    q0 = (2 * u + t) * P
                    mm = pe.matmul(ps_s[u][:, t, :], q_st[g][:, j // 2, q0:q0 + P], k_st[g][:, j, :], start=True, stop=True)
                mm.then_inc(scores_in_psum, 1)

            def scores_T(b, g, k, j):
                n = quad_no(b, g, k) * GROUP + j
                if k == 0 and j == 0:
                    pe.wait_ge(rows_sent, group_no(b, g) * 32 + 32)
                wait(pe, exp_done, n - 1)
                pe.matmul(ps_t[j % 2][:], k_st[g][:, j, k * P:(k + 1) * P], q_st[g][:, j // 2, :],
                          start=True, stop=True).then_inc(t_in_psum, 1)

            def probs_v(b, g, k):
                n = quad_no(b, g, k)
                if k == 0:
                    pe.wait_ge(v_loaded[g], b * 16 + 16)
                    wait(pe, o_copied, group_no(b, g))
                pe.wait_ge(exp_done, n * GROUP + GROUP)
                for j in range(GROUP):
                    mm = pe.matmul(ps_o[32 * j:32 * j + 32, :], v_st[g][:, k, j, :], probs_T[:, k, j, :],
                                   start=(k == 0), stop=(k == TT - 1))
                mm.then_inc(pv_done, 1)

            def turn_lows(b, i):
                pe.wait_ge(low_done, group_no(b, i) * 2 * GROUP + 2 * GROUP)
                return pe.transpose(ps_m[0:GROUP * TT, 0:P], low[:, i % 2, :], ident[:])

            def turn_out(b, i):
                pe.wait_ge(o_copied, group_no(b, i) + 1)
                for t in range(TT):
                    mm = pe.transpose(ps_m[:, t * P:(t + 1) * P], o_sb[:, t * P:(t + 1) * P], ident[:])
                return mm

            def turn_rows(b, i):
                pe.wait_ge(taken["out"], group_no(b, GROUPS - 1) + 1)
                for t in range(TT):
                    mm = pe.transpose(ps_m[:, t * P:(t + 1) * P], attn[:, t, i * P:(i + 1) * P], ident[:])
                return mm

            def project_out(b, i):
                pe.wait_ge(taken["rows"], b * KT + KT)
                for t in range(2):
                    t0 = (2 * i + t) * P
                    for k in range(KT):
                        mm = pe.matmul(ps_m[:, t * DIM:(t + 1) * DIM], attn_T[:, k, t0:t0 + P], wo[:, k, :],
                                       start=(k == 0), stop=(k == KT - 1))
                return mm

            write = {"low": turn_lows, "out": turn_out, "rows": turn_rows, "y": project_out}

            def shared(b, unit):
                kind, off, i = unit
                before = unit_before(b, unit)
                pe.wait_ge(taken[before[0]], before[1] + 1)
                write[kind](b + off, i).then_inc(in_psum[kind], 1)

            def batch(b):
                for g in range(GROUPS):
                    ahead = group_after(b, g, 2)
                    for k in range(TT):
                        back = (b, g, k - 1) if k else (*group_after(b, g, -1), TT - 1)
                        more = exists(ahead[0]) and exists(b)
                        if exists(b):
                            scores_T(b, g, k, 0)
                        if more:
                            scores(*ahead, k, 0)
                        if exists(b):
                            scores_T(b, g, k, 1)
                        if exists(back[0]):
                            probs_v(*back)
                        if exists(b):
                            scores_T(b, g, k, 2)
                        if more:
                            scores(*ahead, k, 1)
                        if exists(b):
                            scores_T(b, g, k, 3)
                        unit = SHARED.get((g, k))
                        if unit and exists(b + unit[1]):
                            shared(b, unit)

            for g in range(2):
                for j in range(GROUP):
                    for u in range(2):
                        scores(0, g, j, u)
                if g == 0:
                    turn_lows(0, 0).then_inc(in_psum["low"], 1)
            batches(pe, batch)
            pe.wait_ge(fits_summed, 1)
            pe.matmul(ps_m[:, 0:1], ones[:], fits_sum[:], start=True, stop=True).then_inc(fits_in_psum, 1)

        @block.vector
        def _(dve):
            dve.wait_ge(consts_set, 2)
            dve.wait_ge(bo_loaded, 16)
            dve.tensor_scalar(bo_gated[:], bo_gated[:], keep["tanh_g"][:, 0:1], None, ALU.mult).then_inc(bo_ready, 1)

            def lows(b, g, j):
                n = head_no(b, g, j)
                if j == 0:
                    wait(dve, in_psum["low"], group_no(b, g) - 1)
                    wait(dve, lows_checked, group_no(b, g) - 1)
                for u in range(2):
                    dve.wait_ge(scores_in_psum, 2 * n + u + 1)
                    at = (j % 2) * 2 * TT + (j // 2) * TT + 2 * u
                    dve.tensor_reduce(low[:, g % 2, at:at + 2], ps_s[u][:], AX_X, ALU.min).then_inc(low_done, 1)

            def check_lows(b, g):
                dve.wait_ge(low_done, group_no(b, g) * 2 * GROUP + 2 * GROUP)
                wait(dve, lows_checked, group_no(b, g))
                dve.scalar_tensor_tensor(out=fits[:, 0, :], in0=low[:, g % 2, :], scalar=FITS, in1=fits[:, 0, :],
                                         op0=ALU.is_le, op1=ALU.add)
                dve.scalar_tensor_tensor(out=fits[:, 1, :], in0=low[:, g % 2, :], scalar=-FITS, in1=fits[:, 1, :],
                                         op0=ALU.is_ge, op1=ALU.add).then_inc(lows_checked, 1)

            def normalise(b, i):
                n = group_no(b, i)
                dve.wait_ge(in_psum["out"], n + 1)
                if i == 0:
                    wait(dve, in_psum["rows"], b * KT)
                wait(dve, taken["out"], n)
                heads = ps_m[:].rearrange("p (t j w) -> p t j w", t=TT, j=GROUP)
                dve.reciprocal(recip[:], heads[:, :, :, HDIM]).then_inc(recip_done, 1)
                count = fits[:, 2, :].rearrange("p (t j) -> p t j", t=TT)
                dve.scalar_tensor_tensor(out=count, in0=heads[:, :, :, HDIM], scalar=SUM_LEAST, in1=count,
                                         op0=ALU.is_ge, op1=ALU.add)
                dve.wait_ge(recip_done, n + 1)
                dve.tensor_tensor(attn[:, :, i * GROUP * HDIM:(i + 1) * GROUP * HDIM].rearrange("p t (j d) -> p t j d", j=GROUP),
                                  heads[:, :, :, 0:HDIM],
                                  recip[:].rearrange("p t (j a) -> p t j a", a=1).to_broadcast([P, TT, GROUP, HDIM]),
                                  ALU.mult).then_inc(taken["out"], 1)

            def add_residual(b, i):
                if i == 0:
                    dve.wait_ge(x_biased, b + 1)
                dve.wait_ge(in_psum["y"], b * 2 + i + 1)
                part = x_res[:, 2 * i:2 * i + 2, :]
                dve.scalar_tensor_tensor(out=part, in0=ps_m[:].rearrange("p (t d) -> p t d", t=2),
                                         scalar=keep["tanh_g"][:, 0:1], in1=part,
                                         op0=ALU.mult, op1=ALU.add).then_inc(taken["y"], 1)

            def batch(b):
                for g in range(GROUPS):
                    ahead = group_after(b, g, 2)
                    for k in range(TT):
                        if exists(ahead[0]) and exists(b):
                            lows(*ahead, k)
                        unit = SHARED.get((g, k))
                        if unit and unit[0] == "out" and exists(b + unit[1]):
                            normalise(b + unit[1], unit[2])
                        if unit and unit[0] == "y" and exists(b + unit[1]):
                            add_residual(b + unit[1], unit[2])
                    if exists(ahead[0]) and exists(b):
                        check_lows(*ahead)

            for g in range(2):
                for j in range(GROUP):
                    lows(0, g, j)
                check_lows(0, g)
            batches(dve, batch)
            dve.wait_ge(lows_checked, BATCH * GROUPS)
            dve.wait_ge(taken["out"], BATCH * GROUPS)
            dve.tensor_reduce(fits_sum[:], fits[:].rearrange("p a n -> p (a n)"), AX_X, ALU.add).then_inc(fits_summed, 1)
            dve.wait_ge(fits_in_psum, 1)
            dve.tensor_scalar(keep["clip_flag"][:], ps_m[:, 0:1], 3 * HEADS * TOKENS - 0.5, None, ALU.is_lt)

        @block.scalar
        def _(act):
            def exps(b, g, k):
                n = quad_no(b, g, k)
                wait(act, pv_done, n - TT + 1)
                for j in range(GROUP):
                    act.wait_ge(t_in_psum, n * GROUP + j + 1)
                    act.activation(probs_T[:, k, j, :], ps_t[j % 2][:], ACT.Exp, scale=-1.0).then_inc(exp_done, 1)

            def copy_out(b, g):
                act.wait_ge(pv_done, quad_no(b, g, TT - 1) + 1)
                wait(act, in_psum["out"], group_no(b, g))
                act.activation(o_sb[:], ps_o[:], ACT.Copy).then_inc(o_copied, 1)

            def take_lows(b, i):
                n = group_no(b, i)
                act.wait_ge(in_psum["low"], n + 1)
                wait(act, rows_sent, n * 32)
                act.activation(low_rows[:], ps_m[0:GROUP * TT, 0:P], ACT.Copy, scale=-1.0).then_inc(taken["low"], 1)

            def take_rows(b, i):
                act.wait_ge(in_psum["rows"], b * KT + i + 1)
                wait(act, in_psum["y"], b * 2)
                act.activation(attn_T[:, i, :], ps_m[:], ACT.Copy).then_inc(taken["rows"], 1)

            def batch(b):
                for g in range(GROUPS):
                    for k in range(TT):
                        if exists(b):
                            exps(b, g, k)
                        back = group_after(b, g, -1)
                        if k == 0 and exists(back[0]):
                            copy_out(*back)
                        unit = SHARED.get((g, k))
                        if unit and unit[0] == "low" and exists(b + unit[1]):
                            take_lows(b + unit[1], unit[2])
                        if unit and unit[0] == "rows" and exists(b + unit[1]):
                            take_rows(b + unit[1], unit[2])

            take_lows(0, 0)
            batches(act, batch)


AHEAD = 2
SLOTS = 4


def transpose_units():
    units = []
    for n in range(HEADS):
        units += [("T", n, k) for k in range(TT)]
        if n == 1:
            units.append(("R", GROUPS - 1))
        if n == 4:
            units += [("Y", 0), ("Y", 1)]
        if n >= 5 and n % GROUP == 1:
            units.append(("R", (n - 5) // GROUP))
    return {u: i for i, u in enumerate(units)}


UNITS = transpose_units()
PER_BATCH = len(UNITS)
CARRIED = 3
assert PER_BATCH % 2 == 0


class Unit:

    def __init__(self, b, unit, epilogue=False):
        if epilogue:
            at, rounds = PER_BATCH * BATCH - CARRIED + {"R": 0, "Y": 1 + unit[1]}[unit[0]], None
            self.bank, self.before, self.order = at % 2, at // 2, at
            return
        carried = unit in (("R", GROUPS - 1), ("Y", 0), ("Y", 1))
        at = UNITS[unit] - CARRIED
        if isinstance(b, int) and b == 0:
            assert not carried
            at += sum(UNITS[c] > UNITS[unit] for c in (("R", GROUPS - 1), ("Y", 0), ("Y", 1)))
        self.bank = at % 2
        self.before = b * (PER_BATCH // 2) + at // 2
        self.order = b * PER_BATCH + at


def build_attend_clipped(nc, io, scratch, keep):
    with ExitStack() as ctx:
        n_ = Names(nc, ctx)
        q_st = [n_.sb(f"g_q_st{i}", [P, GROUP // 2, SEQ], F32R) for i in range(2)]
        k_st = [n_.sb(f"g_k_st{i}", [P, GROUP, SEQ], F32R) for i in range(2)]
        v_st = [n_.sb(f"g_v_st{i}", [P, TT, GROUP, VW]) for i in range(2)]
        wo = n_.sb("g_wo", [P, GROUPS, DIM])
        probs = [n_.sb(f"g_probs{i}", [P, TT, SEQ]) for i in range(SLOTS)]
        low = n_.sb("g_low", [P, SLOTS, TT])
        sums = n_.sb("g_sums", [P, 2, GROUP, TT])
        recip = n_.sb("g_recip", [P, 2, GROUP, TT])
        probs_T = [n_.sb(f"g_probs_T{i}", [P, GROUP, TT, SEQ]) for i in range(2)]
        recip_wide = n_.sb("g_recip_wide", [P, 2, TT, GROUP, VW])
        recip_rows = n_.sb("g_recip_rows", [P, SEQ])
        heads_out = n_.sb("g_heads_out", [P, GROUPS, SEQ])
        x_res = n_.sb("g_x_res", [P, TT, DIM])
        ps_s = [n_.ps(f"g_ps_s{i}", [P, 2, SEQ]) for i in range(2)]
        ps_t = [n_.ps(f"g_ps_t{i}", [P, SEQ]) for i in range(2)]
        ps_o = [n_.ps(f"g_ps_o{i}", [P, SEQ]) for i in range(2)]

        zeroed = n_.sem("g_zeroed")
        wo_loaded = n_.sem("g_wo_loaded")
        qk_loaded = [n_.sem(f"g_qk_loaded{i}") for i in range(2)]
        v_loaded = [n_.sem(f"g_v_loaded{i}") for i in range(2)]
        scores_in_psum = n_.sem("g_scores_in_psum")
        clipped = n_.sem("g_clipped")
        low_ready = n_.sem("g_low_ready")
        probs_ready = n_.sem("g_probs_ready")
        unit_in_psum = n_.sem("g_unit_in_psum")
        unit_taken = [n_.sem(f"g_unit_taken{i}") for i in range(2)]
        pv_done = n_.sem("g_pv_done")
        recip_ready = n_.sem("g_recip_ready")
        recip_spread = n_.sem("g_recip_spread")
        heads_ready = n_.sem("g_heads_ready")
        x_loaded = n_.sem("g_x_loaded")
        x2_stored = n_.sem("g_x2_stored")
        block = ctx.enter_context(nc.Block())
        QK_DMAS = 16

        @block.sync
        def _(sp):
            clip = sp.value_load(keep["clip_flag"][0:1, 0:1], min_val=0, max_val=1)
            with sp.If(clip > 0):
                sp.wait_ge(zeroed, 3)
                for j in range(GROUP):
                    sp.dma_start(wo[32 * j:32 * j + HDIM, :, :],
                                 io["Wo"].rearrange("(g h d) n -> h d g n", g=GROUPS, h=GROUP)[j]).then_inc(wo_loaded, 16)
                sp.dma_start(wo[HDIM:HDIM + 1, 0, :], io["bo"].rearrange("(a n) -> a n", a=1)).then_inc(wo_loaded, 16)

                def load_group(b, g):
                    s = g % 2
                    gi = b * GROUPS + g
                    wait(sp, scores_in_psum, gi * 8 - 8)
                    for name, dst, parts in (("q", q_st[s], (0, 1, 0, 1)), ("k", k_st[s], (0, 0, 1, 1))):
                        for half in range(2):
                            for c, part in enumerate(parts):
                                row = 1 + HDIM * (part if name == "q" else 2 * part)
                                src = scratch[name][bass.ds(b, 1)].rearrange("a (g k h r) t -> (a g) h r k t", g=GROUPS, k=2, h=2)
                                src = src[g, half, row:row + HDIM]
                                at = half * 64 + c * HDIM
                                to = dst[at:at + HDIM, :, :] if name == "q" else dst[at:at + HDIM, half:GROUP:2, :]
                                sp.dma_start(to.bitcast(F32), src).then_inc(qk_loaded[s], 16)
                    wait(sp, pv_done, gi - 1)
                    src = scratch["v"][bass.ds(b, 1), :, :].rearrange("a p (t h w) -> (a p) t (h w)", t=TT, h=HEADS)
                    sp.dma_start(v_st[s][:].rearrange("p t h w -> p t (h w)"),
                                 src[:, :, g * GROUP * VW:(g + 1) * GROUP * VW]).then_inc(v_loaded[s], 16)

                def load_residual(b):
                    wait(sp, x2_stored, b * 16)
                    sp.dma_start(x_res[:], io["x"][bass.ds(b * SEQ, SEQ), :].rearrange("(t p) d -> p t d", p=P)).then_inc(x_loaded, 16)

                def store_x2(b, units):
                    for u in units:
                        sp.wait_ge(unit_taken[u.bank], u.before + 1)
                    sp.dma_start(scratch["x2"][bass.ds(b * SEQ, SEQ), :].rearrange("(t p) d -> p t d", p=P), x_res[:]).then_inc(x2_stored, 16)

                for g in range(GROUPS):
                    load_group(0, g)
                load_residual(0)
                with sp.Fori(1, BATCH) as b:
                    for g in range(GROUPS):
                        load_group(b, g)
                    store_x2(b - 1, [Unit(b, ("Y", i)) for i in range(2)])
                    load_residual(b)
                store_x2(BATCH - 1, [Unit(0, ("Y", i), epilogue=True) for i in range(2)])
                sp.wait_ge(x2_stored, 16 * BATCH)

        @block.gpsimd
        def _(pool):
            clip = pool.value_load(keep["clip_flag"][0:1, 0:1], min_val=0, max_val=1)
            with pool.If(clip > 0):
                pool.memset(wo[:], 0.0).then_inc(zeroed, 1)
                for s in range(2):
                    pool.memset(k_st[s][:].bitcast(F32), 0.0).then_inc(zeroed, 1)

        @block.tensor
        def _(pe):
            clip = pe.value_load(keep["clip_flag"][0:1, 0:1], min_val=0, max_val=1)
            with pe.If(clip > 0):
                def scores(b, m):
                    if m >= HEADS:
                        b, m = b + 1, m - HEADS
                    g, j = m // GROUP, m % GROUP
                    s = g % 2
                    if j == 0:
                        pe.wait_ge(qk_loaded[s], b * (2 * 16 * QK_DMAS) + (g // 2 + 1) * 16 * QK_DMAS)
                    for u in range(2):
                        wait(pe, clipped, b * (2 * HEADS) + 2 * m - 1 + u)
                        for t in range(2):
                            q0 = (2 * u + t) * P
                            mm = pe.matmul(ps_s[u][:, t, :], q_st[s][:, j // 2, q0:q0 + P], k_st[s][:, j, :],
                                           start=True, stop=True)
                        mm.then_inc(scores_in_psum, 1)

                def transposes(b, m):
                    pe.wait_ge(probs_ready, b * HEADS + m + 1)
                    for k in range(TT):
                        u = Unit(b, ("T", m, k))
                        wait(pe, unit_taken[u.bank], u.before)
                        for t in range(TT):
                            mm = pe.transpose(ps_t[u.bank][:, t * P:(t + 1) * P], probs[m % SLOTS][:, t, k * P:(k + 1) * P],
                                              keep["ident"][:])
                        mm.then_inc(unit_in_psum, 1)

                def probs_v(b, g):
                    s = g % 2
                    gi = b * GROUPS + g
                    for k in (TT - 2, TT - 1):
                        u = Unit(b, ("T", g * GROUP + GROUP - 1, k))
                        pe.wait_ge(unit_taken[u.bank], u.before + 1)
                    pe.wait_ge(v_loaded[s], b * 32 + (g // 2 + 1) * 16)
                    wait(pe, heads_ready, gi - 1)
                    for k in range(TT):
                        for j in range(GROUP):
                            mm = pe.matmul(ps_o[s][32 * j:32 * j + 32, :], v_st[s][:, k, j, :], probs_T[s][:, j, k, :],
                                           start=(k == 0), stop=(k == TT - 1))
                    mm.then_inc(pv_done, 1)

                def reciprocals(b, g, u):
                    pe.wait_ge(recip_spread, b * GROUPS + g + 1)
                    wait(pe, unit_taken[u.bank], u.before)
                    for t in range(TT):
                        mm = pe.matmul(ps_t[u.bank][:, t * P:(t + 1) * P],
                                       recip_wide[:, g % 2, t].rearrange("p j w -> p (j w)"), keep["ident"][:],
                                       start=True, stop=True)
                    mm.then_inc(unit_in_psum, 1)

                def project_out(b, units):
                    pe.wait_ge(heads_ready, b * GROUPS + GROUPS)
                    for i, u in enumerate(units):
                        wait(pe, unit_taken[u.bank], u.before)
                        for t in range(2):
                            t0 = (2 * i + t) * P
                            for g in range(GROUPS):
                                mm = pe.matmul(ps_t[u.bank][:, t * DIM:(t + 1) * DIM], heads_out[:, g, t0:t0 + P], wo[:, g, :],
                                               start=(g == 0), stop=(g == GROUPS - 1))
                        mm.then_inc(unit_in_psum, 1)

                def batch(b, first, last):
                    for m in range(HEADS):
                        if m + AHEAD < HEADS or not last:
                            scores(b, m + AHEAD)
                        if m == 1 and not first:
                            probs_v(b - 1, GROUPS - 1)
                        if m >= 5 and m % GROUP == 1:
                            probs_v(b, (m - 5) // GROUP)
                        transposes(b, m)
                        if m == 1 and not first:
                            reciprocals(b - 1, GROUPS - 1, Unit(b, ("R", GROUPS - 1)))
                        if m == 4 and not first:
                            project_out(b - 1, [Unit(b, ("Y", i)) for i in range(2)])
                        if m >= 5 and m % GROUP == 1:
                            g = (m - 5) // GROUP
                            reciprocals(b, g, Unit(b, ("R", g)))

                pe.wait_ge(zeroed, 3)
                for m in range(AHEAD):
                    scores(0, m)
                pe.wait_ge(wo_loaded, 16 * (GROUP + 1))
                batch(0, True, False)
                with pe.Fori(1, BATCH - 1) as b:
                    batch(b, False, False)
                batch(BATCH - 1, False, True)
                end = BATCH - 1
                probs_v(end, GROUPS - 1)
                reciprocals(end, GROUPS - 1, Unit(0, ("R", 0), epilogue=True))
                project_out(end, [Unit(0, ("Y", i), epilogue=True) for i in range(2)])

        @block.vector
        def _(dve):
            clip = dve.value_load(keep["clip_flag"][0:1, 0:1], min_val=0, max_val=1)
            with dve.If(clip > 0):
                def clip_and_low(b, m):
                    head2 = b * (2 * HEADS) + 2 * m
                    if m >= SLOTS:
                        dve.wait_ge(unit_in_psum, Unit(b, ("T", m - SLOTS, TT - 1)).order + 1)
                    elif not (isinstance(b, int) and b == 0):
                        dve.wait_ge(unit_in_psum, Unit(b - 1, ("T", m - SLOTS + HEADS, TT - 1)).order + 1)
                    for u in range(2):
                        dve.wait_ge(scores_in_psum, head2 + u + 1)
                        dve.tensor_scalar(probs[m % SLOTS][:, 2 * u:2 * u + 2, :], ps_s[u][:], CLAMP, -CLAMP,
                                          ALU.min, ALU.max).then_inc(clipped, 1)
                    for u in range(2):
                        dve.wait_ge(clipped, head2 + u + 1)
                        dve.tensor_reduce(low[:, m % SLOTS, 2 * u:2 * u + 2], probs[m % SLOTS][:, 2 * u:2 * u + 2, :],
                                          AX_X, ALU.min).then_inc(low_ready, 1)

                def invert(b, g):
                    gi = b * GROUPS + g
                    dve.wait_ge(probs_ready, gi * GROUP + GROUP)
                    dve.reciprocal(recip[:, g % 2], sums[:, g % 2]).then_inc(recip_ready, 1)
                    dve.wait_ge(recip_ready, gi + 1)
                    dve.tensor_copy(recip_wide[:, g % 2], recip[:, g % 2].rearrange("p j (t a) -> p t j a", a=1)
                                    .to_broadcast([P, TT, GROUP, VW])).then_inc(recip_spread, 1)

                def normalise(b, g, u):
                    dve.wait_ge(unit_taken[u.bank], u.before + 1)
                    dve.wait_ge(pv_done, b * GROUPS + g + 1)
                    dve.tensor_tensor(heads_out[:, g, :], ps_o[g % 2][:], recip_rows[:], ALU.mult).then_inc(heads_ready, 1)

                def add_residual(b, units):
                    dve.wait_ge(x_loaded, b * 16 + 16)
                    for i, u in enumerate(units):
                        dve.wait_ge(unit_in_psum, u.order + 1)
                        part = x_res[:, 2 * i:2 * i + 2, :]
                        dve.scalar_tensor_tensor(out=part, in0=ps_t[u.bank][:].rearrange("p (t d) -> p t d", t=2),
                                                 scalar=keep["tanh_g"][:, 0:1], in1=part,
                                                 op0=ALU.mult, op1=ALU.add).then_inc(unit_taken[u.bank], 1)

                def batch(b, first):
                    for m in range(HEADS):
                        clip_and_low(b, m)
                        if m == 1 and not first:
                            invert(b - 1, GROUPS - 1)
                        if m >= 5 and m % GROUP == 1:
                            invert(b, (m - 5) // GROUP)
                        if m == 3 and not first:
                            normalise(b - 1, GROUPS - 1, Unit(b, ("R", GROUPS - 1)))
                        if m >= 7 and m % GROUP == 3:
                            g = (m - 7) // GROUP
                            normalise(b, g, Unit(b, ("R", g)))
                        if m == 5 and not first:
                            add_residual(b - 1, [Unit(b, ("Y", i)) for i in range(2)])

                batch(0, True)
                with dve.Fori(1, BATCH) as b:
                    batch(b, False)
                end = BATCH - 1
                invert(end, GROUPS - 1)
                normalise(end, GROUPS - 1, Unit(0, ("R", 0), epilogue=True))
                add_residual(end, [Unit(0, ("Y", i), epilogue=True) for i in range(2)])

        @block.scalar
        def _(act):
            clip = act.value_load(keep["clip_flag"][0:1, 0:1], min_val=0, max_val=1)
            with act.If(clip > 0):
                def exps(b, m):
                    g, j = m // GROUP, m % GROUP
                    if j == 0:
                        wait(act, recip_ready, b * GROUPS + g - 1)
                    for u in range(2):
                        act.wait_ge(low_ready, b * (2 * HEADS) + 2 * m + u + 1)
                        for t in (2 * u, 2 * u + 1):
                            tile = probs[m % SLOTS][:, t, :]
                            ins = act.activation(tile, tile, ACT.Exp, bias=low[:, m % SLOTS, t:t + 1], scale=-1.0,
                                                 accum_out=sums[:, g % 2, j, t:t + 1])
                    ins.then_inc(probs_ready, 1)

                def evacuate(b, m):
                    g, j = m // GROUP, m % GROUP
                    if j == 0:
                        wait(act, pv_done, b * GROUPS + g - 1)
                    for k in range(TT):
                        u = Unit(b, ("T", m, k))
                        act.wait_ge(unit_in_psum, u.order + 1)
                        act.activation(probs_T[g % 2][:, j, k, :], ps_t[u.bank][:], ACT.Copy).then_inc(unit_taken[u.bank], 1)

                def take_reciprocals(b, g, u):
                    act.wait_ge(unit_in_psum, u.order + 1)
                    wait(act, heads_ready, b * GROUPS + g)
                    act.activation(recip_rows[:], ps_t[u.bank][:], ACT.Copy).then_inc(unit_taken[u.bank], 1)

                def batch(b, first):
                    for m in range(HEADS):
                        exps(b, m)
                        if m == 0 and not first:
                            evacuate(b - 1, HEADS - 1)
                        if m > 0:
                            evacuate(b, m - 1)
                        if m == 2 and not first:
                            take_reciprocals(b - 1, GROUPS - 1, Unit(b, ("R", GROUPS - 1)))
                        if m >= 6 and m % GROUP == 2:
                            g = (m - 6) // GROUP
                            take_reciprocals(b, g, Unit(b, ("R", g)))

                batch(0, True)
                with act.Fori(1, BATCH) as b:
                    batch(b, False)
                end = BATCH - 1
                evacuate(end, HEADS - 1)
                take_reciprocals(end, GROUPS - 1, Unit(0, ("R", 0), epilogue=True))


RING = 4
LEAD = 2
BITS = 31
TILES = TOKENS // P
PAIRS = EXPERTS // 2


def build_experts(nc, io, scratch, keep):
    with ExitStack() as ctx:
        n = Names(nc, ctx)
        ident = keep["ident"]
        x_hi = n.sb("x_hi", [P, KT, TOKENS], F32R)
        x_lo = n.sb("x_lo", [P, KT, TOKENS], F32R)
        out_T = n.sb("out_T_acc", [P, KT, TOKENS])
        w_raw = n.sb("w_raw", [P, KT * HIDDEN])
        w1_hi = [n.sb(f"w1_hi{i}", [P, KT, HIDDEN], F32R) for i in range(2)]
        w1_lo = [n.sb(f"w1_lo{i}", [P, KT, HIDDEN], F32R) for i in range(2)]
        w2_hi = [n.sb(f"w2_hi{i}", [P, HT, DIM], F32R) for i in range(2)]
        w2_lo = [n.sb(f"w2_lo{i}", [P, HT, DIM], F32R) for i in range(2)]
        b1 = [n.sb(f"b1_{i}", [P, HT]) for i in range(2)]
        b2 = [n.sb(f"b2_{i}", [P, KT]) for i in range(2)]
        gelu = n.sb("gelu", [P, RING, SEQ])
        h_hi = n.sb("h_hi", [P, RING, SEQ], F32R)
        h_lo = n.sb("h_lo", [P, RING, SEQ], F32R)
        gate = n.sb("gate", [P, SEQ])
        gated = n.sb("gated", [P, KT, SEQ])
        x2_t = [gelu[:, 2 * i:2 * i + 2, :].rearrange("p a (b d) -> p (a b) d", d=DIM) for i in range(2)]
        xn = gated[:].rearrange("p a (b d) -> p (a b) d", d=DIM)
        logits_T = gate
        zero = n.sb("zero_c", [P, 1])
        eps = n.sb("eps_c", [P, 1])
        stats = n.sb("stats_c", [P, TT, 6])
        meanvar = n.sb("meanvar_c", [P, 4, TT])
        std = n.sb("std_c", [P, TT])
        newton = n.sb("newton_c", [P, 4, TT])
        gw_raw = n.sb("gw_raw", [P, KT, EXPERTS])
        gw = n.sb("gw", [P, KT, P], F32R)
        pick = n.sb("pick", [P, EXPERTS])
        ones = n.sb("ones_c", [P, P])
        logits = n.sb("logits", [P, EXPERTS, TILES])
        signed = n.sb("signed", [P, EXPERTS, TILES])
        below = n.sb("below", [P, EXPERTS, TILES])
        gates_T = n.sb("gates_T", [P, 2, P])
        count = n.sb("count", [P, 1])
        negative = n.sb("negative", [P, 1])
        sign = n.sb("sign", [P, 1])
        rank = n.sb("rank", [P, 1])
        bit = n.sb("bit", [P, 1], I32)
        prefix = n.sb("prefix", [P, 1], I32)
        candidate = n.sb("candidate", [P, 1], I32)
        passes = n.sb("passes", [P, 1], I32)
        kth = n.sb("kth", [P, 1])
        ps_h = n.ps("ps_h", [P, RING, SEQ])
        ps_y = [n.ps(f"ps_y{i}", [P, KT, SEQ]) for i in range(2)]
        ps_l, ps_c = ps_y
        ps_xn, ps_x2 = ps_h[:, 0:2, :], ps_h[:, 2:4, :]

        consts_set = n.sem("c_consts_set")
        gw_loaded = n.sem("c_gw_loaded")
        gw_hi_done = n.sem("c_gw_hi_done")
        gw_ready = n.sem("c_gw_ready")
        x2_loaded = [n.sem(f"c_x2_loaded{i}") for i in range(2)]
        stats_done = n.sem("c_stats_done")
        std_done = n.sem("c_std_done")
        newton_done = n.sem("c_newton_done")
        xn_ready = n.sem("c_xn_ready")
        turned = n.sem("c_turned")
        hi_done = n.sem("c_hi_done")
        lo_done = n.sem("c_lo_done")
        logits_in_psum = n.sem("c_logits_in_psum")
        logits_T_ready = n.sem("c_logits_T_ready")
        x2T_kept = n.sem("c_x2T_kept")
        picked = n.sem("c_picked")
        logits_kept = n.sem("c_logits_kept")
        step = n.sem("c_step")
        counted = n.sem("c_counted")
        summed = n.sem("c_summed")
        gates_ready = n.sem("c_gates_ready")
        gates_in_psum = n.sem("c_gates_in_psum")
        gates_T_ready = n.sem("c_gates_T_ready")
        gates_stored = n.sem("c_gates_stored")

        raw_loaded = n.sem("d_raw_loaded")
        w_hi_done = n.sem("d_w_hi_done")
        w_ready = n.sem("d_w_ready")
        bias_loaded = [n.sem(f"d_bias_loaded{i}") for i in range(2)]
        gate_loaded = n.sem("d_gate_loaded")
        h_in_psum = n.sem("d_h_in_psum")
        gelu_done = n.sem("d_gelu_done")
        h_hi_done = n.sem("d_h_hi_done")
        h_ready = n.sem("d_h_ready")
        w2_done = n.sem("d_w2_done")
        y_taken = n.sem("d_y_taken")
        added = n.sem("d_added")
        out_stored = n.sem("d_out_stored")
        block = ctx.enter_context(nc.Block())

        def tile_no(e, c, j):
            return e * (BATCH * HT) + c * HT + j

        def chunk_no(e, c):
            return e * BATCH + c

        @block.sync
        def _(sp):
            def load_x2(bb, p):
                b = bb * 2 + p
                wait(sp, turned, b - 1)
                sp.dma_start(x2_t[p], scratch["x2"][bass.ds(b, 1), :].rearrange("a (t p d) -> p (a t) d", p=P, d=DIM)).then_inc(x2_loaded[p], 16)

            def load_w(e, half):
                wait(sp, w_ready, e * 2 + half)
                if half == 0:
                    src = io["w1T"][bass.ds(e, 1), :, :].rearrange("a (k p) h -> p (a k) h", p=P)
                    dst = w_raw[:].rearrange("p (k h) -> p k h", k=KT)
                else:
                    src = io["w2T"][bass.ds(e, 1), :, :].rearrange("a (j p) d -> p (a j) d", p=P)
                    dst = w_raw[:].rearrange("p (j d) -> p j d", j=HT)
                sp.dma_start(dst, src).then_inc(raw_loaded, 16)

            def load_bias(e, p):
                sp.dma_start(b1[p][:], io["b1"][bass.ds(e, 1), :, :].rearrange("a p j -> (a p) j")).then_inc(bias_loaded[p], 16)
                sp.dma_start(b2[p][:], io["b2"][bass.ds(e, 1), :, :].rearrange("a p j -> (a p) j")).then_inc(bias_loaded[p], 16)

            def load_gate(e, c):
                sp.wait_ge(y_taken, chunk_no(e, c) + 2)
                src = scratch["gates"][bass.ds(chunk_no(e, c), 1), :]
                sp.dma_start(gate[:], src.to_broadcast([P, SEQ])).then_inc(gate_loaded, 16)

            sp.dma_start(gw_raw[:], io["gwT"].rearrange("(k p) e -> p k e", p=P)).then_inc(gw_loaded, 16)
            for p in range(2):
                load_x2(0, p)
            for half in range(2):
                load_w(0, half)
            load_bias(0, 0)
            with sp.Fori(1, BATCH // 2) as bb:
                for p in range(2):
                    load_x2(bb, p)
            sp.wait_ge(gates_T_ready, 1)
            for half in range(2):
                rows = scratch["gates"].rearrange("r (a t) -> (r a) t", t=P)[half * P:(half + 1) * P, :]
                sp.dma_start(rows, gates_T[:, half, :]).then_inc(gates_stored, 16)
            sp.wait_ge(gates_stored, 32)

            def expert(e, p, last):
                load_gate(e, 0)
                if not last:
                    load_w(e + 1, 0)
                    load_bias(e + 1, 1 - p)
                load_gate(e, 1)
                if not last:
                    load_w(e + 1, 1)
                if not last:
                    with sp.Fori(2, BATCH) as c:
                        load_gate(e, c)

            with sp.Fori(0, PAIRS - 1) as pair:
                for p in range(2):
                    expert(pair * 2 + p, p, False)
            expert(EXPERTS - 2, 0, False)
            expert(EXPERTS - 1, 1, True)

            def store(c):
                sp.wait_ge(added, chunk_no(EXPERTS - 1, c) + 1)
                sp.dma_start(io["out_T"].rearrange("(k p) t -> p k t", p=P)[:, :, bass.ds(c * SEQ, SEQ)],
                             out_T[:, :, bass.ds(c * SEQ, SEQ)]).then_inc(out_stored, 16)

            for c in range(BATCH):
                if c + 2 < BATCH:
                    load_gate(EXPERTS - 1, c + 2)
                store(c)
            sp.wait_ge(out_stored, 16 * BATCH)

        @block.gpsimd
        def _(pool):
            pool.memset(zero[:], 0.0).then_inc(consts_set, 1)
            pool.memset(gw[:].bitcast(F32), 0.0).then_inc(consts_set, 1)
            pool.memset(ones[:], 1.0).then_inc(consts_set, 1)
            pool.memset(bit[:], 1 << (BITS - 1)).then_inc(consts_set, 1)
            pool.memset(prefix[:], 0).then_inc(consts_set, 1)
            pool.memset(eps[:], EPS).then_inc(consts_set, 1)
            pool.wait_ge(consts_set, 6)

            def split(e, half, hi, lo):
                at = e * 2 + half
                pool.wait_ge(raw_loaded, at * 16 + 16)
                if half == 0:
                    wait(pool, w2_done, tile_no(e, 0, 0) - BATCH * HT + RING if not isinstance(e, int) or e >= 2 else 0)
                hi, lo = (w[:].rearrange("p a b -> p (a b)") for w in (hi, lo))
                pool.tensor_tensor(hi, w_raw[:], zero[:].to_broadcast([P, KT * HIDDEN]), ALU.add).then_inc(w_hi_done, 1)
                pool.wait_ge(w_hi_done, at + 1)
                pool.tensor_tensor(lo, w_raw[:], hi.bitcast(F32), ALU.subtract).then_inc(w_ready, 1)

            def expert(e, p):
                split(e, 0, w1_hi[p], w1_lo[p])
                split(e, 1, w2_hi[p], w2_lo[p])

            for p in range(2):
                expert(p, p)
            with pool.Fori(1, PAIRS) as pair:
                for p in range(2):
                    expert(pair * 2 + p, p)

        @block.tensor
        def _(pe):
            pe.wait_ge(consts_set, 6)
            pe.wait_ge(gw_ready, 2)

            def turn(bb, p):
                b = bb * 2 + p
                pe.wait_ge(x2_loaded[p], bb * 16 + 16)
                pe.wait_ge(x2T_kept, b)
                for k in range(KT):
                    for t in range(TT):
                        pe.transpose(ps_x2[:, k, t * P:(t + 1) * P], x2_t[p][:, t, k * P:(k + 1) * P], ident[:])
                pe.wait_ge(xn_ready, b + 1)
                pe.wait_ge(lo_done, b)
                for k in range(KT):
                    for t in range(TT):
                        mm = pe.transpose(ps_xn[:, k, t * P:(t + 1) * P], xn[:, t, k * P:(k + 1) * P], ident[:])
                mm.then_inc(turned, 1)
                pe.wait_ge(logits_T_ready, b)
                pe.wait_ge(lo_done, b + 1)
                for i, (part, k) in enumerate((part, k) for k in range(KT) for part in (x_hi, x_lo)):
                    mm = pe.matmul(ps_l[:, 0, :], gw[:, k, :], part[:, k, bass.ds(b * SEQ, SEQ)],
                                   start=(i == 0), stop=(i == 2 * KT - 1))
                mm.then_inc(logits_in_psum, 1)
                pe.wait_ge(logits_kept, b)
                pe.wait_ge(logits_T_ready, b + 1)
                for t in range(TT):
                    mm = pe.matmul(ps_l[:, 1, t * EXPERTS:(t + 1) * EXPERTS], logits_T[:, t * P:(t + 1) * P], pick[:],
                                   start=True, stop=True)
                mm.then_inc(picked, 1)

            with pe.Fori(0, BATCH // 2) as bb:
                for p in range(2):
                    turn(bb, p)

            with pe.Fori(0, BITS + 1) as i:
                pe.wait_ge(counted, i + 1)
                pe.matmul(ps_c[:, 0, 0:1], ones[:], count[:], start=True, stop=True).then_inc(summed, 1)
            pe.wait_ge(gates_ready, 1)
            for half in range(2):
                mm = pe.transpose(ps_c[:, 1, half * P:(half + 1) * P],
                                  signed[:, half * 4:half * 4 + 4, :].rearrange("p e t -> p (e t)"), ident[:])
            mm.then_inc(gates_in_psum, 1)

            pe.sem_inc(w2_done, RING)
            pe.wait_ge(x2T_kept, BATCH)
            pe.wait_ge(gates_T_ready, 1)

            def first(e, p, c, j):
                pe.wait_ge(gelu_done, tile_no(e, c, j) + 1)
                at = slice(j * P, (j + 1) * P)
                parts = [(w, x, k) for k in range(KT)
                         for w, x in ((w1_hi[p], x_hi), (w1_hi[p], x_lo), (w1_lo[p], x_hi))]
                for i, (w, x, k) in enumerate(parts):
                    mm = pe.matmul(ps_h[:, j % RING, :], w[:, k, at], x[:, k, bass.ds(c * SEQ, SEQ)],
                                   start=(i == 0), stop=(i == len(parts) - 1))
                mm.then_inc(h_in_psum, 1)

            def second(e, p, c, j, s):
                if j == 0:
                    pe.wait_ge(y_taken, chunk_no(e, c) + 1)
                pe.wait_ge(h_ready, tile_no(e, c, j) + 1 + RING)
                for d in range(KT):
                    at = slice(d * P, (d + 1) * P)
                    for i, (w, h) in enumerate(((w2_hi[p], h_hi), (w2_hi[p], h_lo), (w2_lo[p], h_hi))):
                        mm = pe.matmul(ps_y[s][:, d, :], w[:, j, at], h[:, j % RING, :],
                                       start=(j == 0 and i == 0), stop=(j == HT - 1 and i == 2))
                mm.then_inc(w2_done, 1)

            def chunk(e, p, c, s, ahead):
                for j in range(HT):
                    if j + LEAD < HT:
                        first(e, p, c, j + LEAD)
                    elif ahead:
                        ahead(j + LEAD - HT)
                    second(e, p, c, j, s)

            def start(e, p, j):
                if j == 0:
                    pe.wait_ge(w_ready, e * 2 + 2)
                first(e, p, 0, j)

            def expert(e, p, last):
                with pe.Fori(0, BATCH // 2 - 1) as cc:
                    for s in range(2):
                        chunk(e, p, cc * 2 + s, s, lambda j: first(e, p, cc * 2 + s + 1, j))
                chunk(e, p, BATCH - 2, 0, lambda j: first(e, p, BATCH - 1, j))
                chunk(e, p, BATCH - 1, 1, None if last else lambda j: start(e + 1, 1 - p, j))

            for j in range(LEAD):
                start(0, 0, j)
            with pe.Fori(0, PAIRS - 1) as pair:
                for p in range(2):
                    expert(pair * 2 + p, p, False)
            expert(EXPERTS - 2, 0, False)
            expert(EXPERTS - 1, 1, True)

        @block.scalar
        def _(act):
            act.wait_ge(consts_set, 6)
            act.sem_inc(gelu_done, RING)
            with act.Fori(0, BATCH) as b:
                act.wait_ge(stats_done, b * 4 + 4)
                act.activation(std[:], meanvar[:, 1, :], ACT.Sqrt, bias=eps[:, 0:1]).then_inc(std_done, 1)
                act.wait_ge(picked, b)
                act.wait_ge(logits_in_psum, b + 1)
                act.activation(logits_T[:], ps_l[:, 0, :], ACT.Copy).then_inc(logits_T_ready, 1)
                act.activation(out_T[:, :, bass.ds(b * SEQ, SEQ)], ps_x2, ACT.Copy).then_inc(x2T_kept, 1)
            act.wait_ge(gates_in_psum, 1)
            act.activation(gates_T[:].rearrange("p h t -> p (h t)"), ps_c[:, 1, 0:2 * P], ACT.Copy).then_inc(gates_T_ready, 1)

            with act.Fori(0, PAIRS) as pair:
                for p in range(2):
                    e = pair * 2 + p
                    act.wait_ge(bias_loaded[p], pair * 32 + 32)
                    with act.Fori(0, BATCH) as c:
                        for j in range(HT):
                            act.wait_ge(h_ready, tile_no(e, c, j) + 1)
                            act.wait_ge(h_in_psum, tile_no(e, c, j) + 1)
                            act.activation(gelu[:, j % RING, :], ps_h[:, j % RING, :], ACT.Gelu_apprx_tanh,
                                           bias=b1[p][:, j:j + 1]).then_inc(gelu_done, 1)

        @block.vector
        def _(dve):
            dve.wait_ge(consts_set, 6)
            dve.tensor_tensor(pick[:], ident[:, 0:EXPERTS], ident[:, EXPERTS:2 * EXPERTS], ALU.add).then_inc(gw_ready, 1)
            dve.wait_ge(gw_loaded, 16)
            dve.tensor_copy(gw[:, :, 0:EXPERTS], gw_raw[:]).then_inc(gw_hi_done, 1)
            dve.wait_ge(gw_hi_done, 1)
            dve.tensor_tensor(gw[:, :, EXPERTS:2 * EXPERTS], gw_raw[:], gw[:, :, 0:EXPERTS].bitcast(F32),
                              ALU.subtract).then_inc(gw_ready, 1)

            def normalise(bb, p):
                b = bb * 2 + p
                dve.wait_ge(x2_loaded[p], bb * 16 + 16)
                dve.wait_ge(xn_ready, b)
                mean_variance(dve, [x2_t[p][:, t, :] for t in range(TT)], stats, meanvar, stats_done, b)
                dve.wait_ge(std_done, b + 1)
                rstd = reciprocal_root(dve, std[:], meanvar[:, 1, :], newton, newton_done, b)
                dve.wait_ge(turned, b)
                for t in range(TT):
                    ins = dve.tensor_scalar(xn[:, t, :], x2_t[p][:, t, :], meanvar[:, 0, t:t + 1], rstd[:, t:t + 1],
                                            ALU.subtract, ALU.mult)
                ins.then_inc(xn_ready, 1)

            def split(b):
                at = bass.ds(b * SEQ, SEQ)
                dve.wait_ge(turned, b + 1)
                dve.tensor_scalar(x_hi[:, :, at], ps_xn, 1.0, None, ALU.mult).then_inc(hi_done, 1)
                dve.wait_ge(hi_done, b + 1)
                dve.tensor_tensor(x_lo[:, :, at], ps_xn, x_hi[:, :, at].bitcast(F32), ALU.subtract).then_inc(lo_done, 1)

            def keep_logits(b):
                dve.wait_ge(picked, b + 1)
                dve.tensor_scalar(logits[:, :, bass.ds(b * TT, TT)],
                                  ps_l[:, 1, 0:TT * EXPERTS].rearrange("p (t e) -> p e t", t=TT),
                                  1.0, None, ALU.mult).then_inc(logits_kept, 1)

            normalise(0, 0)
            with dve.Fori(0, BATCH // 2 - 1) as bb:
                for p in range(2):
                    split(bb * 2 + p)
                    normalise(bb + p, 1 - p)
                    keep_logits(bb * 2 + p)
            split(BATCH - 2)
            normalise(BATCH // 2 - 1, 1)
            keep_logits(BATCH - 2)
            split(BATCH - 1)
            keep_logits(BATCH - 1)

            total = EXPERTS * TOKENS
            dve.wait_ge(logits_kept, BATCH)
            dve.tensor_scalar(below[:], logits[:], 0.0, None, ALU.is_lt, ALU.add, accum_out=count[:]).then_inc(counted, 1)
            dve.wait_ge(summed, 1)
            dve.tensor_scalar(negative[:], ps_c[:, 0, 0:1], KEPT_FROM + 0.5, None, ALU.is_gt).then_inc(step, 1)
            dve.wait_ge(step, 1)
            dve.tensor_scalar(sign[:], negative[:], -2.0, 1.0, ALU.mult, ALU.add).then_inc(step, 1)
            dve.tensor_scalar(rank[:], negative[:], float(total - 1 - 2 * KEPT_FROM), float(KEPT_FROM),
                              ALU.mult, ALU.add).then_inc(step, 1)
            dve.wait_ge(step, 3)
            dve.tensor_scalar(signed[:], logits[:], sign[:, 0:1], None, ALU.mult).then_inc(step, 1)
            dve.wait_ge(step, 4)
            with dve.Fori(0, BITS) as i:
                dve.wait_ge(step, i * 4 + 4)
                dve.tensor_tensor(candidate[:], prefix[:], bit[:], ALU.bitwise_or).then_inc(step, 1)
                dve.wait_ge(step, i * 4 + 5)
                dve.tensor_scalar(below[:], signed[:], candidate[:].bitcast(F32), None, ALU.is_lt, ALU.add,
                                  accum_out=count[:]).then_inc(counted, 1)
                dve.wait_ge(summed, i + 2)
                dve.tensor_tensor(passes[:], ps_c[:, 0, 0:1], rank[:], ALU.is_le).then_inc(step, 1)
                dve.wait_ge(step, i * 4 + 6)
                dve.tensor_scalar(bit[:], bit[:], 1, None, ALU.logical_shift_right).then_inc(step, 1)
                dve.copy_predicated(prefix[:], passes[:], candidate[:]).then_inc(step, 1)
            dve.wait_ge(step, BITS * 4 + 4)
            dve.tensor_tensor(kth[:], prefix[:].bitcast(F32), sign[:], ALU.mult).then_inc(step, 1)
            dve.wait_ge(step, BITS * 4 + 5)
            dve.scalar_tensor_tensor(out=below[:], in0=logits[:], scalar=kth[:, 0:1], in1=logits[:],
                                     op0=ALU.is_ge, op1=ALU.mult).then_inc(step, 1)
            dve.wait_ge(step, BITS * 4 + 6)
            dve.tensor_scalar(signed[:], below[:], keep["tanh_g"][:, 1:2], None, ALU.mult).then_inc(gates_ready, 1)

            dve.sem_inc(h_ready, RING)
            dve.sem_inc(y_taken, 2)

            def halves(e, c, j):
                at = tile_no(e, c, j)
                dve.wait_ge(w2_done, at + 1)
                dve.wait_ge(gelu_done, at + 1 + RING)
                dve.tensor_copy(h_hi[:, j % RING, :], gelu[:, j % RING, :]).then_inc(h_hi_done, 1)
                dve.wait_ge(h_hi_done, at + 1)
                dve.tensor_tensor(h_lo[:, j % RING, :], gelu[:, j % RING, :], h_hi[:, j % RING, :].bitcast(F32),
                                  ALU.subtract).then_inc(h_ready, 1)

            def add_chunk(e, p, c, s):
                dve.wait_ge(gate_loaded, chunk_no(e, c) * 16 + 16)
                dve.wait_ge(added, chunk_no(e, c))
                dve.wait_ge(w2_done, tile_no(e, c, HT) + RING)
                for d in range(KT):
                    ins = dve.scalar_tensor_tensor(out=gated[:, d, :], in0=ps_y[s][:, d, :], scalar=b2[p][:, d:d + 1],
                                                   in1=gate[:], op0=ALU.add, op1=ALU.mult)
                ins.then_inc(y_taken, 1)
                dve.wait_ge(y_taken, chunk_no(e, c) + 3)
                part = out_T[:, :, bass.ds(c * SEQ, SEQ)]
                dve.tensor_tensor(part, part, gated[:], ALU.add).then_inc(added, 1)

            def chunk(e, c, before):
                for j in range(HT):
                    halves(e, c, j)
                    if j == LEAD and before:
                        before()

            def expert(e, p, begin):
                if begin:
                    chunk(e, 0, None)
                else:
                    chunk(e, 0, lambda: add_chunk(e - 1, 1 - p, BATCH - 1, 1))
                chunk(e, 1, lambda: add_chunk(e, p, 0, 0))
                with dve.Fori(1, BATCH // 2) as cc:
                    for s in range(2):
                        chunk(e, cc * 2 + s, lambda: add_chunk(e, p, cc * 2 + s - 1, 1 - s))

            for p in range(2):
                expert(p, p, p == 0)
            with dve.Fori(1, PAIRS) as pair:
                for p in range(2):
                    expert(pair * 2 + p, p, False)
            add_chunk(EXPERTS - 1, 1, BATCH - 1, 1)


def build(nc, io):
    with ExitStack() as ctx:
        n = Names(nc, ctx)
        keep = {"ident": n.sb("ident", [P, P]), "tanh_g": n.sb("tanh_g", [P, 2]), "clip_flag": n.sb("clip_flag", [P, 1], I32)}

        def scratch_of(name, shape):
            return nc.dram_tensor(name, shape, F32).ap()

        scratch = {
            "q": scratch_of("q_scratch", (BATCH, HEADS * ROWS, SEQ)),
            "k": scratch_of("k_scratch", (BATCH, HEADS * ROWS, SEQ)),
            "v": scratch_of("v_scratch", (BATCH, P, TT * HEADS * VW)),
            "x2": scratch_of("x2_scratch", (TOKENS, DIM)),
            "gates": scratch_of("gates_scratch", (EXPERTS * BATCH, SEQ)),
        }
        with ExitStack() as attend_ctx:
            n = Names(nc, attend_ctx)
            keep["q_st"] = [n.sb(f"q_st{i}", [P, GROUP // 2, SEQ], F32R) for i in range(GROUPS)]
            keep["k_st"] = [n.sb(f"k_st{i}", [P, GROUP, SEQ], F32R) for i in range(GROUPS)]
            keep["wo"] = n.sb("wo", [P, KT, DIM])
            build_project(nc, io, scratch, keep)
            build_attend(nc, io, scratch, keep)
        build_attend_clipped(nc, io, scratch, keep)
        scratch["x2"] = scratch["x2"].rearrange("(b s) d -> b (s d)", b=BATCH)
        build_experts(nc, io, scratch, keep)


def kernel(**inputs):
    import numpy as np
    import concourse.bacc as bacc
    from concourse.bass_utils import run_bass_kernel_spmd

    a = {k: np.asarray(v) for k, v in inputs.items()}
    attn = {w: a[f"L0_xattn_{w}"] for w in ("Wq", "bq", "Wk", "bk", "Wv", "bv", "Wo", "bo")}
    arrays = {
        "x": a["x"].reshape(TOKENS, DIM),
        "ctxT": a["ctx_768"].transpose(0, 2, 1),
        "g_xattn": a["g_xattn"],
        "g_ffn": a["g_ffn"],
        **attn,
        "bq": attn["bq"].reshape(KT, P).T,
        "gwT": a["L0_ffn_gate_weight"].T,
        "w1T": a["L0_ffn_w1"].transpose(0, 2, 1),
        "b1": a["L0_ffn_b1"].reshape(EXPERTS, HT, P).transpose(0, 2, 1),
        "w2T": a["L0_ffn_w2"].transpose(0, 2, 1),
        "b2": a["L0_ffn_b2"].reshape(EXPERTS, KT, P).transpose(0, 2, 1),
    }
    nc = bacc.Bacc("TRN2", target_bir_lowering=False, num_devices=1)
    io, feeds = {}, {}
    for name, array in arrays.items():
        feeds[f"in_{name}"] = np.ascontiguousarray(array)
        io[name] = nc.dram_tensor(f"in_{name}", array.shape, mybir.dt.from_np(array.dtype), kind="ExternalInput").ap()
    io["out_T"] = nc.dram_tensor("out_T", (DIM, TOKENS), F32, kind="ExternalOutput").ap()
    build(nc, io)
    result = run_bass_kernel_spmd(nc, [feeds], core_ids=[0])
    return np.ascontiguousarray(result.results[0]["out_T"].T).reshape(BATCH, SEQ, DIM)
```

```python
from contextlib import ExitStack

import concourse.bass as bass
from concourse import mybir

F32 = mybir.dt.float32
F32R = mybir.dt.float32r
I32 = mybir.dt.int32
ALU = mybir.AluOpType
ACT = mybir.ActivationFunctionType
AX_X = mybir.AxisListType.X

P = 128
BATCH, SEQ, DIM = 8, 512, 256
CTX = 192
TOKENS = BATCH * SEQ
HEADS, HDIM = 16, 16
CLAMP = 10000.0
EXPERTS, HIDDEN = 8, 1024
EPS = 1e-5
KEPT_FROM = 4 * 256 * 6 - 1
KT = DIM // P
TT = SEQ // P
GROUP = 4
GROUPS = HEADS // GROUP
VW = HDIM + 1
ROWS = 1 + 3 * HDIM
KEPT = 1 + 2 * HDIM
FITS = CLAMP - 104.0
SUM_LEAST = 0.01
HT = HIDDEN // P


def wait(eng, sem, value):
    if isinstance(value, int) and value <= 0:
        return
    eng.wait_ge(sem, value)


class Names:

    def __init__(self, nc, ctx):
        self.nc, self.ctx = nc, ctx

    def sb(self, name, shape, dt=F32, side=None):
        return self.ctx.enter_context(self.nc.sbuf_tensor(name, shape, dt, side=side))

    def ps(self, name, shape):
        return self.ctx.enter_context(self.nc.psum_tensor(name, shape, F32))

    def sem(self, name):
        return self.ctx.enter_context(self.nc.semaphore(name))


def flat(tile):
    return tile[:].rearrange("p a b -> p (a b)")


def build_project(nc, io, scratch, keep):
    with ExitStack() as ctx:
        n = Names(nc, ctx)
        wq = n.sb("wq", [P, KT, DIM])
        wk = n.sb("wk", [P, KT, DIM])
        wv = n.sb("wv", [P, KT, DIM])
        bq = n.sb("bq_col", [P, KT])
        bq_scaled = n.sb("bq_scaled", [P, KT])
        gates_in = n.sb("gates_in", [P, 2])
        eps = n.sb("eps_a", [P, 1])
        x_t = [n.sb(f"x_t{i}", [P, TT, DIM]) for i in range(2)]
        ctx_t = [n.sb(f"ctx_t{i}", [P, KT, SEQ]) for i in range(2)]
        stats = n.sb("stats_a", [P, TT, 6])
        meanvar = n.sb("meanvar_a", [P, 4, TT])
        std = n.sb("std_a", [P, TT])
        newton = n.sb("newton_a", [P, 4, TT])
        xn = [n.sb(f"xn_a{i}", [P, TT, DIM]) for i in range(2)]
        xn_T = n.sb("xn_T", [P, KT, SEQ])
        q_full = n.sb("q_full", [P, KT, SEQ])
        k_full = n.sb("k_full", [P, KT, SEQ])
        q_hl, k_hl = ([n.sb(f"{name}_hl{i}", [P, 2, KT, SEQ], F32R) for i in range(2)] for name in ("q", "k"))
        v_out = [n.sb(f"v_out{i}", [P, TT, HEADS, VW]) for i in range(2)]
        const_rows = n.sb("const_rows", [P, 2, SEQ])
        ps_x = n.ps("ps_x", [P, KT, SEQ])
        ps_q = n.ps("ps_q", [P, KT, SEQ])
        ps_k = n.ps("ps_k", [P, KT, SEQ])
        ps_v = n.ps("ps_v", [P, TT, DIM])

        zeroed = n.sem("a_zeroed")
        const_rows_set = n.sem("a_const_rows_set")
        consts_moved = n.sem("a_consts_moved")
        fills_zeroed = n.sem("a_fills_zeroed")
        first_loaded = n.sem("a_first_loaded")
        ones_set = n.sem("a_ones_set")
        ident_set = n.sem("a_ident_set")
        w_loaded = n.sem("a_w_loaded")
        small_loaded = n.sem("a_small_loaded")
        x_loaded = [n.sem(f"a_x_loaded{i}") for i in range(2)]
        ctx_loaded = [n.sem(f"a_ctx_loaded{i}") for i in range(2)]
        bq_ready = n.sem("a_bq_ready")
        eps_set = n.sem("a_eps_set")
        stats_done = n.sem("a_stats_done")
        std_done = n.sem("a_std_done")
        newton_done = n.sem("a_newton_done")
        xn_ready = n.sem("a_xn_ready")
        xT_in_psum = n.sem("a_xT_in_psum")
        xT_ready = n.sem("a_xT_ready")
        q_in_psum = n.sem("a_q_in_psum")
        k_in_psum = n.sem("a_k_in_psum")
        v_in_psum = n.sem("a_v_in_psum")
        q_full_ready = n.sem("a_q_full_ready")
        k_full_ready = n.sem("a_k_full_ready")
        hi_done = n.sem("a_hi_done")
        q_split = n.sem("a_q_split")
        k_split = n.sem("a_k_split")
        v_ready = n.sem("a_v_ready")
        stored = [n.sem(f"a_stored{i}") for i in range(2)]
        block = ctx.enter_context(nc.Block())
        rest = CTX - P
        STORES = 16 * (2 * 2 * KT + 1)

        def pairs(eng, pair):
            pair(0, False)
            with eng.Fori(1, BATCH // 2 - 1) as bb:
                pair(bb, False)
            pair(BATCH // 2 - 1, True)

        @block.sync
        def _(sp):
            sp.dma_start(gates_in[:, 0:1], io["g_xattn"].rearrange("(a b) -> a b", a=1).to_broadcast([P, 1])).then_inc(small_loaded, 16)
            sp.dma_start(gates_in[:, 1:2], io["g_ffn"].rearrange("(a b) -> a b", a=1).to_broadcast([P, 1])).then_inc(small_loaded, 16)
            sp.dma_start(bq[:], io["bq"]).then_inc(small_loaded, 16)
            sp.dma_start(wq[:], io["Wq"].rearrange("(k p) n -> p k n", p=P)).then_inc(w_loaded, 16)
            sp.dma_start(keep["wo"][:], io["Wo"].rearrange("(k p) n -> p k n", p=P)).then_inc(consts_moved, 16)
            sp.wait_ge(zeroed, 2)
            for w, w_in, b_in in ((wk, "Wk", "bk"), (wv, "Wv", "bv")):
                sp.dma_start(w[:, 0, :], io[w_in][0:P, :]).then_inc(w_loaded, 16)
                sp.dma_start(w[0:rest, 1, :], io[w_in][P:CTX, :]).then_inc(w_loaded, 16)
                sp.dma_start(w[rest:rest + 1, 1, :], io[b_in].rearrange("(a n) -> a n", a=1)).then_inc(w_loaded, 16)

            def load_x(bb, p):
                b = bb * 2 + p
                wait(sp, xn_ready, b - 1)
                sp.dma_start(x_t[p][:], io["x"][bass.ds(b * SEQ, SEQ), :].rearrange("(t p) d -> p t d", p=P)).then_inc(x_loaded[p], 16)

            def load_ctx(bb, p):
                b = bb * 2 + p
                wait(sp, v_in_psum, b - 1)
                sp.dma_start(ctx_t[p][:, 0, :], io["ctxT"][bass.ds(b, 1), 0:P, :].rearrange("a c t -> (a c) t")).then_inc(ctx_loaded[p], 16)
                sp.dma_start(ctx_t[p][0:rest, 1, :], io["ctxT"][bass.ds(b, 1), P:CTX, :].rearrange("a c t -> (a c) t")).then_inc(ctx_loaded[p], 16)

            def store_qk(bb, p):
                b = bb * 2 + p
                for name, tile, ready in (("k", k_hl[p], k_split), ("q", q_hl[p], q_split)):
                    sp.wait_ge(ready, b + 1)
                    rows = scratch[name][bass.ds(b, 1)].rearrange("a (k h r) t -> h r (a k) t", k=KT, r=KEPT)
                    for part in range(2):
                        for k in range(KT):
                            sp.dma_start(rows[:, 1 + part * HDIM:1 + (part + 1) * HDIM, k], tile[:, part, k].bitcast(F32)).then_inc(stored[p], 16)

            def store_v(bb, p):
                b = bb * 2 + p
                sp.wait_ge(v_ready, b + 1)
                sp.dma_start(scratch["v"][bass.ds(b, 1), :, :].rearrange("a p n -> p (a n)"),
                             v_out[p][:].rearrange("p t h w -> p (t h w)")).then_inc(stored[p], 16)

            for p in range(2):
                load_x(0, p)
                load_ctx(0, p)
            sp.wait_ge(const_rows_set, 2)
            for i, name in enumerate(("q", "k")):
                sp.dma_start(scratch[name].rearrange("b (h r) t -> (b h) r t", r=KEPT)[:, 0, :], const_rows[:, i, :]).then_inc(consts_moved, 16)
            with sp.Fori(0, BATCH // 2 - 1) as bb:
                for p in range(2):
                    load_x(bb + 1, p)
                    store_qk(bb, p)
                    load_ctx(bb + 1, p)
                    store_v(bb, p)
            sp.wait_ge(fills_zeroed, 1)
            sp.wait_ge(consts_moved, 48)
            sp.wait_ge(stored[0], STORES)
            for g in range(GROUPS - 1):
                load_qk(sp, scratch, keep, 0, g, first_loaded)
            for p in range(2):
                store_qk(BATCH // 2 - 1, p)
                store_v(BATCH // 2 - 1, p)
            for p in range(2):
                sp.wait_ge(stored[p], STORES * BATCH // 2)
            sp.wait_ge(first_loaded, 128 * (GROUPS - 1))

        @block.gpsimd
        def _(pool):
            pool.memset(wk[rest:P, 1, :], 0.0).then_inc(zeroed, 1)
            pool.memset(wv[rest:P, 1, :], 0.0).then_inc(zeroed, 1)
            for p in range(2):
                pool.memset(ctx_t[p][rest:P, 1, :], 0.0).then_inc(zeroed, 1)
            pool.wait_ge(zeroed, 4)
            for p in range(2):
                pool.memset(ctx_t[p][rest:rest + 1, 1, :], 1.0).then_inc(ones_set, 1)
            pool.wait_ge(ones_set, 2)
            pool.memset(keep["ident"][:], 0.0).then_inc(ident_set, 1)
            pool.wait_ge(ident_set, 1)
            pool.affine_select(out=keep["ident"][:], in_=keep["ident"][:], compare_op=ALU.not_equal, fill=1.0,
                               base=0, pattern=[[-1, P]], channel_multiplier=1).then_inc(ident_set, 1)
            pool.wait_ge(ident_set, 2)
            for p in range(2):
                pool.memset(v_out[p][:], 1.0).then_inc(ones_set, 1)
            for i in range(2):
                pool.memset(const_rows[:, i, :], float(i)).then_inc(const_rows_set, 1)
            for s in range(GROUPS):
                pool.memset(keep["q_st"][s][:].bitcast(F32), 0.0)
                ins = pool.memset(keep["k_st"][s][:].bitcast(F32), 0.0)
            ins.then_inc(fills_zeroed, 1)

        @block.tensor
        def _(pe):
            pe.wait_ge(ident_set, 2)
            pe.wait_ge(ones_set, 2)
            pe.wait_ge(w_loaded, 16 * 7)

            def turn(bb, p):
                b = bb * 2 + p
                pe.wait_ge(xn_ready, b + 1)
                wait(pe, xT_ready, b)
                for k in range(KT):
                    for t in range(TT):
                        mm = pe.transpose(ps_x[:, k, t * P:(t + 1) * P], xn[p][:, t, k * P:(k + 1) * P], keep["ident"][:])
                mm.then_inc(xT_in_psum, 1)

            def project(bb, p):
                b = bb * 2 + p
                pe.wait_ge(ctx_loaded[p], bb * 32 + 32)
                wait(pe, k_full_ready, b)
                for m in range(KT):
                    for k in range(KT):
                        mm = pe.matmul(ps_k[:, m, :], wk[:, k, m * P:(m + 1) * P], ctx_t[p][:, k, :],
                                       start=(k == 0), stop=(k == KT - 1))
                mm.then_inc(k_in_psum, 1)
                pe.wait_ge(xT_ready, b + 1)
                wait(pe, q_full_ready, b * 2)
                for m in range(KT):
                    for k in range(KT):
                        mm = pe.matmul(ps_q[:, m, :], wq[:, k, m * P:(m + 1) * P], xn_T[:, k, :],
                                       start=(k == 0), stop=(k == KT - 1))
                mm.then_inc(q_in_psum, 1)

            def values(bb, p):
                b = bb * 2 + p
                wait(pe, v_ready, b)
                for t in range(TT):
                    for k in range(KT):
                        mm = pe.matmul(ps_v[:, t, :], ctx_t[p][:, k, t * P:(t + 1) * P], wv[:, k, :],
                                       start=(k == 0), stop=(k == KT - 1))
                mm.then_inc(v_in_psum, 1)

            def pair(bb, last):
                for p in range(2):
                    project(bb, p)
                    if not (last and p == 1):
                        turn(bb + p, 1 - p)
                    values(bb, p)

            turn(0, 0)
            pairs(pe, pair)

        @block.scalar
        def _(act):
            act.wait_ge(small_loaded, 48)
            act.activation(keep["tanh_g"][:], gates_in[:], ACT.Tanh)
            act.activation(bq_scaled[:], bq[:], ACT.Copy, scale=-(HDIM ** -0.5)).then_inc(bq_ready, 1)
            act.wait_ge(bq_ready, 1)
            act.wait_ge(eps_set, 1)

            def root(bb, p):
                b = bb * 2 + p
                act.wait_ge(stats_done, b * 4 + 4)
                act.activation(std[:], meanvar[:, 1, :], ACT.Sqrt, bias=eps[:, 0:1]).then_inc(std_done, 1)

            def take_x(bb, p):
                b = bb * 2 + p
                act.wait_ge(xT_in_psum, b + 1)
                wait(act, q_in_psum, b)
                act.activation(xn_T[:], ps_x[:], ACT.Copy).then_inc(xT_ready, 1)

            def take_qk(bb, p):
                b = bb * 2 + p
                act.wait_ge(k_in_psum, b + 1)
                wait(act, k_split, b)
                act.activation(k_full[:], ps_k[:], ACT.Copy).then_inc(k_full_ready, 1)
                act.wait_ge(q_in_psum, b + 1)
                wait(act, q_split, b)
                for m in range(KT):
                    act.activation(q_full[:, m, :], ps_q[:, m, :], ACT.Identity, bias=bq_scaled[:, m:m + 1],
                                   scale=-(HDIM ** -0.5)).then_inc(q_full_ready, 1)

            def pair(bb, last):
                for p in range(2):
                    more = not (last and p == 1)
                    if more:
                        root(bb + p, 1 - p)
                    take_qk(bb, p)
                    if more:
                        take_x(bb + p, 1 - p)

            root(0, 0)
            take_x(0, 0)
            pairs(act, pair)

        @block.vector
        def _(dve):
            dve.memset(eps[:], EPS).then_inc(eps_set, 1)
            dve.wait_ge(eps_set, 1)
            dve.wait_ge(ones_set, 4)

            def split(full, hl, done, count):
                dve.tensor_copy(hl[:, 0], full[:]).then_inc(hi_done, 1)
                dve.wait_ge(hi_done, count)
                dve.tensor_tensor(hl[:, 1], full[:], hl[:, 0].bitcast(F32), ALU.subtract).then_inc(done, 1)

            def layer_norm(bb, p):
                b = bb * 2 + p
                dve.wait_ge(x_loaded[p], bb * 16 + 16)
                wait(dve, xn_ready, b)
                mean_variance(dve, [x_t[p][:, t, :] for t in range(TT)], stats, meanvar, stats_done, b)
                dve.wait_ge(std_done, b + 1)
                rstd = reciprocal_root(dve, std[:], meanvar[:, 1, :], newton, newton_done, b)
                wait(dve, xT_in_psum, b - 1)
                for t in range(TT):
                    ins = dve.tensor_scalar(xn[p][:, t, :], x_t[p][:, t, :], meanvar[:, 0, t:t + 1], rstd[:, t:t + 1],
                                            ALU.subtract, ALU.mult)
                ins.then_inc(xn_ready, 1)

            def take(bb, p):
                b = bb * 2 + p
                wait(dve, stored[p], bb * STORES)
                dve.wait_ge(k_full_ready, b + 1)
                split(k_full, k_hl[p], k_split, b * 2 + 1)
                dve.wait_ge(q_full_ready, b * 2 + 2)
                split(q_full, q_hl[p], q_split, b * 2 + 2)
                dve.wait_ge(v_in_psum, b + 1)
                dve.tensor_copy(v_out[p][:, :, :, 0:HDIM],
                                ps_v[:].rearrange("p t (h d) -> p t h d", h=HEADS)).then_inc(v_ready, 1)

            def pair(bb, last):
                for p in range(2):
                    if not (last and p == 1):
                        layer_norm(bb + p, 1 - p)
                    take(bb, p)

            layer_norm(0, 0)
            pairs(dve, pair)


def load_qk(sp, scratch, keep, b, g, loaded):
    for name, dst, pieces in (("q", keep["q_st"][g], ((0, KEPT), (1, 1 + HDIM))),
                              ("k", keep["k_st"][g], ((0, 1 + HDIM), (1, KEPT)))):
        src = scratch[name][bass.ds(b, 1)].rearrange("a (g k h r) t -> (a g) h r k t", g=GROUPS, k=2, h=2)
        for half in range(2):
            row = half * 64 + 64 - ROWS
            for lo, hi in pieces:
                to = dst[row:row + hi - lo, :, :] if name == "q" else dst[row:row + hi - lo, half:GROUP:2, :]
                sp.dma_start(to.bitcast(F32), src[g, half, lo:hi]).then_inc(loaded, 16)
                row += hi - lo


def mean_variance(dve, tiles, stats, meanvar, done, b):
    size = tiles[0].shape[-1]
    for t, tile in enumerate(tiles):
        ins = dve.bn_stats(stats[:, t, :], tile)
    ins.then_inc(done, 1)
    dve.wait_ge(done, b * 4 + 1)
    mean, var, diff, dev = (meanvar[:, i, :] for i in range(4))
    dve.tensor_tensor(mean, stats[:, :, 1], stats[:, :, 4], ALU.add)
    dve.tensor_tensor(diff, stats[:, :, 1], stats[:, :, 4], ALU.subtract)
    dve.tensor_tensor(dev, stats[:, :, 2], stats[:, :, 5], ALU.add).then_inc(done, 1)
    dve.wait_ge(done, b * 4 + 2)
    dve.tensor_scalar(mean, mean, 0.5, None, ALU.mult)
    dve.tensor_scalar(dev, dev, 1.0 / size, None, ALU.mult)
    dve.scalar_tensor_tensor(out=diff, in0=diff, scalar=0.25, in1=diff, op0=ALU.mult, op1=ALU.mult).then_inc(done, 1)
    dve.wait_ge(done, b * 4 + 3)
    dve.tensor_tensor(var, dev, diff, ALU.add).then_inc(done, 1)


def reciprocal_root(dve, std, var, newton, done, b):
    first, square, scaled, result = (newton[:, i, :] for i in range(4))
    dve.reciprocal(first, std).then_inc(done, 1)
    dve.wait_ge(done, b * 5 + 1)
    dve.tensor_tensor(square, first, first, ALU.mult).then_inc(done, 1)
    dve.wait_ge(done, b * 5 + 2)
    dve.scalar_tensor_tensor(out=scaled, in0=var, scalar=EPS, in1=square, op0=ALU.add, op1=ALU.mult).then_inc(done, 1)
    dve.wait_ge(done, b * 5 + 3)
    dve.tensor_scalar(square, scaled, -0.5, 1.5, ALU.mult, ALU.add).then_inc(done, 1)
    dve.wait_ge(done, b * 5 + 4)
    dve.tensor_tensor(result, first, square, ALU.mult).then_inc(done, 1)
    dve.wait_ge(done, b * 5 + 5)
    return result


SHARED = {
    (0, 0, 1): ("low", 0, 1), (0, 1, 0): ("out", -1, 3), (0, 1, 1): ("rows", -1, 0), (0, 2, 1): ("rows", -1, 1),
    (1, 0, 0): ("y", -1, 0), (1, 0, 1): ("low", 0, 2), (1, 1, 0): ("y", -1, 1), (1, 2, 0): ("out", 0, 0),
    (1, 2, 1): ("x2T", -1, 0), (1, 3, 1): ("x2T", -1, 1),
    (2, 0, 1): ("low", 0, 3), (2, 1, 0): ("out", 0, 1), (2, 3, 1): ("xnT", -1, 0),
    (3, 0, 1): ("low", 1, 0), (3, 1, 0): ("out", 0, 2), (3, 1, 1): ("xnT", -1, 1), (3, 2, 1): ("logits", -1, 0),
    (3, 3, 0): ("pick", -1, 0),
}
NORM_STEPS = {(1, 3): ("statistics", 0), (2, 0): ("statistics", 1), (2, 2): ("normalised", 0), (2, 3): ("normalised", 1)}
STEPS = [(g, k) for g in range(GROUPS) for k in range(TT)]
SHARED_ORDER = [SHARED[at] for at in sorted(SHARED)]
UNITS_OF = {"low": GROUPS, "out": GROUPS, "rows": KT, "y": 2,
            "x2T": KT, "xnT": KT, "logits": 1, "pick": 1}


def exists(b):
    return not isinstance(b, int) or 0 <= b < BATCH


def unit_no(kind, b, i):
    return b * UNITS_OF[kind] + i


def unit_before(b, unit):
    at = SHARED_ORDER.index(unit)
    for back in range(1, 2 * len(SHARED_ORDER) + 1):
        kind, off, i = SHARED_ORDER[(at - back) % len(SHARED_ORDER)]
        owner = b + (at - back) // len(SHARED_ORDER) + off
        if exists(owner):
            return kind, unit_no(kind, owner, i)


def group_after(b, g, steps):
    return b + (g + steps) // GROUPS, (g + steps) % GROUPS


def build_attend(nc, io, scratch, keep):
    with ExitStack() as ctx:
        n_ = Names(nc, ctx)
        ident = keep["ident"]
        q_st, k_st, wo = keep["q_st"], keep["k_st"], keep["wo"]
        v_st = [n_.sb(f"v_st{i}", [P, TT, GROUP, VW]) for i in range(GROUPS)]
        bo_gated = n_.sb("bo_gated", [P, DIM])
        low = n_.sb("low", [P, 2, GROUP * TT])
        low_rows = n_.sb("low_rows", [GROUP * TT, P], F32R)
        probs_T = n_.sb("probs_T", [P, TT, GROUP, SEQ])
        o_sb = n_.sb("o_sb", [P, SEQ])
        recip = n_.sb("recip", [P, TT, GROUP])
        attn = n_.sb("attn", [P, TT, DIM])
        attn_T = n_.sb("attn_T", [P, KT, SEQ])
        x_res = n_.sb("x_res", [P, TT, DIM])
        fits = n_.sb("fits", [P, 3, GROUP * TT])
        xn = n_.sb("xn_b", [P, TT, DIM])
        stats = n_.sb("stats_b", [P, TT, 6])
        moments = n_.sb("moments_b", [P, 10, TT])
        exponent, quarter, half, one = (n_.sb(name, [P, TT]) for name in ("exponent", "quarter", "half", "one"))
        gw_raw = n_.sb("gw_raw", [P, KT, EXPERTS])
        logits_T = n_.sb("logits_T", [P, SEQ])
        x_hi, x_lo, out_T, gw, pick, logits = (keep[name] for name in ("x_hi", "x_lo", "out_T", "gw", "pick", "logits"))
        fits_sum = n_.sb("fits_sum", [P, 1])
        ones = n_.sb("ones_b", [P, P])
        ps_s = [n_.ps(f"ps_s{i}", [P, 2, SEQ]) for i in range(2)]
        ps_t = [n_.ps(f"ps_t{i}", [P, SEQ]) for i in range(2)]
        ps_o = n_.ps("ps_o", [P, SEQ])
        ps_m = n_.ps("ps_m", [P, SEQ])

        consts_set = n_.sem("b_consts_set")
        bo_loaded = n_.sem("b_bo_loaded")
        bo_ready = n_.sem("b_bo_ready")
        qk_loaded = [n_.sem(f"b_qk_loaded{i}") for i in range(GROUPS)]
        v_loaded = [n_.sem(f"b_v_loaded{i}") for i in range(GROUPS)]
        scores_in_psum = n_.sem("b_scores_in_psum")
        low_done = n_.sem("b_low_done")
        rows_sent = n_.sem("b_rows_sent")
        t_in_psum = n_.sem("b_t_in_psum")
        exp_done = n_.sem("b_exp_done")
        pv_done = n_.sem("b_pv_done")
        o_copied = n_.sem("b_o_copied")
        in_psum = {kind: n_.sem(f"b_{kind}_in_psum") for kind in UNITS_OF}
        taken = {kind: n_.sem(f"b_{kind}_taken") for kind in UNITS_OF}
        recip_done = n_.sem("b_recip_done")
        lows_checked = n_.sem("b_lows_checked")
        x_loaded = n_.sem("b_x_loaded")
        x_biased = n_.sem("b_x_biased")
        stats_done = n_.sem("b_stats_done")
        moment_done = n_.sem("b_moment_done")
        rstd_done = n_.sem("b_rstd_done")
        xn_ready = n_.sem("b_xn_ready")
        hi_done = n_.sem("b_hi_done")
        gw_loaded = n_.sem("b_gw_loaded")
        gw_hi_done = n_.sem("b_gw_hi_done")
        gw_ready = n_.sem("b_gw_ready")
        o_zeroed = n_.sem("b_o_zeroed")
        fits_summed = n_.sem("b_fits_summed")
        fits_in_psum = n_.sem("b_fits_in_psum")
        block = ctx.enter_context(nc.Block())

        def head_no(b, g, j):
            return b * HEADS + g * GROUP + j

        def quad_no(b, g, k):
            return b * (GROUPS * TT) + g * TT + k

        def group_no(b, g):
            return b * GROUPS + g

        def batches(eng, batch):
            batch(0)
            with eng.Fori(1, BATCH - 1) as b:
                batch(b)
            batch(BATCH - 1)
            batch(BATCH)

        @block.sync
        def _(sp):
            def load_group(b, g):
                done = group_no(b, g) - GROUPS
                wait(sp, t_in_psum, (done + 1) * TT * GROUP)
                if not (isinstance(b, int) and b == 0 and g < GROUPS - 1):
                    load_qk(sp, scratch, keep, b, g, qk_loaded[g])
                wait(sp, pv_done, (done + 1) * TT)
                src = scratch["v"][bass.ds(b, 1), :, :].rearrange("a p (t h w) -> (a p) t (h w)", t=TT, h=HEADS)
                sp.dma_start(v_st[g][:].rearrange("p t h w -> p t (h w)"),
                             src[:, :, g * GROUP * VW:(g + 1) * GROUP * VW]).then_inc(v_loaded[g], 16)

            def send_lows(b, g):
                sp.wait_ge(taken["low"], group_no(b, g) + 1)
                for half in range(2):
                    row = half * 64 + 64 - ROWS
                    sp.dma_start(q_st[g][row:row + 1].rearrange("a k (t q) -> a (k t) q", q=P).bitcast(F32),
                                 low_rows[half * 8:half * 8 + 8, :].bitcast(F32)).then_inc(rows_sent, 16)

            def batch(b):
                for g in range(GROUPS):
                    ahead = group_after(b, g, 3)
                    if exists(ahead[0]) and exists(b):
                        load_group(*ahead)
                    ahead = group_after(b, g, 1)
                    if exists(ahead[0]) and exists(b):
                        send_lows(*ahead)
                if exists(b):
                    wait(sp, in_psum["x2T"], b * KT)
                    wait(sp, xn_ready, b * 2)
                    sp.dma_start(x_res[:], io["x"][bass.ds(b * SEQ, SEQ), :].rearrange("(t p) d -> p t d", p=P)).then_inc(x_loaded, 16)

            for g in range(GROUPS - 1):
                sp.sem_inc(qk_loaded[g], 128)
            sp.dma_start(gw_raw[:], io["gwT"].rearrange("(k p) e -> p k e", p=P)).then_inc(gw_loaded, 16)
            load_group(0, 0)
            sp.dma_start(bo_gated[:], io["bo"].rearrange("(a n) -> a n", a=1).to_broadcast([P, DIM])).then_inc(bo_loaded, 16)
            for g in (1, 2):
                load_group(0, g)
            send_lows(0, 0)
            batches(sp, batch)

        @block.gpsimd
        def _(pool):
            pool.memset(fits[:], 0.0).then_inc(consts_set, 1)
            pool.memset(gw[:].bitcast(F32), 0.0).then_inc(consts_set, 1)
            pool.memset(ones[:], 1.0).then_inc(consts_set, 1)
            for tile, value in ((exponent, -0.5), (quarter, 0.25), (half, 0.5), (one, 1.0)):
                pool.memset(tile[:], value).then_inc(consts_set, 1)
            pool.wait_ge(consts_set, 7)
            pool.wait_ge(bo_ready, 1)

            def reciprocal_root(b):
                mean, dev, diff, square, spread, var, root, root_2, scaled, rstd = (moments[:, i, :] for i in range(10))
                first = b * 9
                pool.wait_ge(stats_done, b * 2 + 2)
                wait(pool, xn_ready, b * 2)
                pool.tensor_tensor(diff, stats[:, :, 1], stats[:, :, 4], ALU.subtract)
                pool.tensor_tensor(dev, stats[:, :, 2], stats[:, :, 5], ALU.add)
                pool.tensor_tensor(root, stats[:, :, 1], stats[:, :, 4], ALU.add).then_inc(moment_done, 1)
                pool.wait_ge(moment_done, first + 1)
                pool.tensor_tensor(square, diff, diff, ALU.mult)
                pool.tensor_scalar(spread, dev, 1.0 / DIM, EPS, ALU.mult, ALU.add)
                pool.tensor_scalar(mean, root, 0.5, 0.0, ALU.mult, ALU.add).then_inc(moment_done, 1)
                pool.wait_ge(moment_done, first + 2)
                pool.tensor_tensor(diff, square, quarter[:], ALU.mult).then_inc(moment_done, 1)
                pool.wait_ge(moment_done, first + 3)
                pool.tensor_tensor(var, spread, diff, ALU.add).then_inc(moment_done, 1)
                pool.wait_ge(moment_done, first + 4)
                pool.tensor_tensor(root, var, exponent[:], ALU.pow).then_inc(moment_done, 1)
                pool.wait_ge(moment_done, first + 5)
                pool.tensor_tensor(root_2, root, root, ALU.mult).then_inc(moment_done, 1)
                pool.wait_ge(moment_done, first + 6)
                pool.tensor_tensor(scaled, root_2, var, ALU.mult).then_inc(moment_done, 1)
                pool.wait_ge(moment_done, first + 7)
                pool.tensor_tensor(root_2, one[:], scaled, ALU.subtract)
                pool.tensor_tensor(spread, root, half[:], ALU.mult).then_inc(moment_done, 1)
                pool.wait_ge(moment_done, first + 8)
                pool.tensor_tensor(dev, root_2, spread, ALU.mult).then_inc(moment_done, 1)
                pool.wait_ge(moment_done, first + 9)
                pool.tensor_tensor(rstd, root, dev, ALU.add).then_inc(rstd_done, 1)

            with pool.Fori(0, BATCH) as b:
                pool.wait_ge(x_loaded, b * 16 + 16)
                pool.tensor_tensor(x_res[:], x_res[:], bo_gated[:].rearrange("p (a d) -> p a d", a=1)
                                   .to_broadcast([P, TT, DIM]), ALU.add).then_inc(x_biased, 1)
                reciprocal_root(b)

        @block.tensor
        def _(pe):
            def scores(b, g, j, t):
                u, n = t // 2, head_no(b, g, j)
                if j == 0 and t == 0:
                    pe.wait_ge(qk_loaded[g], b * 128 + 128)
                if t % 2 == 0:
                    wait(pe, low_done, 2 * n - 1 + u)
                mm = pe.matmul(ps_s[u][:, t % 2, :], q_st[g][:, j // 2, t * P:(t + 1) * P], k_st[g][:, j, :],
                               start=True, stop=True)
                if t % 2 == 1:
                    mm.then_inc(scores_in_psum, 1)

            def scores_T(b, g, k, j):
                n = quad_no(b, g, k) * GROUP + j
                if k == 0 and j == 0:
                    pe.wait_ge(rows_sent, group_no(b, g) * 32 + 32)
                wait(pe, exp_done, n - 1)
                pe.matmul(ps_t[j % 2][:], k_st[g][:, j, k * P:(k + 1) * P], q_st[g][:, j // 2, :],
                          start=True, stop=True).then_inc(t_in_psum, 1)

            def probs_v(b, g, k):
                n = quad_no(b, g, k)
                if k == 0:
                    pe.wait_ge(v_loaded[g], b * 16 + 16)
                    wait(pe, o_copied, group_no(b, g))
                pe.wait_ge(exp_done, n * GROUP + GROUP)
                for j in range(GROUP):
                    mm = pe.matmul(ps_o[32 * j:32 * j + VW, :], v_st[g][:, k, j, :], probs_T[:, k, j, :],
                                   start=(k == 0), stop=(k == TT - 1))
                mm.then_inc(pv_done, 1)

            def turn_lows(b, i):
                pe.wait_ge(low_done, group_no(b, i) * 2 * GROUP + 2 * GROUP)
                return pe.transpose(ps_m[0:GROUP * TT, 0:P], low[:, i % 2, :], ident[:])

            def turn_out(b, i):
                pe.wait_ge(o_copied, group_no(b, i) + 1)
                for t in range(TT):
                    mm = pe.transpose(ps_m[:, t * P:(t + 1) * P], o_sb[:, t * P:(t + 1) * P], ident[:])
                return mm

            def turn_rows(b, i):
                pe.wait_ge(taken["out"], group_no(b, GROUPS - 1) + 1)
                for t in range(TT):
                    mm = pe.transpose(ps_m[:, t * P:(t + 1) * P], attn[:, t, i * P:(i + 1) * P], ident[:])
                return mm

            def project_out(b, i):
                pe.wait_ge(taken["rows"], b * KT + KT)
                for t in range(2):
                    t0 = (2 * i + t) * P
                    for k in range(KT):
                        mm = pe.matmul(ps_m[:, t * DIM:(t + 1) * DIM], attn_T[:, k, t0:t0 + P], wo[:, k, :],
                                       start=(k == 0), stop=(k == KT - 1))
                return mm

            def turn_x2(b, i):
                pe.wait_ge(taken["y"], b * 2 + 2)
                for t in range(TT):
                    mm = pe.transpose(ps_m[:, t * P:(t + 1) * P], x_res[:, t, i * P:(i + 1) * P], ident[:])
                return mm

            def turn_xn(b, i):
                pe.wait_ge(xn_ready, b * 2 + 2)
                for t in range(TT):
                    mm = pe.transpose(ps_m[:, t * P:(t + 1) * P], xn[:, t, i * P:(i + 1) * P], ident[:])
                return mm

            def gate_logits(b, i):
                pe.wait_ge(taken["xnT"], b * KT + KT)
                parts = [(x, k) for k in range(KT) for x in (x_hi, x_lo)]
                for n, (x, k) in enumerate(parts):
                    mm = pe.matmul(ps_m[:], gw[:, k, :], x[:, k, bass.ds(b * SEQ, SEQ)], start=(n == 0), stop=(n == len(parts) - 1))
                return mm

            def pick_logits(b, i):
                pe.wait_ge(taken["logits"], b + 1)
                for t in range(TT):
                    mm = pe.matmul(ps_m[:, t * EXPERTS:(t + 1) * EXPERTS], logits_T[:, t * P:(t + 1) * P], pick[:],
                                   start=True, stop=True)
                return mm

            write = {"low": turn_lows, "out": turn_out, "rows": turn_rows, "y": project_out,
                     "x2T": turn_x2, "xnT": turn_xn, "logits": gate_logits, "pick": pick_logits}

            def shared(b, unit):
                if not unit or not exists(b + unit[1]):
                    return
                kind, off, i = unit
                before = unit_before(b, unit)
                pe.wait_ge(taken[before[0]], before[1] + 1)
                write[kind](b + off, i).then_inc(in_psum[kind], 1)

            def batch(b):
                for g in range(GROUPS):
                    ahead = group_after(b, g, 2)
                    for k in range(TT):
                        back = (b, g, k - 1) if k else (*group_after(b, g, -1), TT - 1)
                        more = exists(ahead[0]) and exists(b)
                        if exists(b):
                            scores_T(b, g, k, 0)
                        if more:
                            scores(*ahead, k, 0)
                            scores(*ahead, k, 1)
                        if exists(b):
                            scores_T(b, g, k, 1)
                        if exists(back[0]):
                            probs_v(*back)
                        shared(b, SHARED.get((g, k, 0)))
                        if exists(b):
                            scores_T(b, g, k, 2)
                        if more:
                            scores(*ahead, k, 2)
                        if exists(b):
                            scores_T(b, g, k, 3)
                        if more:
                            scores(*ahead, k, 3)
                        shared(b, SHARED.get((g, k, 1)))

            pe.wait_ge(o_zeroed, 1)
            pe.wait_ge(gw_ready, 2)
            for g in range(2):
                for j in range(GROUP):
                    for t in range(TT):
                        scores(0, g, j, t)
                if g == 0:
                    turn_lows(0, 0).then_inc(in_psum["low"], 1)
            batches(pe, batch)
            pe.wait_ge(fits_summed, 1)
            pe.matmul(ps_m[:, 0:1], ones[:], fits_sum[:], start=True, stop=True).then_inc(fits_in_psum, 1)

        @block.vector
        def _(dve):
            dve.memset(ps_o[:], 0.0).then_inc(o_zeroed, 1)
            dve.wait_ge(consts_set, 7)
            dve.tensor_tensor(pick[:], ident[:, 0:EXPERTS], ident[:, EXPERTS:2 * EXPERTS], ALU.add).then_inc(gw_ready, 1)
            dve.wait_ge(gw_loaded, 16)
            dve.tensor_copy(gw[:, :, 0:EXPERTS], gw_raw[:]).then_inc(gw_hi_done, 1)
            dve.wait_ge(gw_hi_done, 1)
            dve.tensor_tensor(gw[:, :, EXPERTS:2 * EXPERTS], gw_raw[:], gw[:, :, 0:EXPERTS].bitcast(F32),
                              ALU.subtract).then_inc(gw_ready, 1)
            dve.wait_ge(bo_loaded, 16)
            dve.tensor_scalar(bo_gated[:], bo_gated[:], keep["tanh_g"][:, 0:1], None, ALU.mult).then_inc(bo_ready, 1)

            def lows(b, g, j, u):
                n = head_no(b, g, j)
                if j == 0 and u == 0:
                    wait(dve, in_psum["low"], group_no(b, g) - 1)
                    wait(dve, lows_checked, group_no(b, g) - 1)
                dve.wait_ge(scores_in_psum, 2 * n + u + 1)
                at = (j % 2) * 2 * TT + (j // 2) * TT + 2 * u
                dve.tensor_reduce(low[:, g % 2, at:at + 2], ps_s[u][:], AX_X, ALU.min).then_inc(low_done, 1)

            def check_lows(b, g):
                dve.wait_ge(low_done, group_no(b, g) * 2 * GROUP + 2 * GROUP)
                wait(dve, lows_checked, group_no(b, g))
                dve.scalar_tensor_tensor(out=fits[:, 0, :], in0=low[:, g % 2, :], scalar=FITS, in1=fits[:, 0, :],
                                         op0=ALU.is_le, op1=ALU.add)
                dve.scalar_tensor_tensor(out=fits[:, 1, :], in0=low[:, g % 2, :], scalar=-FITS, in1=fits[:, 1, :],
                                         op0=ALU.is_ge, op1=ALU.add).then_inc(lows_checked, 1)

            def normalise(b, i):
                n = group_no(b, i)
                dve.wait_ge(in_psum["out"], n + 1)
                if i == 0:
                    wait(dve, in_psum["rows"], b * KT)
                wait(dve, taken["out"], n)
                heads = ps_m[:].rearrange("p (t j w) -> p t j w", t=TT, j=GROUP)
                dve.reciprocal(recip[:], heads[:, :, :, HDIM]).then_inc(recip_done, 1)
                count = fits[:, 2, :].rearrange("p (t j) -> p t j", t=TT)
                dve.scalar_tensor_tensor(out=count, in0=heads[:, :, :, HDIM], scalar=SUM_LEAST, in1=count,
                                         op0=ALU.is_ge, op1=ALU.add)
                dve.wait_ge(recip_done, n + 1)
                dve.tensor_tensor(attn[:, :, i * GROUP * HDIM:(i + 1) * GROUP * HDIM].rearrange("p t (j d) -> p t j d", j=GROUP),
                                  heads[:, :, :, 0:HDIM],
                                  recip[:].rearrange("p t (j a) -> p t j a", a=1).to_broadcast([P, TT, GROUP, HDIM]),
                                  ALU.mult).then_inc(taken["out"], 1)

            def add_residual(b, i):
                if i == 0:
                    dve.wait_ge(x_biased, b + 1)
                dve.wait_ge(in_psum["y"], b * 2 + i + 1)
                part = x_res[:, 2 * i:2 * i + 2, :]
                dve.scalar_tensor_tensor(out=part, in0=ps_m[:].rearrange("p (t d) -> p t d", t=2),
                                         scalar=keep["tanh_g"][:, 0:1], in1=part,
                                         op0=ALU.mult, op1=ALU.add).then_inc(taken["y"], 1)

            def statistics(b, i):
                if i == 0:
                    wait(dve, rstd_done, b)
                dve.wait_ge(taken["y"], b * 2 + i + 1)
                for t in (2 * i, 2 * i + 1):
                    ins = dve.bn_stats(stats[:, t, :], x_res[:, t, :])
                ins.then_inc(stats_done, 1)

            def layer_norm(b, i):
                if i == 0:
                    dve.wait_ge(rstd_done, b + 1)
                    wait(dve, in_psum["xnT"], b * KT)
                for t in (2 * i, 2 * i + 1):
                    ins = dve.tensor_scalar(xn[:, t, :], x_res[:, t, :], moments[:, 0, t:t + 1], moments[:, 9, t:t + 1],
                                            ALU.subtract, ALU.mult)
                ins.then_inc(xn_ready, 1)

            def split(b, i):
                n = b * KT + i
                at = bass.ds(b * SEQ, SEQ)
                dve.wait_ge(hi_done, n + 1)
                dve.tensor_tensor(x_lo[:, i, at], ps_m[:], x_hi[:, i, at].bitcast(F32), ALU.subtract).then_inc(taken["xnT"], 1)

            def keep_logits(b, i):
                dve.wait_ge(in_psum["pick"], b + 1)
                dve.tensor_scalar(logits[:, :, bass.ds(b * TT, TT)], ps_m[:, 0:TT * EXPERTS].rearrange("p (t e) -> p e t", t=TT),
                                  1.0, None, ALU.mult).then_inc(taken["pick"], 1)

            take = {"out": normalise, "y": add_residual, "xnT": split, "pick": keep_logits}

            def take_unit(b, at):
                kind, off, i = SHARED.get(at, (None, 0, 0))
                if kind in take and exists(b + off):
                    take[kind](b + off, i)

            def batch(b):
                for g in range(GROUPS):
                    ahead = group_after(b, g, 2)
                    more = exists(ahead[0]) and exists(b)
                    for k in range(TT):
                        if more:
                            lows(*ahead, k, 0)
                        if (g, k) != (0, 0):
                            take_unit(b, STEPS[STEPS.index((g, k)) - 1] + (1,))
                        kind, i = NORM_STEPS.get((g, k), (None, 0))
                        if kind and exists(b - 1):
                            {"statistics": statistics, "normalised": layer_norm}[kind](b - 1, i)
                        if k == 0:
                            behind = group_after(b, g, 1)
                            if exists(behind[0]) and exists(b):
                                check_lows(*behind)
                        take_unit(b, (g, k, 0))
                        if more:
                            lows(*ahead, k, 1)

            for g in range(2):
                for j in range(GROUP):
                    for u in range(2):
                        lows(0, g, j, u)
                if g == 0:
                    check_lows(0, 0)
            batches(dve, batch)
            dve.wait_ge(lows_checked, BATCH * GROUPS)
            dve.wait_ge(taken["out"], BATCH * GROUPS)
            dve.tensor_reduce(fits_sum[:], fits[:].rearrange("p a n -> p (a n)"), AX_X, ALU.add).then_inc(fits_summed, 1)
            dve.wait_ge(fits_in_psum, 1)
            dve.tensor_scalar(keep["clip_flag"][:], ps_m[:, 0:1], 3 * HEADS * TOKENS - 0.5, None, ALU.is_lt)

        @block.scalar
        def _(act):
            def exps(b, g, k, heads):
                n = quad_no(b, g, k)
                if 0 in heads:
                    wait(act, pv_done, n - TT + 1)
                for j in heads:
                    act.wait_ge(t_in_psum, n * GROUP + j + 1)
                    act.activation(probs_T[:, k, j, :], ps_t[j % 2][:], ACT.Exp, scale=-1.0).then_inc(exp_done, 1)

            def copy_out(b, g):
                act.wait_ge(pv_done, quad_no(b, g, TT - 1) + 1)
                wait(act, in_psum["out"], group_no(b, g))
                act.activation(o_sb[:], ps_o[:], ACT.Copy).then_inc(o_copied, 1)

            def take_lows(b, i):
                n = group_no(b, i)
                act.wait_ge(in_psum["low"], n + 1)
                wait(act, rows_sent, n * 32)
                act.activation(low_rows[:], ps_m[0:GROUP * TT, 0:P], ACT.Copy, scale=-1.0).then_inc(taken["low"], 1)

            def take_rows(b, i):
                act.wait_ge(in_psum["rows"], b * KT + i + 1)
                wait(act, in_psum["y"], b * 2)
                act.activation(attn_T[:, i, :], ps_m[:], ACT.Copy).then_inc(taken["rows"], 1)

            def take_x2(b, i):
                if isinstance(b, int):
                    act.wait_ge(in_psum["x2T"], b * KT + i + 1)
                act.activation(out_T[:, i, bass.ds(b * SEQ, SEQ)], ps_m[:], ACT.Copy).then_inc(taken["x2T"], 1)

            def take_hi(b, i):
                if isinstance(b, int):
                    act.wait_ge(in_psum["xnT"], b * KT + i + 1)
                act.activation(x_hi[:, i, bass.ds(b * SEQ, SEQ)], ps_m[:], ACT.Copy).then_inc(hi_done, 1)

            def take_logits(b, i):
                act.wait_ge(in_psum["logits"], b + 1)
                wait(act, in_psum["pick"], b)
                act.activation(logits_T[:], ps_m[:], ACT.Copy).then_inc(taken["logits"], 1)

            take = {"low": take_lows, "rows": take_rows, "x2T": take_x2, "xnT": take_hi, "logits": take_logits}

            def take_unit(b, at):
                kind, off, i = SHARED.get(at, (None, 0, 0))
                if kind in take and exists(b + off):
                    take[kind](b + off, i)

            def batch(b):
                for g in range(GROUPS):
                    for k in range(TT):
                        if exists(b):
                            exps(b, g, k, (0, 1))
                        if (g, k) != (0, 0):
                            take_unit(b, STEPS[STEPS.index((g, k)) - 1] + (1,))
                        back = group_after(b, g, -1)
                        if k == 0 and exists(back[0]):
                            copy_out(*back)
                        if exists(b):
                            exps(b, g, k, (2, 3))

            take_lows(0, 0)
            batches(act, batch)


AHEAD = 2
SLOTS = 4
WIDE = 32


def transpose_units():
    units = []
    for n in range(HEADS):
        units += [("T", n, k) for k in range(TT)]
        if n == 1:
            units.append(("R", GROUPS - 1))
        if n == 4:
            units += [("Y", 0), ("Y", 1)]
        if n >= 5 and n % GROUP == 1:
            units.append(("R", (n - 5) // GROUP))
    return {u: i for i, u in enumerate(units)}


UNITS = transpose_units()
PER_BATCH = len(UNITS)
CARRIED = 3
assert PER_BATCH % 2 == 0


class Unit:

    def __init__(self, b, unit, epilogue=False):
        if epilogue:
            at, rounds = PER_BATCH * BATCH - CARRIED + {"R": 0, "Y": 1 + unit[1]}[unit[0]], None
            self.bank, self.before, self.order = at % 2, at // 2, at
            return
        carried = unit in (("R", GROUPS - 1), ("Y", 0), ("Y", 1))
        at = UNITS[unit] - CARRIED
        if isinstance(b, int) and b == 0:
            assert not carried
            at += sum(UNITS[c] > UNITS[unit] for c in (("R", GROUPS - 1), ("Y", 0), ("Y", 1)))
        self.bank = at % 2
        self.before = b * (PER_BATCH // 2) + at // 2
        self.order = b * PER_BATCH + at


def build_attend_clipped(nc, io, scratch, keep):
    with ExitStack() as ctx:
        n_ = Names(nc, ctx)
        q_size = GROUP // 2 * SEQ
        q_st = [flat(keep["x_hi"])[:, i * q_size:(i + 1) * q_size].rearrange("p (h k) -> p h k", k=SEQ) for i in range(2)]
        k_st = [flat(keep["x_hi"])[:, (i + 1) * 2 * q_size:(i + 2) * 2 * q_size].rearrange("p (h k) -> p h k", k=SEQ) for i in range(2)]
        v_st = [n_.sb(f"g_v_st{i}", [P, TT, GROUP, WIDE]) for i in range(2)]
        wo = n_.sb("g_wo", [P, GROUPS, DIM])
        probs = [flat(keep["out_T"])[:, i * TT * SEQ:(i + 1) * TT * SEQ].rearrange("p (t k) -> p t k", t=TT) for i in range(SLOTS)]
        low = n_.sb("g_low", [P, SLOTS, TT])
        sums = n_.sb("g_sums", [P, 2, GROUP, TT])
        recip = n_.sb("g_recip", [P, 2, GROUP, TT])
        probs_T = [n_.sb(f"g_probs_T{i}", [P, GROUP, TT, SEQ]) for i in range(2)]
        recip_wide = n_.sb("g_recip_wide", [P, 2, TT, GROUP, WIDE])
        recip_rows = n_.sb("g_recip_rows", [P, SEQ])
        heads_out = n_.sb("g_heads_out", [P, GROUPS, SEQ])
        x_res = n_.sb("g_x_res", [P, TT, DIM])
        ps_s = [n_.ps(f"g_ps_s{i}", [P, 2, SEQ]) for i in range(2)]
        ps_t = [n_.ps(f"g_ps_t{i}", [P, SEQ]) for i in range(2)]
        ps_o = [n_.ps(f"g_ps_o{i}", [P, SEQ]) for i in range(2)]

        zeroed = n_.sem("g_zeroed")
        wo_loaded = n_.sem("g_wo_loaded")
        qk_loaded = [n_.sem(f"g_qk_loaded{i}") for i in range(2)]
        v_loaded = [n_.sem(f"g_v_loaded{i}") for i in range(2)]
        scores_in_psum = n_.sem("g_scores_in_psum")
        clipped = n_.sem("g_clipped")
        low_ready = n_.sem("g_low_ready")
        probs_ready = n_.sem("g_probs_ready")
        unit_in_psum = n_.sem("g_unit_in_psum")
        unit_taken = [n_.sem(f"g_unit_taken{i}") for i in range(2)]
        pv_done = n_.sem("g_pv_done")
        recip_ready = n_.sem("g_recip_ready")
        recip_spread = n_.sem("g_recip_spread")
        heads_ready = n_.sem("g_heads_ready")
        x_loaded = n_.sem("g_x_loaded")
        x2_stored = n_.sem("g_x2_stored")
        block = ctx.enter_context(nc.Block())
        QK_DMAS = 16

        @block.sync
        def _(sp):
            clip = sp.value_load(keep["clip_flag"][0:1, 0:1], min_val=0, max_val=1)
            with sp.If(clip > 0):
                sp.wait_ge(zeroed, 5)
                for j in range(GROUP):
                    sp.dma_start(wo[32 * j:32 * j + HDIM, :, :],
                                 io["Wo"].rearrange("(g h d) n -> h d g n", g=GROUPS, h=GROUP)[j]).then_inc(wo_loaded, 16)
                sp.dma_start(wo[HDIM:HDIM + 1, 0, :], io["bo"].rearrange("(a n) -> a n", a=1)).then_inc(wo_loaded, 16)

                def load_group(b, g):
                    s = g % 2
                    gi = b * GROUPS + g
                    wait(sp, scores_in_psum, gi * 8 - 8)
                    for name, dst, parts in (("q", q_st[s], (0, 1, 0, 1)), ("k", k_st[s], (0, 0, 1, 1))):
                        for half in range(2):
                            for c, part in enumerate(parts):
                                row = 1 + HDIM * part
                                src = scratch[name][bass.ds(b, 1)].rearrange("a (g k h r) t -> (a g) h r k t", g=GROUPS, k=2, h=2)
                                src = src[g, half, row:row + HDIM]
                                at = half * 64 + c * HDIM
                                to = dst[at:at + HDIM, :, :] if name == "q" else dst[at:at + HDIM, half:GROUP:2, :]
                                sp.dma_start(to.bitcast(F32), src).then_inc(qk_loaded[s], 16)
                    wait(sp, pv_done, gi - 1)
                    src = scratch["v"][bass.ds(b, 1), :, :].rearrange("a p (t h w) -> (a p) t h w", t=TT, h=HEADS)
                    for t in range(TT):
                        sp.dma_start(v_st[s][:, t, :, 0:VW], src[:, t, g * GROUP:(g + 1) * GROUP]).then_inc(v_loaded[s], 16)

                def load_residual(b):
                    wait(sp, x2_stored, b * 16)
                    sp.dma_start(x_res[:], io["x"][bass.ds(b * SEQ, SEQ), :].rearrange("(t p) d -> p t d", p=P)).then_inc(x_loaded, 16)

                def store_x2(b, units):
                    for u in units:
                        sp.wait_ge(unit_taken[u.bank], u.before + 1)
                    sp.dma_start(scratch["x2"][bass.ds(b * SEQ, SEQ), :].rearrange("(t p) d -> p t d", p=P), x_res[:]).then_inc(x2_stored, 16)

                for g in range(GROUPS):
                    load_group(0, g)
                load_residual(0)
                with sp.Fori(1, BATCH) as b:
                    for g in range(GROUPS):
                        load_group(b, g)
                    store_x2(b - 1, [Unit(b, ("Y", i)) for i in range(2)])
                    load_residual(b)
                store_x2(BATCH - 1, [Unit(0, ("Y", i), epilogue=True) for i in range(2)])
                sp.wait_ge(x2_stored, 16 * BATCH)

        @block.gpsimd
        def _(pool):
            clip = pool.value_load(keep["clip_flag"][0:1, 0:1], min_val=0, max_val=1)
            with pool.If(clip > 0):
                pool.memset(wo[:], 0.0).then_inc(zeroed, 1)
                for s in range(2):
                    pool.memset(k_st[s][:].bitcast(F32), 0.0).then_inc(zeroed, 1)
                    pool.memset(v_st[s][:], 0.0).then_inc(zeroed, 1)

        @block.tensor
        def _(pe):
            clip = pe.value_load(keep["clip_flag"][0:1, 0:1], min_val=0, max_val=1)
            with pe.If(clip > 0):
                def scores(b, m):
                    if m >= HEADS:
                        b, m = b + 1, m - HEADS
                    g, j = m // GROUP, m % GROUP
                    s = g % 2
                    if j == 0:
                        pe.wait_ge(qk_loaded[s], b * (2 * 16 * QK_DMAS) + (g // 2 + 1) * 16 * QK_DMAS)
                    for u in range(2):
                        wait(pe, clipped, b * (2 * HEADS) + 2 * m - 1 + u)
                        for t in range(2):
                            q0 = (2 * u + t) * P
                            mm = pe.matmul(ps_s[u][:, t, :], q_st[s][:, j // 2, q0:q0 + P], k_st[s][:, j, :],
                                           start=True, stop=True)
                        mm.then_inc(scores_in_psum, 1)

                def transposes(b, m):
                    pe.wait_ge(probs_ready, b * HEADS + m + 1)
                    for k in range(TT):
                        u = Unit(b, ("T", m, k))
                        wait(pe, unit_taken[u.bank], u.before)
                        for t in range(TT):
                            mm = pe.transpose(ps_t[u.bank][:, t * P:(t + 1) * P], probs[m % SLOTS][:, t, k * P:(k + 1) * P],
                                              keep["ident"][:])
                        mm.then_inc(unit_in_psum, 1)

                def probs_v(b, g):
                    s = g % 2
                    gi = b * GROUPS + g
                    for k in (TT - 2, TT - 1):
                        u = Unit(b, ("T", g * GROUP + GROUP - 1, k))
                        pe.wait_ge(unit_taken[u.bank], u.before + 1)
                    pe.wait_ge(v_loaded[s], (b * 32 + (g // 2 + 1) * 16) * TT)
                    wait(pe, heads_ready, gi - 1)
                    for k in range(TT):
                        for j in range(GROUP):
                            mm = pe.matmul(ps_o[s][32 * j:32 * j + 32, :], v_st[s][:, k, j, :], probs_T[s][:, j, k, :],
                                           start=(k == 0), stop=(k == TT - 1))
                    mm.then_inc(pv_done, 1)

                def reciprocals(b, g, u):
                    pe.wait_ge(recip_spread, b * GROUPS + g + 1)
                    wait(pe, unit_taken[u.bank], u.before)
                    for t in range(TT):
                        mm = pe.matmul(ps_t[u.bank][:, t * P:(t + 1) * P],
                                       recip_wide[:, g % 2, t].rearrange("p j w -> p (j w)"), keep["ident"][:],
                                       start=True, stop=True)
                    mm.then_inc(unit_in_psum, 1)

                def project_out(b, units):
                    pe.wait_ge(heads_ready, b * GROUPS + GROUPS)
                    for i, u in enumerate(units):
                        wait(pe, unit_taken[u.bank], u.before)
                        for t in range(2):
                            t0 = (2 * i + t) * P
                            for g in range(GROUPS):
                                mm = pe.matmul(ps_t[u.bank][:, t * DIM:(t + 1) * DIM], heads_out[:, g, t0:t0 + P], wo[:, g, :],
                                               start=(g == 0), stop=(g == GROUPS - 1))
                        mm.then_inc(unit_in_psum, 1)

                def batch(b, first, last):
                    for m in range(HEADS):
                        if m + AHEAD < HEADS or not last:
                            scores(b, m + AHEAD)
                        if m == 1 and not first:
                            probs_v(b - 1, GROUPS - 1)
                        if m >= 5 and m % GROUP == 1:
                            probs_v(b, (m - 5) // GROUP)
                        transposes(b, m)
                        if m == 1 and not first:
                            reciprocals(b - 1, GROUPS - 1, Unit(b, ("R", GROUPS - 1)))
                        if m == 4 and not first:
                            project_out(b - 1, [Unit(b, ("Y", i)) for i in range(2)])
                        if m >= 5 and m % GROUP == 1:
                            g = (m - 5) // GROUP
                            reciprocals(b, g, Unit(b, ("R", g)))

                pe.wait_ge(zeroed, 5)
                for m in range(AHEAD):
                    scores(0, m)
                pe.wait_ge(wo_loaded, 16 * (GROUP + 1))
                batch(0, True, False)
                with pe.Fori(1, BATCH - 1) as b:
                    batch(b, False, False)
                batch(BATCH - 1, False, True)
                end = BATCH - 1
                probs_v(end, GROUPS - 1)
                reciprocals(end, GROUPS - 1, Unit(0, ("R", 0), epilogue=True))
                project_out(end, [Unit(0, ("Y", i), epilogue=True) for i in range(2)])

        @block.vector
        def _(dve):
            clip = dve.value_load(keep["clip_flag"][0:1, 0:1], min_val=0, max_val=1)
            with dve.If(clip > 0):
                def clip_and_low(b, m):
                    head2 = b * (2 * HEADS) + 2 * m
                    if m >= SLOTS:
                        dve.wait_ge(unit_in_psum, Unit(b, ("T", m - SLOTS, TT - 1)).order + 1)
                    elif not (isinstance(b, int) and b == 0):
                        dve.wait_ge(unit_in_psum, Unit(b - 1, ("T", m - SLOTS + HEADS, TT - 1)).order + 1)
                    for u in range(2):
                        dve.wait_ge(scores_in_psum, head2 + u + 1)
                        dve.tensor_scalar(probs[m % SLOTS][:, 2 * u:2 * u + 2, :], ps_s[u][:], CLAMP, -CLAMP,
                                          ALU.min, ALU.max).then_inc(clipped, 1)
                    for u in range(2):
                        dve.wait_ge(clipped, head2 + u + 1)
                        dve.tensor_reduce(low[:, m % SLOTS, 2 * u:2 * u + 2], probs[m % SLOTS][:, 2 * u:2 * u + 2, :],
                                          AX_X, ALU.min).then_inc(low_ready, 1)

                def invert(b, g):
                    gi = b * GROUPS + g
                    dve.wait_ge(probs_ready, gi * GROUP + GROUP)
                    dve.reciprocal(recip[:, g % 2], sums[:, g % 2]).then_inc(recip_ready, 1)
                    dve.wait_ge(recip_ready, gi + 1)
                    dve.tensor_copy(recip_wide[:, g % 2], recip[:, g % 2].rearrange("p j (t a) -> p t j a", a=1)
                                    .to_broadcast([P, TT, GROUP, WIDE])).then_inc(recip_spread, 1)

                def normalise(b, g, u):
                    dve.wait_ge(unit_taken[u.bank], u.before + 1)
                    dve.wait_ge(pv_done, b * GROUPS + g + 1)
                    dve.tensor_tensor(heads_out[:, g, :], ps_o[g % 2][:], recip_rows[:], ALU.mult).then_inc(heads_ready, 1)

                def add_residual(b, units):
                    dve.wait_ge(x_loaded, b * 16 + 16)
                    for i, u in enumerate(units):
                        dve.wait_ge(unit_in_psum, u.order + 1)
                        part = x_res[:, 2 * i:2 * i + 2, :]
                        dve.scalar_tensor_tensor(out=part, in0=ps_t[u.bank][:].rearrange("p (t d) -> p t d", t=2),
                                                 scalar=keep["tanh_g"][:, 0:1], in1=part,
                                                 op0=ALU.mult, op1=ALU.add).then_inc(unit_taken[u.bank], 1)

                def batch(b, first):
                    for m in range(HEADS):
                        clip_and_low(b, m)
                        if m == 1 and not first:
                            invert(b - 1, GROUPS - 1)
                        if m >= 5 and m % GROUP == 1:
                            invert(b, (m - 5) // GROUP)
                        if m == 3 and not first:
                            normalise(b - 1, GROUPS - 1, Unit(b, ("R", GROUPS - 1)))
                        if m >= 7 and m % GROUP == 3:
                            g = (m - 7) // GROUP
                            normalise(b, g, Unit(b, ("R", g)))
                        if m == 5 and not first:
                            add_residual(b - 1, [Unit(b, ("Y", i)) for i in range(2)])

                batch(0, True)
                with dve.Fori(1, BATCH) as b:
                    batch(b, False)
                end = BATCH - 1
                invert(end, GROUPS - 1)
                normalise(end, GROUPS - 1, Unit(0, ("R", 0), epilogue=True))
                add_residual(end, [Unit(0, ("Y", i), epilogue=True) for i in range(2)])

        @block.scalar
        def _(act):
            clip = act.value_load(keep["clip_flag"][0:1, 0:1], min_val=0, max_val=1)
            with act.If(clip > 0):
                def exps(b, m):
                    g, j = m // GROUP, m % GROUP
                    if j == 0:
                        wait(act, recip_ready, b * GROUPS + g - 1)
                    for u in range(2):
                        act.wait_ge(low_ready, b * (2 * HEADS) + 2 * m + u + 1)
                        for t in (2 * u, 2 * u + 1):
                            tile = probs[m % SLOTS][:, t, :]
                            ins = act.activation(tile, tile, ACT.Exp, bias=low[:, m % SLOTS, t:t + 1], scale=-1.0,
                                                 accum_out=sums[:, g % 2, j, t:t + 1])
                    ins.then_inc(probs_ready, 1)

                def evacuate(b, m):
                    g, j = m // GROUP, m % GROUP
                    if j == 0:
                        wait(act, pv_done, b * GROUPS + g - 1)
                    for k in range(TT):
                        u = Unit(b, ("T", m, k))
                        act.wait_ge(unit_in_psum, u.order + 1)
                        act.activation(probs_T[g % 2][:, j, k, :], ps_t[u.bank][:], ACT.Copy).then_inc(unit_taken[u.bank], 1)

                def take_reciprocals(b, g, u):
                    act.wait_ge(unit_in_psum, u.order + 1)
                    wait(act, heads_ready, b * GROUPS + g)
                    act.activation(recip_rows[:], ps_t[u.bank][:], ACT.Copy).then_inc(unit_taken[u.bank], 1)

                def batch(b, first):
                    for m in range(HEADS):
                        exps(b, m)
                        if m == 0 and not first:
                            evacuate(b - 1, HEADS - 1)
                        if m > 0:
                            evacuate(b, m - 1)
                        if m == 2 and not first:
                            take_reciprocals(b - 1, GROUPS - 1, Unit(b, ("R", GROUPS - 1)))
                        if m >= 6 and m % GROUP == 2:
                            g = (m - 6) // GROUP
                            take_reciprocals(b, g, Unit(b, ("R", g)))

                batch(0, True)
                with act.Fori(1, BATCH) as b:
                    batch(b, False)
                end = BATCH - 1
                evacuate(end, HEADS - 1)
                take_reciprocals(end, GROUPS - 1, Unit(0, ("R", 0), epilogue=True))


RING = 4
LEAD = 2
BITS = 31
TILES = TOKENS // P
PAIRS = EXPERTS // 2


def build_experts(nc, io, scratch, keep):
    with ExitStack() as ctx:
        n = Names(nc, ctx)
        ident = keep["ident"]
        x_hi, x_lo, out_T, gw, pick, logits = (keep[name] for name in ("x_hi", "x_lo", "out_T", "gw", "pick", "logits"))
        w_raw = n.sb("w_raw", [P, KT * HIDDEN])
        w1_hi = [n.sb(f"w1_hi{i}", [P, KT, HIDDEN], F32R) for i in range(2)]
        w1_lo = [n.sb(f"w1_lo{i}", [P, KT, HIDDEN], F32R) for i in range(2)]
        w2_hi = [n.sb(f"w2_hi{i}", [P, HT, DIM], F32R) for i in range(2)]
        w2_lo = [n.sb(f"w2_lo{i}", [P, HT, DIM], F32R) for i in range(2)]
        b1 = [n.sb(f"b1_{i}", [P, HT]) for i in range(2)]
        b2 = [n.sb(f"b2_{i}", [P, KT]) for i in range(2)]
        gelu = n.sb("gelu", [P, RING, SEQ])
        h_hi = n.sb("h_hi", [P, RING, SEQ], F32R)
        h_lo = n.sb("h_lo", [P, RING, SEQ], F32R)
        gate = n.sb("gate", [P, SEQ])
        gated = n.sb("gated", [P, KT, SEQ])
        x2_t = [gelu[:, 2 * i:2 * i + 2, :].rearrange("p a (b d) -> p (a b) d", d=DIM) for i in range(2)]
        xn = gated[:].rearrange("p a (b d) -> p (a b) d", d=DIM)
        logits_T = gate
        zero = n.sb("zero_c", [P, 1])
        eps = n.sb("eps_c", [P, 1])
        stats = n.sb("stats_c", [P, TT, 6])
        meanvar = n.sb("meanvar_c", [P, 4, TT])
        std = n.sb("std_c", [P, TT])
        newton = n.sb("newton_c", [P, 4, TT])
        ones = n.sb("ones_c", [P, P])
        signed = n.sb("signed", [P, EXPERTS, TILES])
        below = n.sb("below", [P, EXPERTS, TILES])
        gates_T = n.sb("gates_T", [P, 2, P])
        count = n.sb("count", [P, 1])
        negative = n.sb("negative", [P, 1])
        sign = n.sb("sign", [P, 1])
        rank = n.sb("rank", [P, 1])
        bit = n.sb("bit", [P, 1])
        next_bit = n.sb("next_bit", [P, 1], I32)
        change = n.sb("change", [P, 1], I32)
        candidate = n.sb("candidate", [P, 1], I32)
        kth = n.sb("kth", [P, 1])
        ps_h = n.ps("ps_h", [P, RING, SEQ])
        ps_y = [n.ps(f"ps_y{i}", [P, KT, SEQ]) for i in range(2)]
        ps_l, ps_c = ps_y
        ps_xn, ps_x2 = ps_h[:, 0:2, :], ps_h[:, 2:4, :]

        consts_set = n.sem("c_consts_set")
        x2_loaded = [n.sem(f"c_x2_loaded{i}") for i in range(2)]
        stats_done = n.sem("c_stats_done")
        std_done = n.sem("c_std_done")
        newton_done = n.sem("c_newton_done")
        xn_ready = n.sem("c_xn_ready")
        turned = n.sem("c_turned")
        hi_done = n.sem("c_hi_done")
        lo_done = n.sem("c_lo_done")
        logits_in_psum = n.sem("c_logits_in_psum")
        logits_T_ready = n.sem("c_logits_T_ready")
        x2T_kept = n.sem("c_x2T_kept")
        picked = n.sem("c_picked")
        logits_kept = n.sem("c_logits_kept")
        bit_set = n.sem("c_bit_set")
        step = n.sem("c_step")
        counted = n.sem("c_counted")
        summed = n.sem("c_summed")
        gates_ready = n.sem("c_gates_ready")
        gates_in_psum = n.sem("c_gates_in_psum")
        gates_T_ready = n.sem("c_gates_T_ready")
        gates_stored = n.sem("c_gates_stored")

        raw_loaded = n.sem("d_raw_loaded")
        w_hi_done = n.sem("d_w_hi_done")
        w_ready = n.sem("d_w_ready")
        bias_loaded = [n.sem(f"d_bias_loaded{i}") for i in range(2)]
        gate_loaded = n.sem("d_gate_loaded")
        h_in_psum = n.sem("d_h_in_psum")
        gelu_done = n.sem("d_gelu_done")
        h_hi_done = n.sem("d_h_hi_done")
        h_ready = n.sem("d_h_ready")
        w2_done = n.sem("d_w2_done")
        y_taken = n.sem("d_y_taken")
        added = n.sem("d_added")
        out_stored = n.sem("d_out_stored")
        block = ctx.enter_context(nc.Block())

        def tile_no(e, c, j):
            return e * (BATCH * HT) + c * HT + j

        def chunk_no(e, c):
            return e * BATCH + c

        @block.sync
        def _(sp):
            def load_x2(bb, p):
                b = bb * 2 + p
                wait(sp, turned, b - 1)
                sp.dma_start(x2_t[p], scratch["x2"][bass.ds(b, 1), :].rearrange("a (t p d) -> p (a t) d", p=P, d=DIM)).then_inc(x2_loaded[p], 16)

            def load_w(e, half):
                wait(sp, w_ready, e * 2 + half)
                if half == 0:
                    src = io["w1T"][bass.ds(e, 1), :, :].rearrange("a (k p) h -> p (a k) h", p=P)
                    dst = w_raw[:].rearrange("p (k h) -> p k h", k=KT)
                else:
                    src = io["w2T"][bass.ds(e, 1), :, :].rearrange("a (j p) d -> p (a j) d", p=P)
                    dst = w_raw[:].rearrange("p (j d) -> p j d", j=HT)
                sp.dma_start(dst, src).then_inc(raw_loaded, 16)

            def load_bias(e, p):
                sp.dma_start(b1[p][:], io["b1"][bass.ds(e, 1), :, :].rearrange("a p j -> (a p) j")).then_inc(bias_loaded[p], 16)
                sp.dma_start(b2[p][:], io["b2"][bass.ds(e, 1), :, :].rearrange("a p j -> (a p) j")).then_inc(bias_loaded[p], 16)

            def load_gate(e, c):
                sp.wait_ge(y_taken, chunk_no(e, c) + 2)
                src = scratch["gates"][bass.ds(chunk_no(e, c), 1), :]
                sp.dma_start(gate[:], src.to_broadcast([P, SEQ])).then_inc(gate_loaded, 16)

            clip = sp.value_load(keep["clip_flag"][0:1, 0:1], min_val=0, max_val=1)
            for half in range(2):
                load_w(0, half)
            load_bias(0, 0)
            with sp.If(clip > 0):
                for p in range(2):
                    load_x2(0, p)
                with sp.Fori(1, BATCH // 2) as bb:
                    for p in range(2):
                        load_x2(bb, p)
            sp.wait_ge(gates_T_ready, 1)
            for half in range(2):
                rows = scratch["gates"].rearrange("r (a t) -> (r a) t", t=P)[half * P:(half + 1) * P, :]
                sp.dma_start(rows, gates_T[:, half, :]).then_inc(gates_stored, 16)
            sp.wait_ge(gates_stored, 32)

            def expert(e, p, last):
                load_gate(e, 0)
                if not last:
                    load_w(e + 1, 0)
                    load_bias(e + 1, 1 - p)
                load_gate(e, 1)
                if not last:
                    load_w(e + 1, 1)
                if not last:
                    with sp.Fori(2, BATCH) as c:
                        load_gate(e, c)

            with sp.Fori(0, PAIRS - 1) as pair:
                for p in range(2):
                    expert(pair * 2 + p, p, False)
            expert(EXPERTS - 2, 0, False)
            expert(EXPERTS - 1, 1, True)

            def store(c):
                sp.wait_ge(added, chunk_no(EXPERTS - 1, c) + 1)
                sp.dma_start(io["out_T"].rearrange("(k p) t -> p k t", p=P)[:, :, bass.ds(c * SEQ, SEQ)],
                             out_T[:, :, bass.ds(c * SEQ, SEQ)]).then_inc(out_stored, 16)

            for c in range(BATCH):
                if c + 2 < BATCH:
                    load_gate(EXPERTS - 1, c + 2)
                store(c)
            sp.wait_ge(out_stored, 16 * BATCH)

        @block.gpsimd
        def _(pool):
            pool.memset(zero[:], 0.0).then_inc(consts_set, 1)
            pool.memset(ones[:], 1.0).then_inc(consts_set, 1)
            pool.memset(bit[:], float(1 << BITS)).then_inc(consts_set, 1)
            pool.memset(next_bit[:], 1 << (BITS - 1)).then_inc(consts_set, 1)
            pool.memset(candidate[:], 1 << (BITS - 1)).then_inc(consts_set, 1)
            pool.memset(eps[:], EPS).then_inc(consts_set, 1)
            pool.wait_ge(consts_set, 6)

            def split(e, half, hi, lo):
                at = e * 2 + half
                pool.wait_ge(raw_loaded, at * 16 + 16)
                if half == 0:
                    wait(pool, w2_done, tile_no(e, 0, 0) - BATCH * HT + RING if not isinstance(e, int) or e >= 2 else 0)
                hi, lo = (w[:].rearrange("p a b -> p (a b)") for w in (hi, lo))
                pool.tensor_tensor(hi, w_raw[:], zero[:].to_broadcast([P, KT * HIDDEN]), ALU.add).then_inc(w_hi_done, 1)
                pool.wait_ge(w_hi_done, at + 1)
                pool.tensor_tensor(lo, w_raw[:], hi.bitcast(F32), ALU.subtract).then_inc(w_ready, 1)

            def expert(e, p):
                split(e, 0, w1_hi[p], w1_lo[p])
                split(e, 1, w2_hi[p], w2_lo[p])

            for p in range(2):
                expert(p, p)
            with pool.Fori(1, PAIRS) as pair:
                for p in range(2):
                    expert(pair * 2 + p, p)

        @block.tensor
        def _(pe):
            pe.wait_ge(consts_set, 6)

            clip = pe.value_load(keep["clip_flag"][0:1, 0:1], min_val=0, max_val=1)
            with pe.If(clip > 0):
                def turn(bb, p):
                    b = bb * 2 + p
                    pe.wait_ge(x2_loaded[p], bb * 16 + 16)
                    pe.wait_ge(x2T_kept, b)
                    for k in range(KT):
                        for t in range(TT):
                            pe.transpose(ps_x2[:, k, t * P:(t + 1) * P], x2_t[p][:, t, k * P:(k + 1) * P], ident[:])
                    pe.wait_ge(xn_ready, b + 1)
                    pe.wait_ge(lo_done, b)
                    for k in range(KT):
                        for t in range(TT):
                            mm = pe.transpose(ps_xn[:, k, t * P:(t + 1) * P], xn[:, t, k * P:(k + 1) * P], ident[:])
                    mm.then_inc(turned, 1)
                    pe.wait_ge(logits_T_ready, b)
                    pe.wait_ge(lo_done, b + 1)
                    for i, (part, k) in enumerate((part, k) for k in range(KT) for part in (x_hi, x_lo)):
                        mm = pe.matmul(ps_l[:, 0, :], gw[:, k, :], part[:, k, bass.ds(b * SEQ, SEQ)],
                                       start=(i == 0), stop=(i == 2 * KT - 1))
                    mm.then_inc(logits_in_psum, 1)
                    pe.wait_ge(logits_kept, b)
                    pe.wait_ge(logits_T_ready, b + 1)
                    for t in range(TT):
                        mm = pe.matmul(ps_l[:, 1, t * EXPERTS:(t + 1) * EXPERTS], logits_T[:, t * P:(t + 1) * P], pick[:],
                                       start=True, stop=True)
                    mm.then_inc(picked, 1)

                with pe.Fori(0, BATCH // 2) as bb:
                    for p in range(2):
                        turn(bb, p)
                pe.wait_ge(x2T_kept, BATCH)

            with pe.Fori(0, BITS + 1) as i:
                pe.wait_ge(counted, i + 1)
                pe.matmul(ps_c[:, 0, 0:1], ones[:], count[:], start=True, stop=True).then_inc(summed, 1)
            pe.wait_ge(gates_ready, 1)
            for half in range(2):
                mm = pe.transpose(ps_c[:, 1, half * P:(half + 1) * P],
                                  signed[:, half * 4:half * 4 + 4, :].rearrange("p e t -> p (e t)"), ident[:])
            mm.then_inc(gates_in_psum, 1)

            pe.sem_inc(w2_done, RING)
            pe.wait_ge(gates_T_ready, 1)

            def first(e, p, c, j):
                pe.wait_ge(gelu_done, tile_no(e, c, j) + 1)
                at = slice(j * P, (j + 1) * P)
                parts = [(w, x, k) for k in range(KT)
                         for w, x in ((w1_hi[p], x_hi), (w1_hi[p], x_lo), (w1_lo[p], x_hi))]
                for i, (w, x, k) in enumerate(parts):
                    mm = pe.matmul(ps_h[:, j % RING, :], w[:, k, at], x[:, k, bass.ds(c * SEQ, SEQ)],
                                   start=(i == 0), stop=(i == len(parts) - 1))
                mm.then_inc(h_in_psum, 1)

            def second(e, p, c, j, s):
                if j == 0:
                    pe.wait_ge(y_taken, chunk_no(e, c) + 1)
                pe.wait_ge(h_ready, tile_no(e, c, j) + 1 + RING)
                for d in range(KT):
                    at = slice(d * P, (d + 1) * P)
                    for i, (w, h) in enumerate(((w2_hi[p], h_hi), (w2_hi[p], h_lo), (w2_lo[p], h_hi))):
                        mm = pe.matmul(ps_y[s][:, d, :], w[:, j, at], h[:, j % RING, :],
                                       start=(j == 0 and i == 0), stop=(j == HT - 1 and i == 2))
                mm.then_inc(w2_done, 1)

            def chunk(e, p, c, s, ahead):
                for j in range(HT):
                    if j + LEAD < HT:
                        first(e, p, c, j + LEAD)
                    elif ahead:
                        ahead(j + LEAD - HT)
                    second(e, p, c, j, s)

            def start(e, p, j):
                if j == 0:
                    pe.wait_ge(w_ready, e * 2 + 2)
                first(e, p, 0, j)

            def expert(e, p, last):
                with pe.Fori(0, BATCH // 2 - 1) as cc:
                    for s in range(2):
                        chunk(e, p, cc * 2 + s, s, lambda j: first(e, p, cc * 2 + s + 1, j))
                chunk(e, p, BATCH - 2, 0, lambda j: first(e, p, BATCH - 1, j))
                chunk(e, p, BATCH - 1, 1, None if last else lambda j: start(e + 1, 1 - p, j))

            for j in range(LEAD):
                start(0, 0, j)
            with pe.Fori(0, PAIRS - 1) as pair:
                for p in range(2):
                    expert(pair * 2 + p, p, False)
            expert(EXPERTS - 2, 0, False)
            expert(EXPERTS - 1, 1, True)

        @block.scalar
        def _(act):
            act.wait_ge(consts_set, 6)
            act.sem_inc(gelu_done, RING)
            clip = act.value_load(keep["clip_flag"][0:1, 0:1], min_val=0, max_val=1)
            with act.If(clip > 0):
                with act.Fori(0, BATCH) as b:
                    act.wait_ge(stats_done, b * 4 + 4)
                    act.activation(std[:], meanvar[:, 1, :], ACT.Sqrt, bias=eps[:, 0:1]).then_inc(std_done, 1)
                    act.wait_ge(picked, b)
                    act.wait_ge(logits_in_psum, b + 1)
                    act.activation(logits_T[:], ps_l[:, 0, :], ACT.Copy).then_inc(logits_T_ready, 1)
                    act.activation(out_T[:, :, bass.ds(b * SEQ, SEQ)], ps_x2, ACT.Copy).then_inc(x2T_kept, 1)
            act.wait_ge(gates_in_psum, 1)
            act.activation(gates_T[:].rearrange("p h t -> p (h t)"), ps_c[:, 1, 0:2 * P], ACT.Copy).then_inc(gates_T_ready, 1)

            with act.Fori(0, PAIRS) as pair:
                for p in range(2):
                    e = pair * 2 + p
                    act.wait_ge(bias_loaded[p], pair * 32 + 32)
                    with act.Fori(0, BATCH) as c:
                        for j in range(HT):
                            act.wait_ge(h_ready, tile_no(e, c, j) + 1)
                            act.wait_ge(h_in_psum, tile_no(e, c, j) + 1)
                            act.activation(gelu[:, j % RING, :], ps_h[:, j % RING, :], ACT.Gelu_apprx_tanh,
                                           bias=b1[p][:, j:j + 1]).then_inc(gelu_done, 1)

        @block.vector
        def _(dve):
            dve.wait_ge(consts_set, 6)
            clip = dve.value_load(keep["clip_flag"][0:1, 0:1], min_val=0, max_val=1)
            with dve.If(clip > 0):
                def normalise(bb, p):
                    b = bb * 2 + p
                    dve.wait_ge(x2_loaded[p], bb * 16 + 16)
                    dve.wait_ge(xn_ready, b)
                    mean_variance(dve, [x2_t[p][:, t, :] for t in range(TT)], stats, meanvar, stats_done, b)
                    dve.wait_ge(std_done, b + 1)
                    rstd = reciprocal_root(dve, std[:], meanvar[:, 1, :], newton, newton_done, b)
                    dve.wait_ge(turned, b)
                    for t in range(TT):
                        ins = dve.tensor_scalar(xn[:, t, :], x2_t[p][:, t, :], meanvar[:, 0, t:t + 1], rstd[:, t:t + 1],
                                                ALU.subtract, ALU.mult)
                    ins.then_inc(xn_ready, 1)

                def split(b):
                    at = bass.ds(b * SEQ, SEQ)
                    dve.wait_ge(turned, b + 1)
                    dve.tensor_scalar(x_hi[:, :, at], ps_xn, 1.0, None, ALU.mult).then_inc(hi_done, 1)
                    dve.wait_ge(hi_done, b + 1)
                    dve.tensor_tensor(x_lo[:, :, at], ps_xn, x_hi[:, :, at].bitcast(F32), ALU.subtract).then_inc(lo_done, 1)

                def keep_logits(b):
                    dve.wait_ge(picked, b + 1)
                    dve.tensor_scalar(logits[:, :, bass.ds(b * TT, TT)],
                                      ps_l[:, 1, 0:TT * EXPERTS].rearrange("p (t e) -> p e t", t=TT),
                                      1.0, None, ALU.mult).then_inc(logits_kept, 1)

                normalise(0, 0)
                with dve.Fori(0, BATCH // 2 - 1) as bb:
                    for p in range(2):
                        split(bb * 2 + p)
                        normalise(bb + p, 1 - p)
                        keep_logits(bb * 2 + p)
                split(BATCH - 2)
                normalise(BATCH // 2 - 1, 1)
                keep_logits(BATCH - 2)
                split(BATCH - 1)
                keep_logits(BATCH - 1)
                dve.wait_ge(logits_kept, BATCH)

            total = EXPERTS * TOKENS
            dve.tensor_scalar(below[:], logits[:], 0.0, None, ALU.is_lt, ALU.add, accum_out=count[:]).then_inc(counted, 1)
            dve.wait_ge(summed, 1)
            dve.tensor_scalar(negative[:], ps_c[:, 0, 0:1], KEPT_FROM + 0.5, None, ALU.is_gt).then_inc(step, 1)
            dve.wait_ge(step, 1)
            dve.tensor_scalar(sign[:], negative[:], -2.0, 1.0, ALU.mult, ALU.add).then_inc(step, 1)
            dve.tensor_scalar(rank[:], negative[:], float(total - 1 - 2 * KEPT_FROM), float(KEPT_FROM),
                              ALU.mult, ALU.add).then_inc(step, 1)
            dve.wait_ge(step, 3)
            dve.tensor_scalar(signed[:], logits[:], sign[:, 0:1], None, ALU.mult).then_inc(step, 1)
            dve.wait_ge(step, 4)
            with dve.Fori(0, BITS) as i:
                dve.wait_ge(step, i * 2 + 4)
                dve.tensor_scalar(below[:], signed[:], candidate[:].bitcast(F32), None, ALU.is_lt, ALU.add,
                                  accum_out=count[:]).then_inc(counted, 1)
                dve.tensor_scalar(bit[:], bit[:], 0.5, None, ALU.mult)
                dve.tensor_scalar(next_bit[:], next_bit[:], 1, None, ALU.logical_shift_right).then_inc(bit_set, 1)
                dve.wait_ge(bit_set, i + 1)
                dve.wait_ge(summed, i + 2)
                dve.tensor_scalar(change[:], ps_c[:, 0, 0:1], rank[:, 0:1], bit[:, 0:1], ALU.is_gt, ALU.mult).then_inc(step, 1)
                dve.wait_ge(step, i * 2 + 5)
                dve.scalar_tensor_tensor(out=candidate[:], in0=change[:], scalar=next_bit[:, 0:1], in1=candidate[:],
                                         op0=ALU.bitwise_or, op1=ALU.bitwise_xor).then_inc(step, 1)
            dve.wait_ge(step, BITS * 2 + 4)
            dve.tensor_tensor(kth[:], candidate[:].bitcast(F32), sign[:], ALU.mult).then_inc(step, 1)
            dve.wait_ge(step, BITS * 2 + 5)
            dve.scalar_tensor_tensor(out=below[:], in0=logits[:], scalar=kth[:, 0:1], in1=logits[:],
                                     op0=ALU.is_ge, op1=ALU.mult).then_inc(step, 1)
            dve.wait_ge(step, BITS * 2 + 6)
            dve.tensor_scalar(signed[:], below[:], keep["tanh_g"][:, 1:2], None, ALU.mult).then_inc(gates_ready, 1)

            dve.sem_inc(h_ready, RING)
            dve.sem_inc(y_taken, 2)

            def halves(e, c, j):
                at = tile_no(e, c, j)
                dve.wait_ge(w2_done, at + 1)
                dve.wait_ge(gelu_done, at + 1 + RING)
                dve.tensor_copy(h_hi[:, j % RING, :], gelu[:, j % RING, :]).then_inc(h_hi_done, 1)
                dve.wait_ge(h_hi_done, at + 1)
                dve.tensor_tensor(h_lo[:, j % RING, :], gelu[:, j % RING, :], h_hi[:, j % RING, :].bitcast(F32),
                                  ALU.subtract).then_inc(h_ready, 1)

            def add_chunk(e, p, c, s):
                dve.wait_ge(gate_loaded, chunk_no(e, c) * 16 + 16)
                dve.wait_ge(added, chunk_no(e, c))
                dve.wait_ge(w2_done, tile_no(e, c, HT) + RING)
                for d in range(KT):
                    ins = dve.scalar_tensor_tensor(out=gated[:, d, :], in0=ps_y[s][:, d, :], scalar=b2[p][:, d:d + 1],
                                                   in1=gate[:], op0=ALU.add, op1=ALU.mult)
                ins.then_inc(y_taken, 1)
                dve.wait_ge(y_taken, chunk_no(e, c) + 3)
                part = out_T[:, :, bass.ds(c * SEQ, SEQ)]
                dve.tensor_tensor(part, part, gated[:], ALU.add).then_inc(added, 1)

            def chunk(e, c, before):
                for j in range(HT):
                    halves(e, c, j)
                    if j == LEAD and before:
                        before()

            def expert(e, p, begin):
                if begin:
                    chunk(e, 0, None)
                else:
                    chunk(e, 0, lambda: add_chunk(e - 1, 1 - p, BATCH - 1, 1))
                chunk(e, 1, lambda: add_chunk(e, p, 0, 0))
                with dve.Fori(1, BATCH // 2) as cc:
                    for s in range(2):
                        chunk(e, cc * 2 + s, lambda: add_chunk(e, p, cc * 2 + s - 1, 1 - s))

            for p in range(2):
                expert(p, p, p == 0)
            with dve.Fori(1, PAIRS) as pair:
                for p in range(2):
                    expert(pair * 2 + p, p, False)
            add_chunk(EXPERTS - 1, 1, BATCH - 1, 1)


def build(nc, io):
    with ExitStack() as ctx:
        n = Names(nc, ctx)
        keep = {"ident": n.sb("ident", [P, P]), "tanh_g": n.sb("tanh_g", [P, 2]), "clip_flag": n.sb("clip_flag", [P, 1], I32)}

        def scratch_of(name, shape):
            return nc.dram_tensor(name, shape, F32).ap()

        scratch = {
            "q": scratch_of("q_scratch", (BATCH, HEADS * KEPT, SEQ)),
            "k": scratch_of("k_scratch", (BATCH, HEADS * KEPT, SEQ)),
            "v": scratch_of("v_scratch", (BATCH, P, TT * HEADS * VW)),
            "x2": scratch_of("x2_scratch", (TOKENS, DIM)),
            "gates": scratch_of("gates_scratch", (EXPERTS * BATCH, SEQ)),
        }
        with ExitStack() as loads_ctx:
            loads = Names(nc, loads_ctx)
            keep["q_st"] = [loads.sb(f"q_st{i}", [P, GROUP // 2, SEQ], F32R, "right") for i in range(GROUPS)]
            keep["k_st"] = [loads.sb(f"k_st{i}", [P, GROUP, SEQ], F32R, "right") for i in range(GROUPS)]
            keep["wo"] = loads.sb("wo", [P, KT, DIM], F32, "right")
            build_project(nc, io, scratch, keep)
            for name in ("x_hi", "x_lo"):
                keep[name] = n.sb(name, [P, KT, TOKENS], F32R)
            keep["out_T"] = n.sb("out_T_acc", [P, KT, TOKENS])
            keep["gw"] = n.sb("gw", [P, KT, P], F32R)
            keep["pick"] = n.sb("pick", [P, EXPERTS])
            keep["logits"] = n.sb("logits", [P, EXPERTS, TILES])
            build_attend(nc, io, scratch, keep)
        build_attend_clipped(nc, io, scratch, keep)
        scratch["x2"] = scratch["x2"].rearrange("(b s) d -> b (s d)", b=BATCH)
        build_experts(nc, io, scratch, keep)


def kernel(**inputs):
    import numpy as np
    import concourse.bacc as bacc
    from concourse.bass_utils import run_bass_kernel_spmd

    a = {k: np.asarray(v) for k, v in inputs.items()}
    attn = {w: a[f"L0_xattn_{w}"] for w in ("Wq", "bq", "Wk", "bk", "Wv", "bv", "Wo", "bo")}
    arrays = {
        "x": a["x"].reshape(TOKENS, DIM),
        "ctxT": a["ctx_768"].transpose(0, 2, 1),
        "g_xattn": a["g_xattn"],
        "g_ffn": a["g_ffn"],
        **attn,
        "bq": attn["bq"].reshape(KT, P).T,
        "gwT": a["L0_ffn_gate_weight"].T,
        "w1T": a["L0_ffn_w1"].transpose(0, 2, 1),
        "b1": a["L0_ffn_b1"].reshape(EXPERTS, HT, P).transpose(0, 2, 1),
        "w2T": a["L0_ffn_w2"].transpose(0, 2, 1),
        "b2": a["L0_ffn_b2"].reshape(EXPERTS, KT, P).transpose(0, 2, 1),
    }
    nc = bacc.Bacc("TRN2", target_bir_lowering=False, num_devices=1)
    io, feeds = {}, {}
    for name, array in arrays.items():
        feeds[f"in_{name}"] = np.ascontiguousarray(array)
        io[name] = nc.dram_tensor(f"in_{name}", array.shape, mybir.dt.from_np(array.dtype), kind="ExternalInput").ap()
    io["out_T"] = nc.dram_tensor("out_T", (DIM, TOKENS), F32, kind="ExternalOutput").ap()
    build(nc, io)
    result = run_bass_kernel_spmd(nc, [feeds], core_ids=[0])
    return np.ascontiguousarray(result.results[0]["out_T"].T).reshape(BATCH, SEQ, DIM)
```

```python
from contextlib import ExitStack

import concourse.bass as bass
from concourse import mybir

F32 = mybir.dt.float32
F32R = mybir.dt.float32r
I32 = mybir.dt.int32
ALU = mybir.AluOpType
ACT = mybir.ActivationFunctionType
AX_X = mybir.AxisListType.X

P = 128
BATCH, SEQ, DIM = 8, 512, 256
CTX = 192
TOKENS = BATCH * SEQ
HEADS, HDIM = 16, 16
CLAMP = 10000.0
EXPERTS, HIDDEN = 8, 1024
EPS = 1e-5
KEPT_FROM = 4 * 256 * 6 - 1
KT = DIM // P
TT = SEQ // P
GROUP = 4
GROUPS = HEADS // GROUP
VW = HDIM + 1
ROWS = 1 + 3 * HDIM
KEPT = 1 + 2 * HDIM
FITS = CLAMP - 104.0
SUM_LEAST = 0.01
HT = HIDDEN // P
FIRST_GROUPS = 2
STORES = 16 * (2 * 2 * KT + 1)


def wait(eng, sem, value):
    if isinstance(value, int) and value <= 0:
        return
    eng.wait_ge(sem, value)


class Names:

    def __init__(self, nc, ctx):
        self.nc, self.ctx = nc, ctx

    def sb(self, name, shape, dt=F32, side=None):
        return self.ctx.enter_context(self.nc.sbuf_tensor(name, shape, dt, side=side))

    def ps(self, name, shape):
        return self.ctx.enter_context(self.nc.psum_tensor(name, shape, F32))

    def sem(self, name):
        return self.ctx.enter_context(self.nc.semaphore(name))


def flat(tile):
    return tile[:].rearrange("p a b -> p (a b)")


def build_project(nc, io, scratch, keep):
    with ExitStack() as ctx:
        n = Names(nc, ctx)
        q_hl, k_hl = ([n.sb(f"{name}_hl{i}", [P, 2, KT, SEQ], F32R) for i in range(2)] for name in ("q", "k"))
        v_out = [n.sb(f"v_out{i}", [P, TT, HEADS, VW]) for i in range(2)]
        w_raw, w_hi, w_lo = ({w: n.sb(f"{w}_{part}", [P, KT, DIM], dt) for w in ("wk", "wq", "wv")}
                             for part, dt in (("raw", F32), ("hi", F32R), ("lo", F32R)))
        zero = n.sb("zero_a", [P, 1])
        bq = n.sb("bq_col", [P, KT])
        bq_scaled = n.sb("bq_scaled", [P, KT])
        gates_in = n.sb("gates_in", [P, 2])
        eps = n.sb("eps_a", [P, 1])
        x_t = [n.sb(f"x_t{i}", [P, TT, DIM]) for i in range(2)]
        ctx_t = [n.sb(f"ctx_t{i}", [P, KT, SEQ]) for i in range(2)]
        ctx_hi, ctx_lo = ([n.sb(f"ctx_{part}{i}", [P, KT, SEQ], F32R) for i in range(2)] for part in ("hi", "lo"))
        stats = n.sb("stats_a", [P, TT, 6])
        meanvar = n.sb("meanvar_a", [P, 4, TT])
        std = n.sb("std_a", [P, TT])
        newton = n.sb("newton_a", [P, 4, TT])
        xn = [n.sb(f"xn_a{i}", [P, TT, DIM]) for i in range(2)]
        xn_hi, xn_lo = (n.sb(f"xn_{part}", [P, KT, SEQ], F32R) for part in ("hi", "lo"))
        q_full = n.sb("q_full", [P, KT, SEQ])
        const_rows = n.sb("const_rows", [P, 2, SEQ])
        ps_x = n.ps("ps_x", [P, KT, SEQ])
        ps_q = n.ps("ps_q", [P, KT, SEQ])
        ps_k = n.ps("ps_k", [P, KT, SEQ])
        ps_v = n.ps("ps_v", [P, TT, DIM])

        zeroed = n.sem("a_zeroed")
        fills_set = n.sem("a_fills_set")
        consts_moved = n.sem("a_consts_moved")
        first_loaded = n.sem("a_first_loaded")
        ones_set = n.sem("a_ones_set")
        ident_set = n.sem("a_ident_set")
        w_loaded = {w: n.sem(f"a_{w}_loaded") for w in w_raw}
        w_split = n.sem("a_w_split")
        ctx_split = n.sem("a_ctx_split")
        xn_hi_done = n.sem("a_xn_hi_done")
        small_loaded = n.sem("a_small_loaded")
        x_loaded = [n.sem(f"a_x_loaded{i}") for i in range(2)]
        ctx_loaded = [n.sem(f"a_ctx_loaded{i}") for i in range(2)]
        bq_ready = n.sem("a_bq_ready")
        eps_set = n.sem("a_eps_set")
        stats_done = n.sem("a_stats_done")
        std_done = n.sem("a_std_done")
        newton_done = n.sem("a_newton_done")
        xn_ready = n.sem("a_xn_ready")
        xT_in_psum = n.sem("a_xT_in_psum")
        xT_ready = n.sem("a_xT_ready")
        q_in_psum = n.sem("a_q_in_psum")
        k_in_psum = n.sem("a_k_in_psum")
        v_in_psum = n.sem("a_v_in_psum")
        q_full_ready = n.sem("a_q_full_ready")
        k_hi_done = n.sem("a_k_hi_done")
        q_hi_done = n.sem("a_q_hi_done")
        q_split = n.sem("a_q_split")
        k_split = n.sem("a_k_split")
        v_ready = n.sem("a_v_ready")
        stored = keep["stored"]
        block = ctx.enter_context(nc.Block())
        rest = CTX - P

        def pairs(eng, pair):
            pair(0, False)
            with eng.Fori(1, BATCH // 2 - 1) as bb:
                pair(bb, False)
            pair(BATCH // 2 - 1, True)

        @block.sync
        def _(sp):
            def load_x(bb, p):
                b = bb * 2 + p
                wait(sp, xn_ready, b - 1)
                sp.dma_start(x_t[p][:], io["x"][bass.ds(b * SEQ, SEQ), :].rearrange("(t p) d -> p t d", p=P)).then_inc(x_loaded[p], 16)

            def load_ctx(bb, p):
                b = bb * 2 + p
                wait(sp, ctx_split, b * 2 - 2)
                sp.dma_start(ctx_t[p][:, 0, :], io["ctxT"][bass.ds(b, 1), 0:P, :].rearrange("a c t -> (a c) t")).then_inc(ctx_loaded[p], 16)
                sp.dma_start(ctx_t[p][0:rest, 1, :], io["ctxT"][bass.ds(b, 1), P:CTX, :].rearrange("a c t -> (a c) t")).then_inc(ctx_loaded[p], 16)

            def store_qk(bb, p):
                b = bb * 2 + p
                for name, tile, ready in (("k", k_hl[p], k_split), ("q", q_hl[p], q_split)):
                    sp.wait_ge(ready, b + 1)
                    rows = scratch[name][bass.ds(b, 1)].rearrange("a (k h r) t -> h r (a k) t", k=KT, r=KEPT)
                    for part in range(2):
                        for k in range(KT):
                            sp.dma_start(rows[:, 1 + part * HDIM:1 + (part + 1) * HDIM, k], tile[:, part, k].bitcast(F32)).then_inc(stored[p], 16)

            def store_v(bb, p):
                b = bb * 2 + p
                sp.wait_ge(v_ready, b + 1)
                sp.dma_start(scratch["v"][bass.ds(b, 1), :, :].rearrange("a p n -> p (a n)"),
                             v_out[p][:].rearrange("p t h w -> p (t h w)")).then_inc(stored[p], 16)

            def load_with_bias(w, w_in, b_in):
                sp.dma_start(w_raw[w][:, 0, :], io[w_in][0:P, :]).then_inc(w_loaded[w], 16)
                sp.dma_start(w_raw[w][0:rest, 1, :], io[w_in][P:CTX, :]).then_inc(w_loaded[w], 16)
                sp.dma_start(w_raw[w][rest:rest + 1, 1, :], io[b_in].rearrange("(a n) -> a n", a=1)).then_inc(w_loaded[w], 16)

            load_x(0, 0)
            sp.wait_ge(zeroed, 2)
            load_with_bias("wk", "Wk", "bk")
            load_ctx(0, 0)
            sp.dma_start(w_raw["wq"][:], io["Wq"].rearrange("(k p) n -> p k n", p=P)).then_inc(w_loaded["wq"], 16)
            for i, gate in enumerate(("g_xattn", "g_ffn")):
                sp.dma_start(gates_in[:, i:i + 1], io[gate].rearrange("(a b) -> a b", a=1).to_broadcast([P, 1])).then_inc(small_loaded, 16)
            sp.dma_start(bq[:], io["bq"]).then_inc(small_loaded, 16)
            load_with_bias("wv", "Wv", "bv")
            load_x(0, 1)
            load_ctx(0, 1)
            sp.dma_start(keep["wo"][:], io["Wo"].rearrange("(k p) n -> p k n", p=P)).then_inc(consts_moved, 16)
            sp.wait_ge(fills_set, 2)
            for i, name in enumerate(("q", "k")):
                sp.dma_start(scratch[name].rearrange("b (h r) t -> (b h) r t", r=KEPT)[:, 0, :], const_rows[:, i, :]).then_inc(consts_moved, 16)
            with sp.Fori(0, BATCH // 2 - 1) as bb:
                for p in range(2):
                    load_x(bb + 1, p)
                    load_ctx(bb + 1, p)
                    store_qk(bb, p)
                    store_v(bb, p)
            sp.wait_ge(fills_set, 3)
            sp.wait_ge(consts_moved, 48)
            sp.wait_ge(stored[0], STORES)
            for g in range(FIRST_GROUPS):
                load_qk(sp, scratch, keep, 0, g, first_loaded)
            for p in range(2):
                store_qk(BATCH // 2 - 1, p)
                store_v(BATCH // 2 - 1, p)
            sp.wait_ge(first_loaded, 128 * FIRST_GROUPS)

        @block.gpsimd
        def _(pool):
            for w in ("wk", "wv"):
                pool.memset(w_raw[w][rest:P, 1, :], 0.0).then_inc(zeroed, 1)
            for p in range(2):
                pool.memset(ctx_t[p][rest:P, 1, :], 0.0).then_inc(zeroed, 1)
            pool.wait_ge(zeroed, 4)
            for p in range(2):
                pool.memset(ctx_t[p][rest:rest + 1, 1, :], 1.0).then_inc(ones_set, 1)
            pool.wait_ge(ones_set, 2)
            pool.memset(keep["ident"][:], 0.0).then_inc(ident_set, 1)
            pool.wait_ge(ident_set, 1)
            pool.affine_select(out=keep["ident"][:], in_=keep["ident"][:], compare_op=ALU.not_equal, fill=1.0,
                               base=0, pattern=[[-1, P]], channel_multiplier=1).then_inc(ident_set, 1)
            pool.wait_ge(ident_set, 2)
            pool.memset(zero[:], 0.0).then_inc(ones_set, 1)
            pool.wait_ge(ones_set, 3)

            def split_weights(i, w, loads):
                pool.wait_ge(w_loaded[w], loads * 16)
                pool.tensor_tensor(w_hi[w][:], w_raw[w][:], zero[:].rearrange("p (a b) -> p a b", a=1).to_broadcast([P, KT, DIM]),
                                   ALU.add).then_inc(w_split, 1)
                pool.wait_ge(w_split, 2 * i + 1)
                pool.tensor_tensor(w_lo[w][:], w_raw[w][:], w_hi[w][:].bitcast(F32), ALU.subtract).then_inc(w_split, 1)

            def split_ctx(bb, p):
                b = bb * 2 + p
                pool.wait_ge(ctx_loaded[p], bb * 32 + 32)
                wait(pool, v_in_psum, b - 1)
                pool.tensor_tensor(ctx_hi[p][:], ctx_t[p][:], zero[:].rearrange("p (a b) -> p a b", a=1).to_broadcast([P, KT, SEQ]),
                                   ALU.add).then_inc(ctx_split, 1)
                pool.wait_ge(ctx_split, b * 2 + 1)
                pool.tensor_tensor(ctx_lo[p][:], ctx_t[p][:], ctx_hi[p][:].bitcast(F32), ALU.subtract).then_inc(ctx_split, 1)

            split_weights(0, "wk", 3)
            split_ctx(0, 0)
            split_weights(1, "wq", 1)
            split_weights(2, "wv", 3)
            for p in range(2):
                pool.memset(v_out[p][:], 1.0).then_inc(ones_set, 1)
            split_ctx(0, 1)
            for i in range(2):
                pool.memset(const_rows[:, i, :], float(i)).then_inc(fills_set, 1)
            for s in range(GROUPS):
                pool.memset(keep["q_st"][s][:].bitcast(F32), 0.0)
                ins = pool.memset(keep["k_st"][s][:].bitcast(F32), 0.0)
            ins.then_inc(fills_set, 1)
            pool.memset(keep["nan_flag"][:], 0)
            with pool.Fori(1, BATCH // 2) as bb:
                for p in range(2):
                    split_ctx(bb, p)

        @block.tensor
        def _(pe):
            pe.wait_ge(ident_set, 2)

            def product(out, w, x):
                parts = [(a, b, k) for k in range(KT) for a, b in ((0, 0), (0, 1), (1, 0))]
                for i, (a, b, k) in enumerate(parts):
                    mm = pe.matmul(out, w(a, k), x(b, k), start=(i == 0), stop=(i == len(parts) - 1))
                return mm

            def turn(bb, p):
                b = bb * 2 + p
                pe.wait_ge(xn_ready, b + 1)
                wait(pe, xT_ready, b)
                for k in range(KT):
                    for t in range(TT):
                        mm = pe.transpose(ps_x[:, k, t * P:(t + 1) * P], xn[p][:, t, k * P:(k + 1) * P], keep["ident"][:])
                mm.then_inc(xT_in_psum, 1)

            def project(bb, p):
                b = bb * 2 + p
                if isinstance(bb, int) and b == 0:
                    pe.wait_ge(w_split, 2)
                pe.wait_ge(ctx_split, b * 2 + 2)
                wait(pe, k_split, b)
                wk, wq = ((w_hi[w], w_lo[w]) for w in ("wk", "wq"))
                ctx_parts, xn_parts = (ctx_hi[p], ctx_lo[p]), (xn_hi, xn_lo)
                for m in range(KT):
                    mm = product(ps_k[:, m, :], lambda a, k: wk[a][:, k, m * P:(m + 1) * P], lambda a, k: ctx_parts[a][:, k, :])
                mm.then_inc(k_in_psum, 1)
                if isinstance(bb, int) and b == 0:
                    pe.wait_ge(w_split, 4)
                pe.wait_ge(xT_ready, b + 1)
                wait(pe, q_full_ready, b * 2)
                for m in range(KT):
                    mm = product(ps_q[:, m, :], lambda a, k: wq[a][:, k, m * P:(m + 1) * P], lambda a, k: xn_parts[a][:, k, :])
                mm.then_inc(q_in_psum, 1)

            def values(bb, p):
                b = bb * 2 + p
                if isinstance(bb, int) and b == 0:
                    pe.wait_ge(w_split, 6)
                wait(pe, v_ready, b)
                ctx_parts, wv = (ctx_hi[p], ctx_lo[p]), (w_hi["wv"], w_lo["wv"])
                for t in range(TT):
                    mm = product(ps_v[:, t, :], lambda a, k: ctx_parts[a][:, k, t * P:(t + 1) * P], lambda a, k: wv[a][:, k, :])
                mm.then_inc(v_in_psum, 1)

            def pair(bb, last):
                for p in range(2):
                    project(bb, p)
                    if not (last and p == 1):
                        turn(bb + p, 1 - p)
                    values(bb, p)

            turn(0, 0)
            pairs(pe, pair)

        @block.scalar
        def _(act):
            act.wait_ge(eps_set, 1)

            def root(bb, p):
                b = bb * 2 + p
                act.wait_ge(stats_done, b * 4 + 4)
                act.activation(std[:], meanvar[:, 1, :], ACT.Sqrt, bias=eps[:, 0:1]).then_inc(std_done, 1)

            def take_x(bb, p):
                b = bb * 2 + p
                act.wait_ge(xT_in_psum, b + 1)
                wait(act, q_in_psum, b)
                act.activation(xn_hi[:], ps_x[:], ACT.Copy).then_inc(xn_hi_done, 1)

            def take_qk(bb, p):
                b = bb * 2 + p
                wait(act, stored[p], bb * STORES)
                act.wait_ge(k_in_psum, b + 1)
                act.activation(k_hl[p][:, 0], ps_k[:], ACT.Copy).then_inc(k_hi_done, 1)
                act.wait_ge(q_in_psum, b + 1)
                wait(act, q_split, b)
                for m in range(KT):
                    act.activation(q_full[:, m, :], ps_q[:, m, :], ACT.Identity, bias=bq_scaled[:, m:m + 1],
                                   scale=-(HDIM ** -0.5)).then_inc(q_full_ready, 1)

            def take_v(bb, p):
                b = bb * 2 + p
                act.wait_ge(v_in_psum, b + 1)
                act.activation(v_out[p][:, :, :, 0:HDIM], ps_v[:].rearrange("p t (h d) -> p t h d", h=HEADS),
                               ACT.Copy).then_inc(v_ready, 1)

            def pair(bb, last):
                for p in range(2):
                    more = not (last and p == 1)
                    if more:
                        root(bb + p, 1 - p)
                    take_qk(bb, p)
                    if more:
                        take_x(bb + p, 1 - p)
                    take_v(bb, p)

            root(0, 0)
            act.wait_ge(small_loaded, 48)
            act.activation(bq_scaled[:], bq[:], ACT.Copy, scale=-(HDIM ** -0.5)).then_inc(bq_ready, 1)
            take_x(0, 0)
            act.activation(keep["tanh_g"][:], gates_in[:], ACT.Tanh)
            act.wait_ge(bq_ready, 1)
            act.wait_ge(ones_set, 5)
            pairs(act, pair)

        @block.vector
        def _(dve):
            dve.memset(eps[:], EPS).then_inc(eps_set, 1)
            dve.wait_ge(eps_set, 1)

            def layer_norm(bb, p):
                b = bb * 2 + p
                dve.wait_ge(x_loaded[p], bb * 16 + 16)
                wait(dve, xn_ready, b)
                mean_variance(dve, [x_t[p][:, t, :] for t in range(TT)], stats, meanvar, stats_done, b)
                dve.wait_ge(std_done, b + 1)
                rstd = reciprocal_root(dve, std[:], meanvar[:, 1, :], newton, newton_done, b)
                wait(dve, xT_in_psum, b - 1)
                for t in range(TT):
                    ins = dve.tensor_scalar(xn[p][:, t, :], x_t[p][:, t, :], meanvar[:, 0, t:t + 1], rstd[:, t:t + 1],
                                            ALU.subtract, ALU.mult)
                ins.then_inc(xn_ready, 1)

            def take(bb, p):
                b = bb * 2 + p
                wait(dve, stored[p], bb * STORES)
                dve.wait_ge(k_hi_done, b + 1)
                dve.tensor_tensor(k_hl[p][:, 1], ps_k[:], k_hl[p][:, 0].bitcast(F32), ALU.subtract).then_inc(k_split, 1)
                dve.wait_ge(q_full_ready, b * 2 + 2)
                dve.tensor_copy(q_hl[p][:, 0], q_full[:]).then_inc(q_hi_done, 1)
                dve.wait_ge(q_hi_done, b + 1)
                dve.tensor_tensor(q_hl[p][:, 1], q_full[:], q_hl[p][:, 0].bitcast(F32), ALU.subtract).then_inc(q_split, 1)

            def split_x(bb, p):
                dve.wait_ge(xn_hi_done, bb * 2 + p + 1)
                dve.tensor_tensor(xn_lo[:], ps_x[:], xn_hi[:].bitcast(F32), ALU.subtract).then_inc(xT_ready, 1)

            def pair(bb, last):
                for p in range(2):
                    if not (last and p == 1):
                        layer_norm(bb + p, 1 - p)
                    take(bb, p)
                    if not (last and p == 1):
                        split_x(bb + p, 1 - p)

            layer_norm(0, 0)
            split_x(0, 0)
            pairs(dve, pair)


def load_qk(sp, scratch, keep, b, g, loaded):
    for name, dst, pieces in (("q", keep["q_st"][g], ((0, KEPT), (1, 1 + HDIM))),
                              ("k", keep["k_st"][g], ((0, 1 + HDIM), (1, KEPT)))):
        src = scratch[name][bass.ds(b, 1)].rearrange("a (g k h r) t -> (a g) h r k t", g=GROUPS, k=2, h=2)
        for half in range(2):
            row = half * 64 + 64 - ROWS
            for lo, hi in pieces:
                to = dst[row:row + hi - lo, :, :] if name == "q" else dst[row:row + hi - lo, half:GROUP:2, :]
                sp.dma_start(to.bitcast(F32), src[g, half, lo:hi]).then_inc(loaded, 16)
                row += hi - lo


def mean_variance(dve, tiles, stats, meanvar, done, b):
    size = tiles[0].shape[-1]
    for t, tile in enumerate(tiles):
        ins = dve.bn_stats(stats[:, t, :], tile)
    ins.then_inc(done, 1)
    dve.wait_ge(done, b * 4 + 1)
    mean, var, diff, dev = (meanvar[:, i, :] for i in range(4))
    dve.tensor_tensor(mean, stats[:, :, 1], stats[:, :, 4], ALU.add)
    dve.tensor_tensor(diff, stats[:, :, 1], stats[:, :, 4], ALU.subtract)
    dve.tensor_tensor(dev, stats[:, :, 2], stats[:, :, 5], ALU.add).then_inc(done, 1)
    dve.wait_ge(done, b * 4 + 2)
    dve.tensor_scalar(mean, mean, 0.5, None, ALU.mult)
    dve.tensor_scalar(dev, dev, 1.0 / size, None, ALU.mult)
    dve.scalar_tensor_tensor(out=diff, in0=diff, scalar=0.25, in1=diff, op0=ALU.mult, op1=ALU.mult).then_inc(done, 1)
    dve.wait_ge(done, b * 4 + 3)
    dve.tensor_tensor(var, dev, diff, ALU.add).then_inc(done, 1)


def reciprocal_root(dve, std, var, newton, done, b):
    first, square, scaled, result = (newton[:, i, :] for i in range(4))
    dve.reciprocal(first, std).then_inc(done, 1)
    dve.wait_ge(done, b * 5 + 1)
    dve.tensor_tensor(square, first, first, ALU.mult).then_inc(done, 1)
    dve.wait_ge(done, b * 5 + 2)
    dve.scalar_tensor_tensor(out=scaled, in0=var, scalar=EPS, in1=square, op0=ALU.add, op1=ALU.mult).then_inc(done, 1)
    dve.wait_ge(done, b * 5 + 3)
    dve.tensor_scalar(square, scaled, -0.5, 1.5, ALU.mult, ALU.add).then_inc(done, 1)
    dve.wait_ge(done, b * 5 + 4)
    dve.tensor_tensor(result, first, square, ALU.mult).then_inc(done, 1)
    dve.wait_ge(done, b * 5 + 5)
    return result


SHARED = {
    (0, 0, 1): ("low", 0, 1), (0, 1, 0): ("out", -1, 3), (0, 1, 1): ("rows", -1, 0),
    (0, 2, 1): ("rows", -1, 1), (0, 3, 1): ("y", -1, 0), (1, 0, 1): ("low", 0, 2),
    (1, 1, 0): ("y", -1, 1), (1, 1, 1): ("out", 0, 0), (1, 2, 1): ("x2T", -1, 0),
    (1, 3, 1): ("x2T", -1, 1), (2, 0, 1): ("low", 0, 3), (2, 1, 1): ("out", 0, 1),
    (2, 2, 1): ("xnT", -1, 0), (2, 3, 1): ("xnT", -1, 1), (3, 0, 1): ("low", 1, 0),
    (3, 1, 0): ("out", 0, 2), (3, 1, 1): ("logits", -1, 0), (3, 3, 0): ("pick", -1, 0),
}
NORM_STEPS = {(1, 1): ("statistics", 0), (1, 2): ("statistics", 1), (2, 1): ("normalised", 0), (2, 2): ("normalised", 1)}
STEPS = [(g, k) for g in range(GROUPS) for k in range(TT)]
SHARED_ORDER = [SHARED[at] for at in sorted(SHARED)]
LATE = [(kind, i) for kind, off, i in SHARED_ORDER if off == -1]
LATE_BANKS = 4
BANKS = 3
PRODUCTS = HEADS * TT
BANK_OF = [i % BANKS for i in range(PRODUCTS)]
BANK_OF[-1] = 1
UNITS_OF = {"low": GROUPS, "out": GROUPS, "rows": KT, "y": 2,
            "x2T": KT, "xnT": KT, "logits": 1, "pick": 1}


def exists(b):
    return not isinstance(b, int) or 0 <= b < BATCH


def unit_no(kind, b, i):
    return b * UNITS_OF[kind] + i


def unit_before(b, unit):
    late = LATE.index((unit[0], unit[2])) if isinstance(b, int) and b == BATCH else 0
    if late:
        late -= LATE_BANKS
        return None if late < 0 else (LATE[late][0], unit_no(LATE[late][0], BATCH - 1, LATE[late][1]))
    at = SHARED_ORDER.index(unit)
    for back in range(1, 2 * len(SHARED_ORDER) + 1):
        kind, off, i = SHARED_ORDER[(at - back) % len(SHARED_ORDER)]
        owner = b + (at - back) // len(SHARED_ORDER) + off
        if exists(owner):
            return kind, unit_no(kind, owner, i)


def group_after(b, g, steps):
    return b + (g + steps) // GROUPS, (g + steps) % GROUPS


def load_weights(sp, io, to, e, half):
    name, at = ("w1T", "a (k p) h -> p (a k) h") if half == 0 else ("w2T", "a (j p) d -> p (a j) d")
    dst = to.rearrange("p (k n) -> p k n", k=KT if half == 0 else HT)
    return sp.dma_start(dst, io[name][bass.ds(e, 1), :, :].rearrange(at, p=P))


def build_attend(nc, io, scratch, keep):
    with ExitStack() as ctx:
        n_ = Names(nc, ctx)
        ident = keep["ident"]
        q_st, k_st, wo = keep["q_st"], keep["k_st"], keep["wo"]
        v_st = [n_.sb(f"v_st{i}", [P, TT, GROUP, VW]) for i in range(GROUPS)]
        bo_gated = n_.sb("bo_gated", [P, DIM])
        low = n_.sb("low", [P, 2, GROUP * TT])
        low_rows = n_.sb("low_rows", [GROUP * TT, P], F32R)
        probs_T = [keep["w_raw"][:].rearrange("p (j q) -> p j q", j=GROUP)]
        probs_T += [n_.sb(f"probs_T{k}", [P, GROUP, SEQ]) for k in range(1, TT)]
        o_sb = n_.sb("o_sb", [P, SEQ])
        recip = n_.sb("recip", [P, TT, GROUP])
        attn = n_.sb("attn", [P, TT, DIM])
        attn_T = n_.sb("attn_T", [P, KT, SEQ])
        x_res = n_.sb("x_res", [P, TT, DIM])
        fits = n_.sb("fits", [P, 3, GROUP * TT])
        xn = n_.sb("xn_b", [P, TT, DIM])
        stats = n_.sb("stats_b", [P, TT, 6])
        moments = n_.sb("moments_b", [P, 10, TT])
        exponent, quarter, half, one = (n_.sb(name, [P, TT]) for name in ("exponent", "quarter", "half", "one"))
        gw_raw = n_.sb("gw_raw", [P, KT, EXPERTS])
        logits_T = n_.sb("logits_T", [P, SEQ])
        x_hi, x_lo, out_T, gw, pick, logits = (keep[name] for name in ("x_hi", "x_lo", "out_T", "gw", "pick", "logits"))
        fits_sum = n_.sb("fits_sum", [P, 1])
        ones = n_.sb("ones_b", [P, P])
        zero = n_.sb("zero_b", [P, 1])
        ps_s = [n_.ps(f"ps_s{i}", [P, SEQ]) for i in range(BANKS)]
        ps_t = [n_.ps(f"ps_t{i}", [P, SEQ]) for i in range(BANKS)]
        ps_o = n_.ps("ps_o", [P, SEQ])
        ps_m = n_.ps("ps_m", [P, SEQ])

        consts_set = n_.sem("b_consts_set")
        consts_loaded = n_.sem("b_consts_loaded")
        consts_ready = n_.sem("b_consts_ready")
        qk_loaded = [n_.sem(f"b_qk_loaded{i}") for i in range(GROUPS)]
        v_loaded = [n_.sem(f"b_v_loaded{i}") for i in range(GROUPS)]
        scores_in_psum = n_.sem("b_scores_in_psum")
        low_done = n_.sem("b_low_done")
        rows_sent = n_.sem("b_rows_sent")
        t_in_psum = n_.sem("b_t_in_psum")
        exp_done = n_.sem("b_exp_done")
        pv_done = n_.sem("b_pv_done")
        o_copied = n_.sem("b_o_copied")
        in_psum = {kind: n_.sem(f"b_{kind}_in_psum") for kind in UNITS_OF}
        taken = {kind: n_.sem(f"b_{kind}_taken") for kind in UNITS_OF}
        recip_done = n_.sem("b_recip_done")
        lows_checked = n_.sem("b_lows_checked")
        x_loaded = n_.sem("b_x_loaded")
        x_biased = n_.sem("b_x_biased")
        stats_done = n_.sem("b_stats_done")
        moment_done = n_.sem("b_moment_done")
        rstd_done = n_.sem("b_rstd_done")
        xn_ready = n_.sem("b_xn_ready")
        hi_done = n_.sem("b_hi_done")
        o_zeroed = n_.sem("b_o_zeroed")
        fits_summed = n_.sem("b_fits_summed")
        fits_in_psum = n_.sem("b_fits_in_psum")
        block = ctx.enter_context(nc.Block())

        def quad_no(b, g, k):
            return b * (GROUPS * TT) + g * TT + k

        def group_no(b, g):
            return b * GROUPS + g

        def free_after(b, at):
            back = next(n for n in range(1, PRODUCTS) if BANK_OF[at - n] == BANK_OF[at])
            return b * PRODUCTS + at - back + 1

        late_banks = [bank[:] for bank in [ps_m] + ps_s]
        assert len(late_banks) == LATE_BANKS

        def bank(kind, b, i):
            late = isinstance(b, int) and b == BATCH - 1 and (kind, i) in LATE
            return late_banks[LATE.index((kind, i)) % LATE_BANKS] if late else ps_m[:]

        def batches(eng, batch):
            batch(0)
            with eng.Fori(1, BATCH - 1) as b:
                batch(b)
            batch(BATCH - 1)
            batch(BATCH)

        @block.sync
        def _(sp):
            def load_group(b, g):
                done = group_no(b, g) - GROUPS
                wait(sp, t_in_psum, (done + 1) * TT * GROUP)
                if not (isinstance(b, int) and b == 0 and g < FIRST_GROUPS):
                    load_qk(sp, scratch, keep, b, g, qk_loaded[g])
                wait(sp, pv_done, (done + 1) * TT)
                src = scratch["v"][bass.ds(b, 1), :, :].rearrange("a p (t h w) -> (a p) t (h w)", t=TT, h=HEADS)
                sp.dma_start(v_st[g][:].rearrange("p t h w -> p t (h w)"),
                             src[:, :, g * GROUP * VW:(g + 1) * GROUP * VW]).then_inc(v_loaded[g], 16)

            def send_lows(b, g):
                sp.wait_ge(taken["low"], group_no(b, g) + 1)
                for half in range(2):
                    row = half * 64 + 64 - ROWS
                    sp.dma_start(q_st[g][row:row + 1].rearrange("a k (t q) -> a (k t) q", q=P).bitcast(F32),
                                 low_rows[half * 8:half * 8 + 8, :].bitcast(F32)).then_inc(rows_sent, 16)

            def batch(b):
                for g in range(GROUPS):
                    ahead = group_after(b, g, 3)
                    if exists(ahead[0]) and exists(b):
                        load_group(*ahead)
                    ahead = group_after(b, g, 1)
                    if exists(ahead[0]) and exists(b):
                        send_lows(*ahead)
                if exists(b):
                    wait(sp, in_psum["x2T"], b * KT)
                    wait(sp, xn_ready, b * 2)
                    sp.dma_start(x_res[:], io["x"][bass.ds(b * SEQ, SEQ), :].rearrange("(t p) d -> p t d", p=P)).then_inc(x_loaded, 16)

            for g in range(FIRST_GROUPS):
                sp.sem_inc(qk_loaded[g], 128)
            sp.dma_start(gw_raw[:], io["gwT"].rearrange("(k p) e -> p k e", p=P)).then_inc(consts_loaded, 16)
            load_group(0, 0)
            sp.dma_start(bo_gated[:], io["bo"].rearrange("(a n) -> a n", a=1).to_broadcast([P, DIM])).then_inc(consts_loaded, 16)
            for g in (1, 2):
                load_group(0, g)
            send_lows(0, 0)
            for p in range(2):
                sp.wait_ge(keep["stored"][p], STORES * BATCH // 2)
            batches(sp, batch)
            sp.wait_ge(pv_done, quad_no(BATCH - 1, GROUPS - 1, 0) + 1)
            load_weights(sp, io, keep["w_raw"][:], 0, 0).then_inc(keep["raw_loaded"][0], 16)

        @block.gpsimd
        def _(pool):
            pool.memset(fits[:], 0.0).then_inc(consts_set, 1)
            pool.memset(gw[:].bitcast(F32), 0.0).then_inc(consts_set, 1)
            pool.memset(ones[:], 1.0).then_inc(consts_set, 1)
            for tile, value in ((exponent, -0.5), (quarter, 0.25), (half, 0.5), (one, 1.0)):
                pool.memset(tile[:], value).then_inc(consts_set, 1)
            pool.memset(zero[:], 0.0).then_inc(consts_set, 1)
            pool.wait_ge(consts_set, 8)
            pool.tensor_tensor(pick[:], ident[:, 0:EXPERTS], ident[:, EXPERTS:2 * EXPERTS], ALU.add).then_inc(consts_ready, 1)
            pool.wait_ge(consts_loaded, 32)
            pool.tensor_tensor(gw[:, :, 0:EXPERTS], gw_raw[:], zero[:].rearrange("p (a b) -> p a b", a=1).to_broadcast([P, KT, EXPERTS]),
                               ALU.add).then_inc(consts_ready, 1)
            pool.wait_ge(consts_ready, 2)
            pool.tensor_tensor(gw[:, :, EXPERTS:2 * EXPERTS], gw_raw[:], gw[:, :, 0:EXPERTS].bitcast(F32),
                               ALU.subtract).then_inc(consts_ready, 1)
            pool.tensor_tensor(bo_gated[:], bo_gated[:], keep["tanh_g"][:, 0:1].to_broadcast([P, DIM]), ALU.mult).then_inc(consts_ready, 1)
            pool.wait_ge(consts_ready, 4)

            def reciprocal_root(b):
                mean, dev, diff, square, spread, var, root, root_2, scaled, rstd = (moments[:, i, :] for i in range(10))
                first = b * 9
                pool.wait_ge(stats_done, b * 2 + 2)
                wait(pool, xn_ready, b * 2)
                pool.tensor_tensor(diff, stats[:, :, 1], stats[:, :, 4], ALU.subtract)
                pool.tensor_tensor(dev, stats[:, :, 2], stats[:, :, 5], ALU.add)
                pool.tensor_tensor(root, stats[:, :, 1], stats[:, :, 4], ALU.add).then_inc(moment_done, 1)
                pool.wait_ge(moment_done, first + 1)
                pool.tensor_tensor(square, diff, diff, ALU.mult)
                pool.tensor_scalar(spread, dev, 1.0 / DIM, EPS, ALU.mult, ALU.add)
                pool.tensor_scalar(mean, root, 0.5, 0.0, ALU.mult, ALU.add).then_inc(moment_done, 1)
                pool.wait_ge(moment_done, first + 2)
                pool.tensor_tensor(diff, square, quarter[:], ALU.mult).then_inc(moment_done, 1)
                pool.wait_ge(moment_done, first + 3)
                pool.tensor_tensor(var, spread, diff, ALU.add).then_inc(moment_done, 1)
                pool.wait_ge(moment_done, first + 4)
                pool.tensor_tensor(root, var, exponent[:], ALU.pow).then_inc(moment_done, 1)
                pool.wait_ge(moment_done, first + 5)
                pool.tensor_tensor(root_2, root, root, ALU.mult).then_inc(moment_done, 1)
                pool.wait_ge(moment_done, first + 6)
                pool.tensor_tensor(scaled, root_2, var, ALU.mult).then_inc(moment_done, 1)
                pool.wait_ge(moment_done, first + 7)
                pool.tensor_tensor(root_2, one[:], scaled, ALU.subtract)
                pool.tensor_tensor(spread, root, half[:], ALU.mult).then_inc(moment_done, 1)
                pool.wait_ge(moment_done, first + 8)
                pool.tensor_tensor(dev, root_2, spread, ALU.mult).then_inc(moment_done, 1)
                pool.wait_ge(moment_done, first + 9)
                pool.tensor_tensor(rstd, root, dev, ALU.add).then_inc(rstd_done, 1)

            with pool.Fori(0, BATCH) as b:
                pool.wait_ge(x_loaded, b * 16 + 16)
                pool.tensor_tensor(x_res[:], x_res[:], bo_gated[:].rearrange("p (a d) -> p a d", a=1)
                                   .to_broadcast([P, TT, DIM]), ALU.add).then_inc(x_biased, 1)
                reciprocal_root(b)

        @block.tensor
        def _(pe):
            def scores(b, g, j, t):
                at = (g * GROUP + j) * TT + t
                if j == 0 and t == 0:
                    pe.wait_ge(qk_loaded[g], b * 128 + 128)
                wait(pe, low_done, free_after(b, at))
                pe.matmul(ps_s[BANK_OF[at]][:], q_st[g][:, j // 2, t * P:(t + 1) * P], k_st[g][:, j, :],
                          start=True, stop=True).then_inc(scores_in_psum, 1)

            def scores_T(b, g, k, j):
                at = (g * TT + k) * GROUP + j
                if k == 0 and j == 0:
                    pe.wait_ge(rows_sent, group_no(b, g) * 32 + 32)
                wait(pe, exp_done, free_after(b, at))
                pe.matmul(ps_t[BANK_OF[at]][:], k_st[g][:, j, k * P:(k + 1) * P], q_st[g][:, j // 2, :],
                          start=True, stop=True).then_inc(t_in_psum, 1)

            def probs_v(b, g, k):
                n = quad_no(b, g, k)
                if k == 0:
                    pe.wait_ge(v_loaded[g], b * 16 + 16)
                    wait(pe, o_copied, group_no(b, g))
                pe.wait_ge(exp_done, n * GROUP + GROUP)
                for j in range(GROUP):
                    mm = pe.matmul(ps_o[32 * j:32 * j + VW, :], v_st[g][:, k, j, :], probs_T[k][:, j, :],
                                   start=(k == 0), stop=(k == TT - 1))
                mm.then_inc(pv_done, 1)

            def turn_lows(ps_m, b, i):
                pe.wait_ge(low_done, group_no(b, i) * GROUP * TT + GROUP * TT)
                return pe.transpose(ps_m[0:GROUP * TT, 0:P], low[:, i % 2, :], ident[:])

            def turn_out(ps_m, b, i):
                pe.wait_ge(o_copied, group_no(b, i) + 1)
                for t in range(TT):
                    mm = pe.transpose(ps_m[:, t * P:(t + 1) * P], o_sb[:, t * P:(t + 1) * P], ident[:])
                return mm

            def turn_rows(ps_m, b, i):
                pe.wait_ge(taken["out"], group_no(b, GROUPS - 1) + 1)
                for t in range(TT):
                    mm = pe.transpose(ps_m[:, t * P:(t + 1) * P], attn[:, t, i * P:(i + 1) * P], ident[:])
                return mm

            def project_out(ps_m, b, i):
                pe.wait_ge(taken["rows"], b * KT + KT)
                for t in range(2):
                    t0 = (2 * i + t) * P
                    for k in range(KT):
                        mm = pe.matmul(ps_m[:, t * DIM:(t + 1) * DIM], attn_T[:, k, t0:t0 + P], wo[:, k, :],
                                       start=(k == 0), stop=(k == KT - 1))
                return mm

            def turn_x2(ps_m, b, i):
                pe.wait_ge(taken["y"], b * 2 + 2)
                for t in range(TT):
                    mm = pe.transpose(ps_m[:, t * P:(t + 1) * P], x_res[:, t, i * P:(i + 1) * P], ident[:])
                return mm

            def turn_xn(ps_m, b, i):
                pe.wait_ge(xn_ready, b * 2 + 2)
                for t in range(TT):
                    mm = pe.transpose(ps_m[:, t * P:(t + 1) * P], xn[:, t, i * P:(i + 1) * P], ident[:])
                return mm

            def gate_logits(ps_m, b, i):
                pe.wait_ge(taken["xnT"], b * KT + KT)
                parts = [(x, k) for k in range(KT) for x in (x_hi, x_lo)]
                for n, (x, k) in enumerate(parts):
                    mm = pe.matmul(ps_m[:], gw[:, k, :], x[:, k, bass.ds(b * SEQ, SEQ)], start=(n == 0), stop=(n == len(parts) - 1))
                return mm

            def pick_logits(ps_m, b, i):
                pe.wait_ge(taken["logits"], b + 1)
                for t in range(TT):
                    mm = pe.matmul(ps_m[:, t * EXPERTS:(t + 1) * EXPERTS], logits_T[:, t * P:(t + 1) * P], pick[:],
                                   start=True, stop=True)
                return mm

            write = {"low": turn_lows, "out": turn_out, "rows": turn_rows, "y": project_out,
                     "x2T": turn_x2, "xnT": turn_xn, "logits": gate_logits, "pick": pick_logits}

            def shared(b, unit):
                if not unit or not exists(b + unit[1]):
                    return
                kind, off, i = unit
                before = unit_before(b, unit)
                if before:
                    pe.wait_ge(taken[before[0]], before[1] + 1)
                write[kind](bank(kind, b + off, i), b + off, i).then_inc(in_psum[kind], 1)

            def batch(b):
                for g in range(GROUPS):
                    ahead = group_after(b, g, 2)
                    for k in range(TT):
                        back = (b, g, k - 1) if k else (*group_after(b, g, -1), TT - 1)
                        more = exists(ahead[0]) and exists(b)
                        if exists(b):
                            scores_T(b, g, k, 0)
                        if more:
                            scores(*ahead, k, 0)
                        if exists(b):
                            scores_T(b, g, k, 1)
                        if more:
                            scores(*ahead, k, 1)
                        if exists(back[0]):
                            probs_v(*back)
                        shared(b, SHARED.get((g, k, 0)))
                        if exists(b):
                            scores_T(b, g, k, 2)
                        if more:
                            scores(*ahead, k, 2)
                        if exists(b):
                            scores_T(b, g, k, 3)
                        if more:
                            scores(*ahead, k, 3)
                        shared(b, SHARED.get((g, k, 1)))

            for g in range(2):
                for j in range(GROUP):
                    for t in range(TT):
                        scores(0, g, j, t)
                if g == 0:
                    turn_lows(ps_m, 0, 0).then_inc(in_psum["low"], 1)
            pe.wait_ge(o_zeroed, 1)
            pe.wait_ge(consts_ready, 3)
            batches(pe, batch)
            pe.wait_ge(fits_summed, 1)
            pe.matmul(ps_m[:, 0:1], ones[:], fits_sum[:], start=True, stop=True).then_inc(fits_in_psum, 1)

        @block.vector
        def _(dve):
            dve.memset(ps_o[:], 0.0).then_inc(o_zeroed, 1)
            dve.wait_ge(consts_set, 8)

            def lows(b, g, j, u):
                if j == 0 and u == 0:
                    wait(dve, in_psum["low"], group_no(b, g) - 1)
                    wait(dve, lows_checked, group_no(b, g) - 1)
                for t in (2 * u, 2 * u + 1):
                    at = (g * GROUP + j) * TT + t
                    dve.wait_ge(scores_in_psum, b * PRODUCTS + at + 1)
                    column = (j % 2) * 2 * TT + (j // 2) * TT + t
                    dve.tensor_reduce(low[:, g % 2, column:column + 1], ps_s[BANK_OF[at]][:], AX_X, ALU.min).then_inc(low_done, 1)

            def check_lows(b, g):
                dve.wait_ge(low_done, group_no(b, g) * GROUP * TT + GROUP * TT)
                wait(dve, lows_checked, group_no(b, g))
                dve.scalar_tensor_tensor(out=fits[:, 0, :], in0=low[:, g % 2, :], scalar=FITS, in1=fits[:, 0, :],
                                         op0=ALU.is_le, op1=ALU.add)
                dve.scalar_tensor_tensor(out=fits[:, 1, :], in0=low[:, g % 2, :], scalar=-FITS, in1=fits[:, 1, :],
                                         op0=ALU.is_ge, op1=ALU.add).then_inc(lows_checked, 1)

            def normalise(b, i):
                n = group_no(b, i)
                dve.wait_ge(in_psum["out"], n + 1)
                if i == 0:
                    wait(dve, in_psum["rows"], b * KT)
                wait(dve, taken["out"], n)
                heads = bank("out", b, i)[:].rearrange("p (t j w) -> p t j w", t=TT, j=GROUP)
                dve.reciprocal(recip[:], heads[:, :, :, HDIM]).then_inc(recip_done, 1)
                count = fits[:, 2, :].rearrange("p (t j) -> p t j", t=TT)
                dve.scalar_tensor_tensor(out=count, in0=heads[:, :, :, HDIM], scalar=SUM_LEAST, in1=count,
                                         op0=ALU.is_ge, op1=ALU.add)
                dve.wait_ge(recip_done, n + 1)
                dve.tensor_tensor(attn[:, :, i * GROUP * HDIM:(i + 1) * GROUP * HDIM].rearrange("p t (j d) -> p t j d", j=GROUP),
                                  heads[:, :, :, 0:HDIM],
                                  recip[:].rearrange("p t (j a) -> p t j a", a=1).to_broadcast([P, TT, GROUP, HDIM]),
                                  ALU.mult).then_inc(taken["out"], 1)

            def add_residual(b, i):
                if i == 0:
                    dve.wait_ge(x_biased, b + 1)
                dve.wait_ge(in_psum["y"], b * 2 + i + 1)
                part = x_res[:, 2 * i:2 * i + 2, :]
                dve.scalar_tensor_tensor(out=part, in0=bank("y", b, i)[:].rearrange("p (t d) -> p t d", t=2),
                                         scalar=keep["tanh_g"][:, 0:1], in1=part,
                                         op0=ALU.mult, op1=ALU.add).then_inc(taken["y"], 1)

            def statistics(b, i):
                if i == 0:
                    wait(dve, rstd_done, b)
                dve.wait_ge(taken["y"], b * 2 + i + 1)
                for t in (2 * i, 2 * i + 1):
                    ins = dve.bn_stats(stats[:, t, :], x_res[:, t, :])
                ins.then_inc(stats_done, 1)

            def layer_norm(b, i):
                if i == 0:
                    dve.wait_ge(rstd_done, b + 1)
                    wait(dve, in_psum["xnT"], b * KT)
                for t in (2 * i, 2 * i + 1):
                    ins = dve.tensor_scalar(xn[:, t, :], x_res[:, t, :], moments[:, 0, t:t + 1], moments[:, 9, t:t + 1],
                                            ALU.subtract, ALU.mult)
                ins.then_inc(xn_ready, 1)

            def split(b, i):
                n = b * KT + i
                at = bass.ds(b * SEQ, SEQ)
                dve.wait_ge(hi_done, n + 1)
                dve.tensor_tensor(x_lo[:, i, at], bank("xnT", b, i)[:], x_hi[:, i, at].bitcast(F32), ALU.subtract).then_inc(taken["xnT"], 1)

            def keep_logits(b, i):
                dve.wait_ge(in_psum["pick"], b + 1)
                dve.tensor_scalar(logits[:, :, bass.ds(b * TT, TT)], bank("pick", b, i)[:, 0:TT * EXPERTS].rearrange("p (t e) -> p e t", t=TT),
                                  1.0, None, ALU.mult).then_inc(taken["pick"], 1)

            take = {"out": normalise, "y": add_residual, "xnT": split, "pick": keep_logits}

            def take_unit(b, at):
                kind, off, i = SHARED.get(at, (None, 0, 0))
                if kind in take and exists(b + off):
                    take[kind](b + off, i)

            def batch(b):
                for g in range(GROUPS):
                    ahead = group_after(b, g, 2)
                    more = exists(ahead[0]) and exists(b)
                    for k in range(TT):
                        if more:
                            lows(*ahead, k, 0)
                        if (g, k) != (0, 0):
                            take_unit(b, STEPS[STEPS.index((g, k)) - 1] + (1,))
                        kind, i = NORM_STEPS.get((g, k), (None, 0))
                        if kind and exists(b - 1):
                            {"statistics": statistics, "normalised": layer_norm}[kind](b - 1, i)
                        if k == 0:
                            behind = group_after(b, g, 1)
                            if exists(behind[0]) and exists(b):
                                check_lows(*behind)
                        take_unit(b, (g, k, 0))
                        if more:
                            lows(*ahead, k, 1)

            for g in range(2):
                for j in range(GROUP):
                    for u in range(2):
                        lows(0, g, j, u)
                if g == 0:
                    check_lows(0, 0)
            batches(dve, batch)
            dve.wait_ge(lows_checked, BATCH * GROUPS)
            dve.wait_ge(taken["out"], BATCH * GROUPS)
            dve.tensor_reduce(fits_sum[:], fits[:].rearrange("p a n -> p (a n)"), AX_X, ALU.add).then_inc(fits_summed, 1)
            dve.wait_ge(fits_in_psum, 1)
            dve.tensor_scalar(keep["clip_flag"][:], ps_m[:, 0:1], 3 * HEADS * TOKENS - 0.5, None, ALU.is_lt)

        @block.scalar
        def _(act):
            def exps(b, g, k, heads):
                n = quad_no(b, g, k)
                if 0 in heads:
                    wait(act, pv_done, n - TT + 1)
                for j in heads:
                    act.wait_ge(t_in_psum, n * GROUP + j + 1)
                    act.activation(probs_T[k][:, j, :], ps_t[BANK_OF[(g * TT + k) * GROUP + j]][:], ACT.Exp, scale=-1.0).then_inc(exp_done, 1)

            def copy_out(b, g):
                act.wait_ge(pv_done, quad_no(b, g, TT - 1) + 1)
                wait(act, in_psum["out"], group_no(b, g))
                act.activation(o_sb[:], ps_o[:], ACT.Copy).then_inc(o_copied, 1)

            def take_lows(b, i):
                n = group_no(b, i)
                act.wait_ge(in_psum["low"], n + 1)
                wait(act, rows_sent, n * 32)
                act.activation(low_rows[:], ps_m[0:GROUP * TT, 0:P], ACT.Copy, scale=-1.0).then_inc(taken["low"], 1)

            def take_rows(b, i):
                act.wait_ge(in_psum["rows"], b * KT + i + 1)
                wait(act, in_psum["y"], b * 2)
                act.activation(attn_T[:, i, :], bank("rows", b, i)[:], ACT.Copy).then_inc(taken["rows"], 1)

            def take_x2(b, i):
                if isinstance(b, int):
                    act.wait_ge(in_psum["x2T"], b * KT + i + 1)
                act.activation(out_T[:, i, bass.ds(b * SEQ, SEQ)], bank("x2T", b, i)[:], ACT.Copy).then_inc(taken["x2T"], 1)

            def take_hi(b, i):
                if isinstance(b, int):
                    act.wait_ge(in_psum["xnT"], b * KT + i + 1)
                act.activation(x_hi[:, i, bass.ds(b * SEQ, SEQ)], bank("xnT", b, i)[:], ACT.Copy).then_inc(hi_done, 1)

            def take_logits(b, i):
                act.wait_ge(in_psum["logits"], b + 1)
                wait(act, in_psum["pick"], b)
                act.activation(logits_T[:], bank("logits", b, i)[:], ACT.Copy).then_inc(taken["logits"], 1)

            take = {"low": take_lows, "rows": take_rows, "x2T": take_x2, "xnT": take_hi, "logits": take_logits}

            def take_unit(b, at):
                kind, off, i = SHARED.get(at, (None, 0, 0))
                if kind in take and exists(b + off):
                    take[kind](b + off, i)

            def batch(b):
                for g in range(GROUPS):
                    for k in range(TT):
                        if exists(b):
                            exps(b, g, k, (0, 1))
                        if (g, k) != (0, 0):
                            take_unit(b, STEPS[STEPS.index((g, k)) - 1] + (1,))
                        back = group_after(b, g, -1)
                        if k == 0 and exists(back[0]):
                            copy_out(*back)
                        if exists(b):
                            exps(b, g, k, (2, 3))

            take_lows(0, 0)
            batches(act, batch)


AHEAD = 2
SLOTS = 4
WIDE = 32


def transpose_units():
    units = []
    for n in range(HEADS):
        units += [("T", n, k) for k in range(TT)]
        if n == 1:
            units.append(("R", GROUPS - 1))
        if n == 4:
            units += [("Y", 0), ("Y", 1)]
        if n >= 5 and n % GROUP == 1:
            units.append(("R", (n - 5) // GROUP))
    return {u: i for i, u in enumerate(units)}


UNITS = transpose_units()
PER_BATCH = len(UNITS)
CARRIED = 3
assert PER_BATCH % 2 == 0


class Unit:

    def __init__(self, b, unit, epilogue=False):
        if epilogue:
            at, rounds = PER_BATCH * BATCH - CARRIED + {"R": 0, "Y": 1 + unit[1]}[unit[0]], None
            self.bank, self.before, self.order = at % 2, at // 2, at
            return
        carried = unit in (("R", GROUPS - 1), ("Y", 0), ("Y", 1))
        at = UNITS[unit] - CARRIED
        if isinstance(b, int) and b == 0:
            assert not carried
            at += sum(UNITS[c] > UNITS[unit] for c in (("R", GROUPS - 1), ("Y", 0), ("Y", 1)))
        self.bank = at % 2
        self.before = b * (PER_BATCH // 2) + at // 2
        self.order = b * PER_BATCH + at


def build_attend_clipped(nc, io, scratch, keep):
    with ExitStack() as ctx:
        n_ = Names(nc, ctx)
        q_size = GROUP // 2 * SEQ
        q_st = [flat(keep["x_hi"])[:, i * q_size:(i + 1) * q_size].rearrange("p (h k) -> p h k", k=SEQ) for i in range(2)]
        k_st = [flat(keep["x_hi"])[:, (i + 1) * 2 * q_size:(i + 2) * 2 * q_size].rearrange("p (h k) -> p h k", k=SEQ) for i in range(2)]
        v_st = [n_.sb(f"g_v_st{i}", [P, TT, GROUP, WIDE]) for i in range(2)]
        wo = n_.sb("g_wo", [P, GROUPS, DIM])
        probs = [flat(keep["out_T"])[:, i * TT * SEQ:(i + 1) * TT * SEQ].rearrange("p (t k) -> p t k", t=TT) for i in range(SLOTS)]
        low = n_.sb("g_low", [P, SLOTS, TT])
        sums = n_.sb("g_sums", [P, 2, GROUP, TT])
        recip = n_.sb("g_recip", [P, 2, GROUP, TT])
        probs_T = [n_.sb(f"g_probs_T{i}", [P, GROUP, TT, SEQ]) for i in range(2)]
        recip_wide = n_.sb("g_recip_wide", [P, 2, TT, GROUP, WIDE])
        recip_rows = n_.sb("g_recip_rows", [P, SEQ])
        heads_out = n_.sb("g_heads_out", [P, GROUPS, SEQ])
        x_res = n_.sb("g_x_res", [P, TT, DIM])
        numbers = n_.sb("g_numbers", [P, 2, SEQ])
        all_numbers = n_.sb("g_all_numbers", [P, 2])
        ones = n_.sb("g_ones", [P, P])
        ps_s = [n_.ps(f"g_ps_s{i}", [P, 2, SEQ]) for i in range(2)]
        ps_t = [n_.ps(f"g_ps_t{i}", [P, SEQ]) for i in range(2)]
        ps_o = [n_.ps(f"g_ps_o{i}", [P, SEQ]) for i in range(2)]

        zeroed = n_.sem("g_zeroed")
        consts_set = n_.sem("g_consts_set")
        wo_loaded = n_.sem("g_wo_loaded")
        qk_loaded = [n_.sem(f"g_qk_loaded{i}") for i in range(2)]
        v_loaded = [n_.sem(f"g_v_loaded{i}") for i in range(2)]
        scores_in_psum = n_.sem("g_scores_in_psum")
        checked = n_.sem("g_checked")
        numbers_in_psum = n_.sem("g_numbers_in_psum")
        clipped = n_.sem("g_clipped")
        low_ready = n_.sem("g_low_ready")
        probs_ready = n_.sem("g_probs_ready")
        unit_in_psum = n_.sem("g_unit_in_psum")
        unit_taken = [n_.sem(f"g_unit_taken{i}") for i in range(2)]
        pv_done = n_.sem("g_pv_done")
        recip_ready = n_.sem("g_recip_ready")
        recip_spread = n_.sem("g_recip_spread")
        heads_ready = n_.sem("g_heads_ready")
        x_loaded = n_.sem("g_x_loaded")
        x2_stored = n_.sem("g_x2_stored")
        block = ctx.enter_context(nc.Block())
        QK_DMAS = 16

        @block.sync
        def _(sp):
            clip = sp.value_load(keep["clip_flag"][0:1, 0:1], min_val=0, max_val=1)
            with sp.If(clip > 0):
                sp.wait_ge(zeroed, 5)
                for j in range(GROUP):
                    sp.dma_start(wo[32 * j:32 * j + HDIM, :, :],
                                 io["Wo"].rearrange("(g h d) n -> h d g n", g=GROUPS, h=GROUP)[j]).then_inc(wo_loaded, 16)
                sp.dma_start(wo[HDIM:HDIM + 1, 0, :], io["bo"].rearrange("(a n) -> a n", a=1)).then_inc(wo_loaded, 16)

                def load_group(b, g):
                    s = g % 2
                    gi = b * GROUPS + g
                    wait(sp, scores_in_psum, gi * 8 - 8)
                    for name, dst, parts in (("q", q_st[s], (0, 1, 0, 1)), ("k", k_st[s], (0, 0, 1, 1))):
                        for half in range(2):
                            for c, part in enumerate(parts):
                                row = 1 + HDIM * part
                                src = scratch[name][bass.ds(b, 1)].rearrange("a (g k h r) t -> (a g) h r k t", g=GROUPS, k=2, h=2)
                                src = src[g, half, row:row + HDIM]
                                at = half * 64 + c * HDIM
                                to = dst[at:at + HDIM, :, :] if name == "q" else dst[at:at + HDIM, half:GROUP:2, :]
                                sp.dma_start(to.bitcast(F32), src).then_inc(qk_loaded[s], 16)
                    wait(sp, pv_done, gi - 1)
                    src = scratch["v"][bass.ds(b, 1), :, :].rearrange("a p (t h w) -> (a p) t h w", t=TT, h=HEADS)
                    for t in range(TT):
                        sp.dma_start(v_st[s][:, t, :, 0:VW], src[:, t, g * GROUP:(g + 1) * GROUP]).then_inc(v_loaded[s], 16)

                def load_residual(b):
                    wait(sp, x2_stored, b * 16)
                    sp.dma_start(x_res[:], io["x"][bass.ds(b * SEQ, SEQ), :].rearrange("(t p) d -> p t d", p=P)).then_inc(x_loaded, 16)

                def store_x2(b, units):
                    for u in units:
                        sp.wait_ge(unit_taken[u.bank], u.before + 1)
                    sp.dma_start(scratch["x2"][bass.ds(b * SEQ, SEQ), :].rearrange("(t p) d -> p t d", p=P), x_res[:]).then_inc(x2_stored, 16)

                for g in range(GROUPS):
                    load_group(0, g)
                load_residual(0)
                with sp.Fori(1, BATCH) as b:
                    for g in range(GROUPS):
                        load_group(b, g)
                    store_x2(b - 1, [Unit(b, ("Y", i)) for i in range(2)])
                    load_residual(b)
                store_x2(BATCH - 1, [Unit(0, ("Y", i), epilogue=True) for i in range(2)])
                sp.wait_ge(x2_stored, 16 * BATCH)

        @block.gpsimd
        def _(pool):
            clip = pool.value_load(keep["clip_flag"][0:1, 0:1], min_val=0, max_val=1)
            with pool.If(clip > 0):
                pool.memset(wo[:], 0.0).then_inc(zeroed, 1)
                pool.memset(ones[:], 1.0).then_inc(consts_set, 1)
                pool.memset(all_numbers[:], 1.0).then_inc(consts_set, 1)
                for s in range(2):
                    pool.memset(k_st[s][:].bitcast(F32), 0.0).then_inc(zeroed, 1)
                    pool.memset(v_st[s][:], 0.0).then_inc(zeroed, 1)

        @block.tensor
        def _(pe):
            clip = pe.value_load(keep["clip_flag"][0:1, 0:1], min_val=0, max_val=1)
            with pe.If(clip > 0):
                def scores(b, m):
                    if m >= HEADS:
                        b, m = b + 1, m - HEADS
                    g, j = m // GROUP, m % GROUP
                    s = g % 2
                    if j == 0:
                        pe.wait_ge(qk_loaded[s], b * (2 * 16 * QK_DMAS) + (g // 2 + 1) * 16 * QK_DMAS)
                    for u in range(2):
                        wait(pe, clipped, b * (2 * HEADS) + 2 * m - 1 + u)
                        for t in range(2):
                            q0 = (2 * u + t) * P
                            mm = pe.matmul(ps_s[u][:, t, :], q_st[s][:, j // 2, q0:q0 + P], k_st[s][:, j, :],
                                           start=True, stop=True)
                        mm.then_inc(scores_in_psum, 1)

                def transposes(b, m):
                    pe.wait_ge(probs_ready, b * HEADS + m + 1)
                    for k in range(TT):
                        u = Unit(b, ("T", m, k))
                        wait(pe, unit_taken[u.bank], u.before)
                        for t in range(TT):
                            mm = pe.transpose(ps_t[u.bank][:, t * P:(t + 1) * P], probs[m % SLOTS][:, t, k * P:(k + 1) * P],
                                              keep["ident"][:])
                        mm.then_inc(unit_in_psum, 1)

                def probs_v(b, g):
                    s = g % 2
                    gi = b * GROUPS + g
                    for k in (TT - 2, TT - 1):
                        u = Unit(b, ("T", g * GROUP + GROUP - 1, k))
                        pe.wait_ge(unit_taken[u.bank], u.before + 1)
                    pe.wait_ge(v_loaded[s], (b * 32 + (g // 2 + 1) * 16) * TT)
                    wait(pe, heads_ready, gi - 1)
                    for k in range(TT):
                        for j in range(GROUP):
                            mm = pe.matmul(ps_o[s][32 * j:32 * j + 32, :], v_st[s][:, k, j, :], probs_T[s][:, j, k, :],
                                           start=(k == 0), stop=(k == TT - 1))
                    mm.then_inc(pv_done, 1)

                def reciprocals(b, g, u):
                    pe.wait_ge(recip_spread, b * GROUPS + g + 1)
                    wait(pe, unit_taken[u.bank], u.before)
                    for t in range(TT):
                        mm = pe.matmul(ps_t[u.bank][:, t * P:(t + 1) * P],
                                       recip_wide[:, g % 2, t].rearrange("p j w -> p (j w)"), keep["ident"][:],
                                       start=True, stop=True)
                    mm.then_inc(unit_in_psum, 1)

                def project_out(b, units):
                    pe.wait_ge(heads_ready, b * GROUPS + GROUPS)
                    for i, u in enumerate(units):
                        wait(pe, unit_taken[u.bank], u.before)
                        for t in range(2):
                            t0 = (2 * i + t) * P
                            for g in range(GROUPS):
                                mm = pe.matmul(ps_t[u.bank][:, t * DIM:(t + 1) * DIM], heads_out[:, g, t0:t0 + P], wo[:, g, :],
                                               start=(g == 0), stop=(g == GROUPS - 1))
                        mm.then_inc(unit_in_psum, 1)

                def batch(b, first, last):
                    for m in range(HEADS):
                        if m + AHEAD < HEADS or not last:
                            scores(b, m + AHEAD)
                        if m == 1 and not first:
                            probs_v(b - 1, GROUPS - 1)
                        if m >= 5 and m % GROUP == 1:
                            probs_v(b, (m - 5) // GROUP)
                        transposes(b, m)
                        if m == 1 and not first:
                            reciprocals(b - 1, GROUPS - 1, Unit(b, ("R", GROUPS - 1)))
                        if m == 4 and not first:
                            project_out(b - 1, [Unit(b, ("Y", i)) for i in range(2)])
                        if m >= 5 and m % GROUP == 1:
                            g = (m - 5) // GROUP
                            reciprocals(b, g, Unit(b, ("R", g)))

                pe.wait_ge(zeroed, 5)
                for m in range(AHEAD):
                    scores(0, m)
                pe.wait_ge(wo_loaded, 16 * (GROUP + 1))
                batch(0, True, False)
                with pe.Fori(1, BATCH - 1) as b:
                    batch(b, False, False)
                batch(BATCH - 1, False, True)
                end = BATCH - 1
                probs_v(end, GROUPS - 1)
                reciprocals(end, GROUPS - 1, Unit(0, ("R", 0), epilogue=True))
                project_out(end, [Unit(0, ("Y", i), epilogue=True) for i in range(2)])
                pe.wait_ge(consts_set, 2)
                pe.wait_ge(checked, 4 * 2 * HEADS * BATCH)
                pe.matmul(ps_o[0][:, 0:1], ones[:], all_numbers[:, 1:2], start=True, stop=True).then_inc(numbers_in_psum, 1)

        @block.vector
        def _(dve):
            clip = dve.value_load(keep["clip_flag"][0:1, 0:1], min_val=0, max_val=1)
            with dve.If(clip > 0):
                def check_numbers(n, scores):
                    wait(dve, checked, n * 4)
                    dve.tensor_copy(numbers[:], scores).then_inc(checked, 1)
                    dve.wait_ge(checked, n * 4 + 1)
                    dve.tensor_tensor(numbers[:], numbers[:], scores, ALU.is_equal).then_inc(checked, 1)
                    dve.wait_ge(checked, n * 4 + 2)
                    dve.tensor_reduce(all_numbers[:, 0:1], numbers[:].rearrange("p t k -> p (t k)"), AX_X, ALU.min).then_inc(checked, 1)
                    dve.wait_ge(checked, n * 4 + 3)
                    dve.tensor_tensor(all_numbers[:, 1:2], all_numbers[:, 1:2], all_numbers[:, 0:1], ALU.min).then_inc(checked, 1)

                def clip_and_low(b, m):
                    head2 = b * (2 * HEADS) + 2 * m
                    if m >= SLOTS:
                        dve.wait_ge(unit_in_psum, Unit(b, ("T", m - SLOTS, TT - 1)).order + 1)
                    elif not (isinstance(b, int) and b == 0):
                        dve.wait_ge(unit_in_psum, Unit(b - 1, ("T", m - SLOTS + HEADS, TT - 1)).order + 1)
                    for u in range(2):
                        dve.wait_ge(scores_in_psum, head2 + u + 1)
                        check_numbers(head2 + u, ps_s[u][:])
                        dve.tensor_scalar(probs[m % SLOTS][:, 2 * u:2 * u + 2, :], ps_s[u][:], CLAMP, -CLAMP,
                                          ALU.min, ALU.max).then_inc(clipped, 1)
                    for u in range(2):
                        dve.wait_ge(clipped, head2 + u + 1)
                        dve.tensor_reduce(low[:, m % SLOTS, 2 * u:2 * u + 2], probs[m % SLOTS][:, 2 * u:2 * u + 2, :],
                                          AX_X, ALU.min).then_inc(low_ready, 1)

                def invert(b, g):
                    gi = b * GROUPS + g
                    dve.wait_ge(probs_ready, gi * GROUP + GROUP)
                    dve.reciprocal(recip[:, g % 2], sums[:, g % 2]).then_inc(recip_ready, 1)
                    dve.wait_ge(recip_ready, gi + 1)
                    dve.tensor_copy(recip_wide[:, g % 2], recip[:, g % 2].rearrange("p j (t a) -> p t j a", a=1)
                                    .to_broadcast([P, TT, GROUP, WIDE])).then_inc(recip_spread, 1)

                def normalise(b, g, u):
                    dve.wait_ge(unit_taken[u.bank], u.before + 1)
                    dve.wait_ge(pv_done, b * GROUPS + g + 1)
                    dve.tensor_tensor(heads_out[:, g, :], ps_o[g % 2][:], recip_rows[:], ALU.mult).then_inc(heads_ready, 1)

                def add_residual(b, units):
                    dve.wait_ge(x_loaded, b * 16 + 16)
                    for i, u in enumerate(units):
                        dve.wait_ge(unit_in_psum, u.order + 1)
                        part = x_res[:, 2 * i:2 * i + 2, :]
                        dve.scalar_tensor_tensor(out=part, in0=ps_t[u.bank][:].rearrange("p (t d) -> p t d", t=2),
                                                 scalar=keep["tanh_g"][:, 0:1], in1=part,
                                                 op0=ALU.mult, op1=ALU.add).then_inc(unit_taken[u.bank], 1)

                def batch(b, first):
                    for m in range(HEADS):
                        clip_and_low(b, m)
                        if m == 1 and not first:
                            invert(b - 1, GROUPS - 1)
                        if m >= 5 and m % GROUP == 1:
                            invert(b, (m - 5) // GROUP)
                        if m == 3 and not first:
                            normalise(b - 1, GROUPS - 1, Unit(b, ("R", GROUPS - 1)))
                        if m >= 7 and m % GROUP == 3:
                            g = (m - 7) // GROUP
                            normalise(b, g, Unit(b, ("R", g)))
                        if m == 5 and not first:
                            add_residual(b - 1, [Unit(b, ("Y", i)) for i in range(2)])

                dve.wait_ge(consts_set, 2)
                batch(0, True)
                with dve.Fori(1, BATCH) as b:
                    batch(b, False)
                end = BATCH - 1
                invert(end, GROUPS - 1)
                normalise(end, GROUPS - 1, Unit(0, ("R", 0), epilogue=True))
                add_residual(end, [Unit(0, ("Y", i), epilogue=True) for i in range(2)])
                dve.wait_ge(numbers_in_psum, 1)
                dve.tensor_scalar(keep["nan_flag"][:], ps_o[0][:, 0:1], P - 0.5, None, ALU.is_lt)

        @block.scalar
        def _(act):
            clip = act.value_load(keep["clip_flag"][0:1, 0:1], min_val=0, max_val=1)
            with act.If(clip > 0):
                def exps(b, m):
                    g, j = m // GROUP, m % GROUP
                    if j == 0:
                        wait(act, recip_ready, b * GROUPS + g - 1)
                    for u in range(2):
                        act.wait_ge(low_ready, b * (2 * HEADS) + 2 * m + u + 1)
                        for t in (2 * u, 2 * u + 1):
                            tile = probs[m % SLOTS][:, t, :]
                            ins = act.activation(tile, tile, ACT.Exp, bias=low[:, m % SLOTS, t:t + 1], scale=-1.0,
                                                 accum_out=sums[:, g % 2, j, t:t + 1])
                    ins.then_inc(probs_ready, 1)

                def evacuate(b, m):
                    g, j = m // GROUP, m % GROUP
                    if j == 0:
                        wait(act, pv_done, b * GROUPS + g - 1)
                    for k in range(TT):
                        u = Unit(b, ("T", m, k))
                        act.wait_ge(unit_in_psum, u.order + 1)
                        act.activation(probs_T[g % 2][:, j, k, :], ps_t[u.bank][:], ACT.Copy).then_inc(unit_taken[u.bank], 1)

                def take_reciprocals(b, g, u):
                    act.wait_ge(unit_in_psum, u.order + 1)
                    wait(act, heads_ready, b * GROUPS + g)
                    act.activation(recip_rows[:], ps_t[u.bank][:], ACT.Copy).then_inc(unit_taken[u.bank], 1)

                def batch(b, first):
                    for m in range(HEADS):
                        exps(b, m)
                        if m == 0 and not first:
                            evacuate(b - 1, HEADS - 1)
                        if m > 0:
                            evacuate(b, m - 1)
                        if m == 2 and not first:
                            take_reciprocals(b - 1, GROUPS - 1, Unit(b, ("R", GROUPS - 1)))
                        if m >= 6 and m % GROUP == 2:
                            g = (m - 6) // GROUP
                            take_reciprocals(b, g, Unit(b, ("R", g)))

                batch(0, True)
                with act.Fori(1, BATCH) as b:
                    batch(b, False)
                end = BATCH - 1
                evacuate(end, HEADS - 1)
                take_reciprocals(end, GROUPS - 1, Unit(0, ("R", 0), epilogue=True))


def build_attend_uniform(nc, io, scratch, keep):
    with ExitStack() as ctx:
        n = Names(nc, ctx)
        v = n.sb("u_v", [P, TT, DIM])
        wo = n.sb("u_wo", [P, KT, DIM])
        bo = n.sb("u_bo", [P, DIM])
        share = n.sb("u_share", [P, P])
        mean_T = n.sb("u_mean_T", [P, KT, P])
        y = n.sb("u_y", [P, DIM])
        x_res = n.sb("u_x_res", [P, TT, DIM])
        ps_mean = n.ps("u_ps_mean", [P, KT, P])
        ps_y = n.ps("u_ps_y", [P, DIM])
        consts_ready = n.sem("u_consts_ready")
        batch_loaded = n.sem("u_batch_loaded")
        mean_in_psum = n.sem("u_mean_in_psum")
        mean_ready = n.sem("u_mean_ready")
        y_in_psum = n.sem("u_y_in_psum")
        y_ready = n.sem("u_y_ready")
        added = n.sem("u_added")
        x2_stored = n.sem("u_x2_stored")
        block = ctx.enter_context(nc.Block())

        @block.sync
        def _(sp):
            uniform = sp.value_load(keep["nan_flag"][0:1, 0:1], min_val=0, max_val=1)
            with sp.If(uniform > 0):
                sp.dma_start(wo[:], io["Wo"].rearrange("(k p) n -> p k n", p=P)).then_inc(consts_ready, 16)
                sp.dma_start(bo[:], io["bo"].rearrange("(a n) -> a n", a=1).to_broadcast([P, DIM])).then_inc(consts_ready, 16)

                def batch(b):
                    wait(sp, x2_stored, b * 16)
                    src = scratch["v"][bass.ds(b, 1), :, :].rearrange("a p (n w) -> (a p) n w", w=VW)
                    sp.dma_start(v[:].rearrange("p t (h d) -> p (t h) d", d=HDIM), src[:, :, 0:HDIM]).then_inc(batch_loaded, 16)
                    sp.dma_start(x_res[:], io["x"][bass.ds(b * SEQ, SEQ), :].rearrange("(t p) d -> p t d", p=P)).then_inc(batch_loaded, 16)
                    sp.wait_ge(added, b + 1)
                    sp.dma_start(scratch["x2"][bass.ds(b * SEQ, SEQ), :].rearrange("(t p) d -> p t d", p=P), x_res[:]).then_inc(x2_stored, 16)

                batch(0)
                with sp.Fori(1, BATCH) as b:
                    batch(b)
                sp.wait_ge(x2_stored, 16 * BATCH)

        @block.gpsimd
        def _(pool):
            uniform = pool.value_load(keep["nan_flag"][0:1, 0:1], min_val=0, max_val=1)
            with pool.If(uniform > 0):
                pool.memset(share[:], 1.0 / SEQ).then_inc(consts_ready, 1)

        @block.tensor
        def _(pe):
            uniform = pe.value_load(keep["nan_flag"][0:1, 0:1], min_val=0, max_val=1)
            with pe.If(uniform > 0):
                pe.wait_ge(consts_ready, 33)
                with pe.Fori(0, BATCH) as b:
                    pe.wait_ge(batch_loaded, b * 32 + 32)
                    for k in range(KT):
                        for t in range(TT):
                            mm = pe.matmul(ps_mean[:, k, :], v[:, t, k * P:(k + 1) * P], share[:],
                                           start=(t == 0), stop=(t == TT - 1))
                    mm.then_inc(mean_in_psum, 1)
                    pe.wait_ge(mean_ready, b + 1)
                    for k in range(KT):
                        mm = pe.matmul(ps_y[:], mean_T[:, k, :], wo[:, k, :], start=(k == 0), stop=(k == KT - 1))
                    mm.then_inc(y_in_psum, 1)

        @block.scalar
        def _(act):
            uniform = act.value_load(keep["nan_flag"][0:1, 0:1], min_val=0, max_val=1)
            with act.If(uniform > 0):
                with act.Fori(0, BATCH) as b:
                    act.wait_ge(mean_in_psum, b + 1)
                    act.activation(mean_T[:], ps_mean[:], ACT.Copy).then_inc(mean_ready, 1)

        @block.vector
        def _(dve):
            uniform = dve.value_load(keep["nan_flag"][0:1, 0:1], min_val=0, max_val=1)
            with dve.If(uniform > 0):
                dve.wait_ge(consts_ready, 33)
                with dve.Fori(0, BATCH) as b:
                    dve.wait_ge(y_in_psum, b + 1)
                    dve.tensor_tensor(y[:], ps_y[:], bo[:], ALU.add).then_inc(y_ready, 1)
                    dve.wait_ge(batch_loaded, b * 32 + 32)
                    dve.wait_ge(y_ready, b + 1)
                    for t in range(TT):
                        ins = dve.scalar_tensor_tensor(out=x_res[:, t, :], in0=y[:], scalar=keep["tanh_g"][:, 0:1], in1=x_res[:, t, :],
                                                       op0=ALU.mult, op1=ALU.add)
                    ins.then_inc(added, 1)


RING = 4
LEAD = 2
GELUS = 2
BITS = 31
SEARCH = (BITS + 1) // HT
KEPT_CHUNKS = SEARCH - 1
assert (BITS + 1) % HT == 0 and SEARCH == 4
TILES = TOKENS // P
PAIRS = EXPERTS // 2


def build_experts(nc, io, scratch, keep):
    with ExitStack() as ctx:
        n = Names(nc, ctx)
        ident = keep["ident"]
        x_hi, x_lo, out_T, gw, pick, logits = (keep[name] for name in ("x_hi", "x_lo", "out_T", "gw", "pick", "logits"))
        w_raw, raw_loaded = keep["w_raw"][:], keep["raw_loaded"]
        w1_hi = [n.sb(f"w1_hi{i}", [P, KT, HIDDEN], F32R) for i in range(2)]
        w1_lo = [n.sb(f"w1_lo{i}", [P, KT, HIDDEN], F32R) for i in range(2)]
        w2_hi = [n.sb(f"w2_hi{i}", [P, HT, DIM], F32R) for i in range(2)]
        w2_lo = [n.sb(f"w2_lo{i}", [P, HT, DIM], F32R) for i in range(2)]
        b1 = [n.sb(f"b1_{i}", [P, HT]) for i in range(2)]
        b2 = [n.sb(f"b2_{i}", [P, KT]) for i in range(2)]
        gelu = n.sb("gelu", [P, GELUS, SEQ])
        h_hi = n.sb("h_hi", [P, RING, SEQ], F32R)
        h_lo = n.sb("h_lo", [P, RING, SEQ], F32R)
        gate = [n.sb(f"gate{i}", [P, SEQ]) for i in range(2)]
        gated = n.sb("gated", [P, KT, SEQ])
        early_both = n.sb("early", [P, 2, KT * SEQ])
        early = [early_both[:, i, :].rearrange("p (k t) -> p k t", k=KT) for i in range(2)] + [gated]
        first_w2 = flat(early_both)
        x2_t = [early_both[:, i, :].rearrange("p (t d) -> p t d", d=DIM) for i in range(2)]
        xn = gated[:].rearrange("p a (b d) -> p (a b) d", d=DIM)
        logits_T = gate[0]
        zero = n.sb("zero_c", [P, 1])
        eps = n.sb("eps_c", [P, 1])
        stats = n.sb("stats_c", [P, TT, 6])
        meanvar = n.sb("meanvar_c", [P, 4, TT])
        std = n.sb("std_c", [P, TT])
        newton = n.sb("newton_c", [P, 4, TT])
        ones = n.sb("ones_c", [P, P], F32R)
        signed, below = (gate[0][:, i * P * 2:(i + 1) * P * 2].rearrange("p (e t) -> p e t", e=EXPERTS) for i in range(2))
        gates_T = gate[1][:, 0:2 * P].rearrange("p (h t) -> p h t", h=2)
        assert EXPERTS * TILES == 2 * P and SEQ == 4 * P
        count = n.sb("count", [P, 2], F32R)
        negative = n.sb("negative", [P, 1])
        sign = n.sb("sign", [P, 1])
        rank = n.sb("rank", [P, 1])
        bit = n.sb("bit", [P, 1])
        next_bit = n.sb("next_bit", [P, 1], I32)
        change = n.sb("change", [P, 1], I32)
        candidate = n.sb("candidate", [P, 1], I32)
        kth = n.sb("kth", [P, 1])
        ps_h = n.ps("ps_h", [P, RING, SEQ])
        ps_y = [n.ps(f"ps_y{i}", [P, KT, SEQ]) for i in range(2)]
        ps_l = ps_y[0]
        ps_xn, ps_x2 = ps_h[:, 0:2, :], ps_h[:, 2:4, :]

        consts_set = n.sem("c_consts_set")
        x2_loaded = [n.sem(f"c_x2_loaded{i}") for i in range(2)]
        stats_done = n.sem("c_stats_done")
        std_done = n.sem("c_std_done")
        newton_done = n.sem("c_newton_done")
        xn_ready = n.sem("c_xn_ready")
        turned = n.sem("c_turned")
        hi_done = n.sem("c_hi_done")
        lo_done = n.sem("c_lo_done")
        logits_in_psum = n.sem("c_logits_in_psum")
        logits_T_ready = n.sem("c_logits_T_ready")
        x2T_kept = n.sem("c_x2T_kept")
        picked = n.sem("c_picked")
        logits_kept = n.sem("c_logits_kept")
        counted = n.sem("d_counted")
        summed = n.sem("d_summed")
        sums_read = n.sem("d_sums_read")
        bit_set = n.sem("d_bit_set")
        candidate_set = n.sem("d_candidate_set")
        sign_set = n.sem("d_sign_set")
        gate_step = n.sem("d_gate_step")
        gates_ready = n.sem("d_gates_ready")
        gates_in_psum = n.sem("d_gates_in_psum")
        gates_T_ready = n.sem("d_gates_T_ready")
        gates_stored = n.sem("d_gates_stored")

        w2_lead_loaded = n.sem("d_w2_lead_loaded")
        lead_ready = n.sem("d_lead_ready")
        w_hi_done = n.sem("d_w_hi_done")
        w_ready = n.sem("d_w_ready")
        bias_loaded = [n.sem(f"d_bias_loaded{i}") for i in range(2)]
        gate_loaded = [n.sem(f"d_gate_loaded{i}") for i in range(2)]
        h_in_psum = n.sem("d_h_in_psum")
        gelu_done = n.sem("d_gelu_done")
        h_hi_done = n.sem("d_h_hi_done")
        h_ready = n.sem("d_h_ready")
        w2_done = n.sem("d_w2_done")
        y_taken = n.sem("d_y_taken")
        early_gated = n.sem("d_early_gated")
        added = n.sem("d_added")
        out_stored = n.sem("d_out_stored")
        block = ctx.enter_context(nc.Block())

        def tile_no(e, c, j):
            return e * (BATCH * HT) + c * HT + j

        def chunk_no(e, c):
            return e * BATCH + c

        def weight_views(p, half, raw, tiles):
            if half == 0:
                return [w[:, :, tiles.start * P:tiles.stop * P] for w in
                        (w1_hi[p], w1_lo[p], raw.rearrange("p (k h) -> p k h", k=KT))]
            return [w[:, tiles, :] for w in (w2_hi[p], w2_lo[p], raw.rearrange("p (j d) -> p j d", j=HT))]

        first_order = [KEPT_CHUNKS - 1, KEPT_CHUNKS] + list(range(KEPT_CHUNKS - 1)) + list(range(SEARCH, BATCH))
        assert all(c % 2 == i % 2 for i, c in enumerate(first_order))

        @block.sync
        def _(sp):
            def load_x2(bb, p):
                b = bb * 2 + p
                wait(sp, turned, b - 1)
                sp.dma_start(x2_t[p], scratch["x2"][bass.ds(b, 1), :].rearrange("a (t p d) -> p (a t) d", p=P, d=DIM)).then_inc(x2_loaded[p], 16)

            def load_w(e, half):
                sp.wait_ge(w_ready, e * 2 + half)
                load_weights(sp, io, w_raw, e, half).then_inc(raw_loaded[half], 16)

            def load_bias(e, p):
                sp.dma_start(b1[p][:], io["b1"][bass.ds(e, 1), :, :].rearrange("a p j -> (a p) j")).then_inc(bias_loaded[p], 16)
                sp.dma_start(b2[p][:], io["b2"][bass.ds(e, 1), :, :].rearrange("a p j -> (a p) j")).then_inc(bias_loaded[p], 16)

            def load_gate(e, c, s, order=None):
                wait(sp, added, chunk_no(e, c if order is None else order) - 1)
                src = scratch["gates"][bass.ds(chunk_no(e, c), 1), :]
                sp.dma_start(gate[s][:], src.to_broadcast([P, SEQ])).then_inc(gate_loaded[s], 16)

            clip = sp.value_load(keep["clip_flag"][0:1, 0:1], min_val=0, max_val=1)
            load_bias(0, 0)
            with sp.If(clip > 0):
                for p in range(2):
                    load_x2(0, p)
                with sp.Fori(1, BATCH // 2) as bb:
                    for p in range(2):
                        load_x2(bb, p)
                sp.wait_ge(turned, BATCH)
            w2_rows = io["w2T"][0].rearrange("(j p) d -> p j d", p=P)
            for rows, loaded in ((slice(0, LEAD), w2_lead_loaded), (slice(LEAD, HT), raw_loaded[1])):
                sp.dma_start(first_w2.rearrange("p (j d) -> p j d", j=HT)[:, rows, :], w2_rows[:, rows, :]).then_inc(loaded, 16)
            load_bias(1, 1)
            sp.wait_ge(lead_ready, 4)
            for half in range(2):
                load_w(1, half)
            sp.wait_ge(gates_T_ready, 1)
            for half in range(2):
                rows = scratch["gates"].rearrange("r (a t) -> (r a) t", t=P)[half * P:(half + 1) * P, :]
                sp.dma_start(rows, gates_T[:, half, :]).then_inc(gates_stored, 16)
            sp.wait_ge(gates_stored, 32)
            for i, c in enumerate(first_order):
                load_gate(0, c, c % 2, order=i)

            def expert(e, p):
                for c in range(2):
                    load_gate(e, c, c)
                load_bias(e + 1, 1 - p)
                for half in range(2):
                    load_w(e + 1, half)
                with sp.Fori(1, BATCH // 2) as cc:
                    for s in range(2):
                        load_gate(e, cc * 2 + s, s)

            with sp.Fori(0, PAIRS - 1) as pair:
                for i in range(2):
                    expert(pair * 2 + i + 1, 1 - i)

            def store(c):
                sp.wait_ge(added, chunk_no(EXPERTS - 1, c) + 1)
                sp.dma_start(io["out_T"].rearrange("(k p) t -> p k t", p=P)[:, :, bass.ds(c * SEQ, SEQ)],
                             out_T[:, :, bass.ds(c * SEQ, SEQ)]).then_inc(out_stored, 16)

            for c in range(2):
                load_gate(EXPERTS - 1, c, c)
            for c in range(BATCH):
                store(c)
                if c + 2 < BATCH:
                    load_gate(EXPERTS - 1, c + 2, c % 2)
            sp.wait_ge(out_stored, 16 * BATCH)

        @block.gpsimd
        def _(pool):
            pool.memset(zero[:], 0.0).then_inc(consts_set, 1)
            pool.memset(count[:].bitcast(F32), 0.0).then_inc(consts_set, 1)
            pool.memset(ones[:].bitcast(F32), 1.0).then_inc(consts_set, 1)
            pool.memset(bit[:], float(1 << BITS)).then_inc(consts_set, 1)
            pool.memset(next_bit[:], 1 << (BITS - 1)).then_inc(consts_set, 1)
            pool.memset(candidate[:], 1 << (BITS - 1)).then_inc(consts_set, 1)
            pool.memset(eps[:], EPS).then_inc(consts_set, 1)
            pool.wait_ge(consts_set, 7)

            def split(e, p, half, skip=0):
                at = e * 2 + half
                pool.wait_ge(raw_loaded[half], e * 16 + 16)
                if half == 0:
                    wait(pool, w2_done, tile_no(e, 0, 0) - BATCH * HT + RING if not isinstance(e, int) or e >= 2 else 0)
                raw = first_w2 if half == 1 and isinstance(e, int) and e == 0 else w_raw
                hi, lo, raw = weight_views(p, half, raw, slice(skip, HT))
                pool.tensor_tensor(hi, raw, zero[:].to_broadcast(hi.shape), ALU.add).then_inc(w_hi_done, 1)
                pool.wait_ge(w_hi_done, at + 1)
                pool.tensor_tensor(lo, raw, hi.bitcast(F32), ALU.subtract).then_inc(w_ready, 1)

            for half in range(2):
                split(0, 0, half, skip=2 * LEAD if half == 0 else LEAD)
            for half in range(2):
                split(1, 1, half)
            with pool.Fori(1, PAIRS) as pair:
                for p in range(2):
                    for half in range(2):
                        split(pair * 2 + p, p, half)

        @block.tensor
        def _(pe):
            pe.wait_ge(consts_set, 7)

            clip = pe.value_load(keep["clip_flag"][0:1, 0:1], min_val=0, max_val=1)
            with pe.If(clip > 0):
                def turn(bb, p):
                    b = bb * 2 + p
                    pe.wait_ge(x2_loaded[p], bb * 16 + 16)
                    pe.wait_ge(x2T_kept, b)
                    for k in range(KT):
                        for t in range(TT):
                            pe.transpose(ps_x2[:, k, t * P:(t + 1) * P], x2_t[p][:, t, k * P:(k + 1) * P], ident[:])
                    pe.wait_ge(xn_ready, b + 1)
                    pe.wait_ge(lo_done, b)
                    for k in range(KT):
                        for t in range(TT):
                            mm = pe.transpose(ps_xn[:, k, t * P:(t + 1) * P], xn[:, t, k * P:(k + 1) * P], ident[:])
                    mm.then_inc(turned, 1)
                    pe.wait_ge(logits_T_ready, b)
                    pe.wait_ge(lo_done, b + 1)
                    for i, (part, k) in enumerate((part, k) for k in range(KT) for part in (x_hi, x_lo)):
                        mm = pe.matmul(ps_l[:, 0, :], gw[:, k, :], part[:, k, bass.ds(b * SEQ, SEQ)],
                                       start=(i == 0), stop=(i == 2 * KT - 1))
                    mm.then_inc(logits_in_psum, 1)
                    pe.wait_ge(logits_kept, b)
                    pe.wait_ge(logits_T_ready, b + 1)
                    for t in range(TT):
                        mm = pe.matmul(ps_l[:, 1, t * EXPERTS:(t + 1) * EXPERTS], logits_T[:, t * P:(t + 1) * P], pick[:],
                                       start=True, stop=True)
                    mm.then_inc(picked, 1)

                with pe.Fori(0, BATCH // 2) as bb:
                    for p in range(2):
                        turn(bb, p)
                pe.wait_ge(x2T_kept, BATCH)

            pe.sem_inc(w2_done, RING)

            def first(e, p, c, j):
                pe.wait_ge(gelu_done, tile_no(e, c, j) + 1)
                at = slice(j * P, (j + 1) * P)
                parts = [(w, x, k) for k in range(KT)
                         for w, x in ((w1_hi[p], x_hi), (w1_hi[p], x_lo), (w1_lo[p], x_hi))]
                for i, (w, x, k) in enumerate(parts):
                    mm = pe.matmul(ps_h[:, j % RING, :], w[:, k, at], x[:, k, bass.ds(c * SEQ, SEQ)],
                                   start=(i == 0), stop=(i == len(parts) - 1))
                mm.then_inc(h_in_psum, 1)

            def second(e, p, c, j, s):
                if j == 0:
                    if isinstance(e, int) and e == 0:
                        pe.wait_ge(lead_ready, 6)
                    pe.wait_ge(y_taken, chunk_no(e, c) + 1)
                pe.wait_ge(h_ready, tile_no(e, c, j) + 1 + RING)
                for d in range(KT):
                    at = slice(d * P, (d + 1) * P)
                    for i, (w, h) in enumerate(((w2_hi[p], h_hi), (w2_hi[p], h_lo), (w2_lo[p], h_hi))):
                        mm = pe.matmul(ps_y[s][:, d, :], w[:, j, at], h[:, j % RING, :],
                                       start=(j == 0 and i == 0), stop=(j == HT - 1 and i == 2))
                mm.then_inc(w2_done, 1)

            def chunk(e, p, c, s, ahead, before=None, after=None):
                for j in range(HT):
                    if j + LEAD < HT:
                        if before:
                            before(c, j + LEAD)
                        first(e, p, c, j + LEAD)
                    elif ahead:
                        ahead(j + LEAD - HT)
                    second(e, p, c, j, s)
                    if after:
                        after(c, j)

            def start(e, p, j):
                if j == 0:
                    pe.wait_ge(w_ready, e * 2 + 2)
                first(e, p, 0, j)

            def expert(e, p, last):
                with pe.Fori(0, BATCH // 2 - 1) as cc:
                    for s in range(2):
                        chunk(e, p, cc * 2 + s, s, lambda j: first(e, p, cc * 2 + s + 1, j))
                chunk(e, p, BATCH - 2, 0, lambda j: first(e, p, BATCH - 1, j))
                chunk(e, p, BATCH - 1, 1, None if last else lambda j: start(e + 1, 1 - p, j))

            def sums_gone(c, j):
                pe.wait_ge(sums_read, tile_no(0, c, j) + 1)

            def sum_round(c, j):
                pe.wait_ge(counted, tile_no(0, c, j) + 1)
                pe.matmul(ps_h[:, j % RING, 0:2], ones[:], count[:], start=True, stop=True).then_inc(summed, 1)

            def search_chunk(c, s):
                def before(c, j):
                    if j == LEAD:
                        pe.wait_ge(lead_ready, 4)
                    if j == 2 * LEAD:
                        pe.wait_ge(w_ready, 1)
                    sums_gone(c, j)

                def ahead(j):
                    sums_gone(c + 1, j)
                    first(0, 0, c + 1, j)

                def after(c, j):
                    sum_round(c, j)
                    if j == LEAD - 1:
                        pe.wait_ge(w_ready, 2)

                chunk(0, 0, c, s, ahead, before, after)

            def gates_chunk(c, s):
                def before(c, j):
                    if j < RING:
                        sums_gone(c, j)
                    elif j == RING:
                        pe.wait_ge(gates_T_ready, 1)

                def after(c, j):
                    if j == 0:
                        pe.wait_ge(gates_ready, 1)
                        for half in range(2):
                            mm = pe.transpose(ps_h[:, 0, half * P:(half + 1) * P],
                                              signed[:, half * 4:half * 4 + 4, :].rearrange("p e t -> p (e t)"), ident[:])
                        mm.then_inc(gates_in_psum, 1)

                chunk(0, 0, c, s, lambda j: first(0, 0, c + 1, j), before, after)

            pe.wait_ge(lead_ready, 2)
            for j in range(LEAD):
                first(0, 0, 0, j)
            with pe.Fori(0, SEARCH // 2) as cc:
                for s in range(2):
                    search_chunk(cc * 2 + s, s)
            gates_chunk(SEARCH, 0)
            for c in range(SEARCH + 1, BATCH - 1):
                chunk(0, 0, c, c % 2, lambda j: first(0, 0, c + 1, j))
            chunk(0, 0, BATCH - 1, 1, lambda j: start(1, 1, j))
            with pe.Fori(0, PAIRS - 1) as pair:
                for i in range(2):
                    expert(pair * 2 + i + 1, 1 - i, False)
            expert(EXPERTS - 1, 1, True)

        @block.scalar
        def _(act):
            act.wait_ge(consts_set, 7)
            act.sem_inc(gelu_done, RING)
            clip = act.value_load(keep["clip_flag"][0:1, 0:1], min_val=0, max_val=1)
            with act.If(clip > 0):
                with act.Fori(0, BATCH) as b:
                    act.wait_ge(stats_done, b * 4 + 4)
                    act.activation(std[:], meanvar[:, 1, :], ACT.Sqrt, bias=eps[:, 0:1]).then_inc(std_done, 1)
                    act.wait_ge(picked, b)
                    act.wait_ge(logits_in_psum, b + 1)
                    act.activation(logits_T[:], ps_l[:, 0, :], ACT.Copy).then_inc(logits_T_ready, 1)
                    act.activation(out_T[:, :, bass.ds(b * SEQ, SEQ)], ps_x2, ACT.Copy).then_inc(x2T_kept, 1)
            def gelu_tile(e, p, c, j):
                act.wait_ge(h_ready, tile_no(e, c, j) + 1 + RING - GELUS)
                act.wait_ge(h_in_psum, tile_no(e, c, j) + 1)
                act.activation(gelu[:, j % GELUS, :], ps_h[:, j % RING, :], ACT.Gelu_apprx_tanh,
                               bias=b1[p][:, j:j + 1]).then_inc(gelu_done, 1)

            def keep_early(c):
                act.wait_ge(w2_done, tile_no(0, c, HT) + RING)
                for d in range(KT):
                    ins = act.activation(early[c][:, d, :], ps_y[c % 2][:, d, :], ACT.Identity, bias=b2[0][:, d:d + 1])
                ins.then_inc(y_taken, 1)

            act.wait_ge(bias_loaded[0], 32)
            for c in range(SEARCH + 1):
                for j in range(HT):
                    gelu_tile(0, 0, c, j)
                    if 0 < c < SEARCH and j == RING - 1:
                        keep_early(c - 1)
                    if c == SEARCH and j == LEAD:
                        act.wait_ge(gates_in_psum, 1)
                        act.activation(gates_T[:].rearrange("p h t -> p (h t)"), ps_h[:, 0, 0:2 * P], ACT.Copy).then_inc(gates_T_ready, 1)
            with act.Fori(SEARCH + 1, BATCH) as c:
                for j in range(HT):
                    gelu_tile(0, 0, c, j)

            def expert(e, p, loads):
                act.wait_ge(bias_loaded[p], loads * 32)
                with act.Fori(0, BATCH) as c:
                    for j in range(HT):
                        gelu_tile(e, p, c, j)

            with act.Fori(0, PAIRS - 1) as pair:
                for i in range(2):
                    expert(pair * 2 + i + 1, 1 - i, pair + 1 + i)
            expert(EXPERTS - 1, 1, PAIRS)

        @block.vector
        def _(dve):
            def split_lead(n, half, raw, loaded, tiles):
                hi, lo, raw = weight_views(0, half, raw, tiles)
                dve.wait_ge(loaded, 16)
                dve.tensor_copy(hi, raw).then_inc(lead_ready, 1)
                dve.wait_ge(lead_ready, n * 2 + 1)
                dve.tensor_tensor(lo, raw, hi.bitcast(F32), ALU.subtract).then_inc(lead_ready, 1)

            for n in range(2):
                split_lead(n, 0, w_raw, raw_loaded[0], slice(n * LEAD, (n + 1) * LEAD))

            dve.wait_ge(consts_set, 7)
            clip = dve.value_load(keep["clip_flag"][0:1, 0:1], min_val=0, max_val=1)
            with dve.If(clip > 0):
                def normalise(bb, p):
                    b = bb * 2 + p
                    dve.wait_ge(x2_loaded[p], bb * 16 + 16)
                    dve.wait_ge(xn_ready, b)
                    mean_variance(dve, [x2_t[p][:, t, :] for t in range(TT)], stats, meanvar, stats_done, b)
                    dve.wait_ge(std_done, b + 1)
                    rstd = reciprocal_root(dve, std[:], meanvar[:, 1, :], newton, newton_done, b)
                    dve.wait_ge(turned, b)
                    for t in range(TT):
                        ins = dve.tensor_scalar(xn[:, t, :], x2_t[p][:, t, :], meanvar[:, 0, t:t + 1], rstd[:, t:t + 1],
                                                ALU.subtract, ALU.mult)
                    ins.then_inc(xn_ready, 1)

                def split(b):
                    at = bass.ds(b * SEQ, SEQ)
                    dve.wait_ge(turned, b + 1)
                    dve.tensor_scalar(x_hi[:, :, at], ps_xn, 1.0, None, ALU.mult).then_inc(hi_done, 1)
                    dve.wait_ge(hi_done, b + 1)
                    dve.tensor_tensor(x_lo[:, :, at], ps_xn, x_hi[:, :, at].bitcast(F32), ALU.subtract).then_inc(lo_done, 1)

                def keep_logits(b):
                    dve.wait_ge(picked, b + 1)
                    dve.tensor_scalar(logits[:, :, bass.ds(b * TT, TT)],
                                      ps_l[:, 1, 0:TT * EXPERTS].rearrange("p (t e) -> p e t", t=TT),
                                      1.0, None, ALU.mult).then_inc(logits_kept, 1)

                normalise(0, 0)
                with dve.Fori(0, BATCH // 2 - 1) as bb:
                    for p in range(2):
                        split(bb * 2 + p)
                        normalise(bb + p, 1 - p)
                        keep_logits(bb * 2 + p)
                split(BATCH - 2)
                normalise(BATCH // 2 - 1, 1)
                keep_logits(BATCH - 2)
                split(BATCH - 1)
                keep_logits(BATCH - 1)
                dve.wait_ge(logits_kept, BATCH)

            dve.sem_inc(h_ready, RING)
            dve.sem_inc(y_taken, 2)
            dve.sem_inc(sums_read, RING)

            def split_hi(at, j):
                dve.wait_ge(w2_done, at + 1)
                dve.wait_ge(gelu_done, at + 1 + RING)
                dve.tensor_copy(h_hi[:, j % RING, :], gelu[:, j % GELUS, :]).then_inc(h_hi_done, 1)

            def split_lo(at, j):
                dve.wait_ge(h_hi_done, at + 1)
                dve.tensor_tensor(h_lo[:, j % RING, :], gelu[:, j % GELUS, :], h_hi[:, j % RING, :].bitcast(F32),
                                  ALU.subtract).then_inc(h_ready, 1)

            def halves(e, c, j):
                split_hi(tile_no(e, c, j), j)
                split_lo(tile_no(e, c, j), j)

            total = EXPERTS * TOKENS
            dve.tensor_scalar(below[:], logits[:], 0.0, None, ALU.is_lt, ALU.add, accum_out=count[:, 0:1]).then_inc(counted, 1)
            split_lead(2, 1, first_w2, w2_lead_loaded, slice(0, LEAD))
            for j in range(LEAD):
                halves(0, 0, j)
            dve.wait_ge(summed, 1)
            dve.tensor_scalar(negative[:], ps_h[:, 0, 0:1], KEPT_FROM + 0.5, None, ALU.is_gt).then_inc(sums_read, 1)
            split_hi(LEAD, LEAD)
            dve.wait_ge(sums_read, RING + 1)
            dve.tensor_scalar(sign[:], negative[:], -2.0, 1.0, ALU.mult, ALU.add).then_inc(sign_set, 1)
            dve.tensor_scalar(rank[:], negative[:], float(total - 1 - 2 * KEPT_FROM), float(KEPT_FROM),
                              ALU.mult, ALU.add).then_inc(sign_set, 1)
            split_lo(LEAD, LEAD)
            dve.wait_ge(sign_set, 2)
            dve.tensor_scalar(signed[:], logits[:], sign[:, 0:1], None, ALU.mult).then_inc(candidate_set, 1)

            def search_round(i, slot):
                dve.wait_ge(candidate_set, i)
                dve.tensor_scalar(below[:], signed[:], candidate[:].bitcast(F32), None, ALU.is_lt, ALU.add,
                                  accum_out=count[:, 0:1]).then_inc(counted, 1)
                dve.tensor_scalar(bit[:], bit[:], 0.5, None, ALU.mult)
                dve.tensor_scalar(next_bit[:], next_bit[:], 1, None, ALU.logical_shift_right).then_inc(bit_set, 1)
                dve.wait_ge(bit_set, i)
                dve.wait_ge(summed, i + 1)
                dve.tensor_scalar(change[:], ps_h[:, slot, 0:1], rank[:, 0:1], bit[:, 0:1], ALU.is_gt, ALU.mult).then_inc(sums_read, 1)
                split_hi(i + LEAD, (slot + LEAD) % RING)
                dve.wait_ge(sums_read, i + 1 + RING)
                dve.scalar_tensor_tensor(out=candidate[:], in0=change[:], scalar=next_bit[:, 0:1], in1=candidate[:],
                                         op0=ALU.bitwise_or, op1=ALU.bitwise_xor).then_inc(candidate_set, 1)
                split_lo(i + LEAD, (slot + LEAD) % RING)

            with dve.Fori(0, BITS // RING) as turn:
                for i in range(RING):
                    search_round(turn * RING + i + 1, (i + 1) % RING)
            for i in range(BITS // RING * RING + 1, BITS + 1):
                search_round(i, i % RING)
            dve.wait_ge(candidate_set, BITS + 1)
            dve.tensor_tensor(kth[:], candidate[:].bitcast(F32), sign[:], ALU.mult).then_inc(gate_step, 1)
            dve.wait_ge(gate_step, 1)
            dve.scalar_tensor_tensor(out=below[:], in0=logits[:], scalar=kth[:, 0:1], in1=logits[:],
                                     op0=ALU.is_ge, op1=ALU.mult).then_inc(gate_step, 1)
            dve.wait_ge(gate_step, 2)
            dve.tensor_scalar(signed[:], below[:], keep["tanh_g"][:, 1:2], None, ALU.mult).then_inc(gates_ready, 1)

            def add_chunk(e, p, c, s, order=None):
                n = chunk_no(e, c if order is None else order)
                dve.wait_ge(gate_loaded[s], (n - s) * 8 + 16)
                wait(dve, added, n)
                dve.wait_ge(w2_done, tile_no(e, c, HT) + RING)
                for d in range(KT):
                    ins = dve.scalar_tensor_tensor(out=gated[:, d, :], in0=ps_y[s][:, d, :], scalar=b2[p][:, d:d + 1],
                                                   in1=gate[s][:], op0=ALU.add, op1=ALU.mult)
                ins.then_inc(y_taken, 1)
                dve.wait_ge(y_taken, chunk_no(e, c) + 3)
                part = out_T[:, :, bass.ds(c * SEQ, SEQ)]
                dve.tensor_tensor(part, part, gated[:], ALU.add).then_inc(added, 1)

            def add_early(c, order):
                dve.wait_ge(gate_loaded[c % 2], order // 2 * 16 + 16)
                dve.wait_ge(y_taken, c + 3)
                for d in range(KT):
                    ins = dve.tensor_tensor(early[c][:, d, :], early[c][:, d, :], gate[c % 2][:], ALU.mult)
                ins.then_inc(early_gated, 1)
                wait(dve, added, order)
                dve.wait_ge(early_gated, max(order, 1))
                part = out_T[:, :, c * SEQ:(c + 1) * SEQ]
                dve.tensor_tensor(part, part, early[c][:], ALU.add).then_inc(added, 1)

            def chunk(e, c, before, tiles=range(HT)):
                for j in tiles:
                    halves(e, c, j)
                    if j == LEAD and before:
                        before()

            def expert(e, p):
                chunk(e, 0, lambda: add_chunk(e - 1, 1 - p, BATCH - 1, 1))
                chunk(e, 1, lambda: add_chunk(e, p, 0, 0))
                with dve.Fori(1, BATCH // 2) as cc:
                    for s in range(2):
                        chunk(e, cc * 2 + s, lambda: add_chunk(e, p, cc * 2 + s - 1, 1 - s))

            chunk(0, SEARCH, None, range(LEAD, HT - SEARCH + 1))
            for i, c in enumerate(first_order[:SEARCH]):
                j = HT - SEARCH + 1 + i
                halves(0, SEARCH + j // HT, j % HT)
                if c < KEPT_CHUNKS:
                    add_early(c, i)
                else:
                    add_chunk(0, 0, c, c % 2, order=i)
            chunk(0, SEARCH + 1, lambda: add_chunk(0, 0, SEARCH, 0), range(1, HT))
            for c in range(SEARCH + 2, BATCH):
                chunk(0, c, lambda: add_chunk(0, 0, c - 1, (c - 1) % 2))
            with dve.Fori(0, PAIRS - 1) as pair:
                for i in range(2):
                    expert(pair * 2 + i + 1, 1 - i)
            expert(EXPERTS - 1, 1)
            add_chunk(EXPERTS - 1, 1, BATCH - 1, 1)


def build(nc, io):
    with ExitStack() as ctx:
        n = Names(nc, ctx)
        keep = {"ident": n.sb("ident", [P, P]), "tanh_g": n.sb("tanh_g", [P, 2]), "clip_flag": n.sb("clip_flag", [P, 1], I32)}
        keep["nan_flag"] = n.sb("nan_flag", [P, 1], I32)

        def scratch_of(name, shape):
            return nc.dram_tensor(name, shape, F32).ap()

        scratch = {
            "q": scratch_of("q_scratch", (BATCH, HEADS * KEPT, SEQ)),
            "k": scratch_of("k_scratch", (BATCH, HEADS * KEPT, SEQ)),
            "v": scratch_of("v_scratch", (BATCH, P, TT * HEADS * VW)),
            "x2": scratch_of("x2_scratch", (TOKENS, DIM)),
            "gates": scratch_of("gates_scratch", (EXPERTS * BATCH, SEQ)),
        }
        keep["w_raw"] = n.sb("w_raw", [P, KT * HIDDEN], F32, "right")
        keep["raw_loaded"] = [n.sem(f"w{i}_raw_loaded") for i in (1, 2)]
        assert GROUP * SEQ == KT * HIDDEN == HT * DIM
        with ExitStack() as loads_ctx:
            loads = Names(nc, loads_ctx)
            keep["q_st"] = [loads.sb(f"q_st{i}", [P, GROUP // 2, SEQ], F32R, "right") for i in range(GROUPS)]
            keep["k_st"] = [loads.sb(f"k_st{i}", [P, GROUP, SEQ], F32R, "right") for i in range(GROUPS)]
            keep["wo"] = loads.sb("wo", [P, KT, DIM], F32, "right")
            keep["stored"] = [loads.sem(f"a_stored{i}") for i in range(2)]
            build_project(nc, io, scratch, keep)
            for name in ("x_hi", "x_lo"):
                keep[name] = n.sb(name, [P, KT, TOKENS], F32R)
            keep["out_T"] = n.sb("out_T_acc", [P, KT, TOKENS])
            keep["gw"] = n.sb("gw", [P, KT, P], F32R)
            keep["pick"] = n.sb("pick", [P, EXPERTS])
            keep["logits"] = n.sb("logits", [P, EXPERTS, TILES])
            build_attend(nc, io, scratch, keep)
        build_attend_clipped(nc, io, scratch, keep)
        build_attend_uniform(nc, io, scratch, keep)
        scratch["x2"] = scratch["x2"].rearrange("(b s) d -> b (s d)", b=BATCH)
        build_experts(nc, io, scratch, keep)


def kernel(**inputs):
    import numpy as np
    import concourse.bacc as bacc
    from concourse.bass_utils import run_bass_kernel_spmd

    a = {k: np.asarray(v) for k, v in inputs.items()}
    attn = {w: a[f"L0_xattn_{w}"] for w in ("Wq", "bq", "Wk", "bk", "Wv", "bv", "Wo", "bo")}
    arrays = {
        "x": a["x"].reshape(TOKENS, DIM),
        "ctxT": a["ctx_768"].transpose(0, 2, 1),
        "g_xattn": a["g_xattn"],
        "g_ffn": a["g_ffn"],
        **attn,
        "bq": attn["bq"].reshape(KT, P).T,
        "gwT": a["L0_ffn_gate_weight"].T,
        "w1T": a["L0_ffn_w1"].transpose(0, 2, 1),
        "b1": a["L0_ffn_b1"].reshape(EXPERTS, HT, P).transpose(0, 2, 1),
        "w2T": a["L0_ffn_w2"].transpose(0, 2, 1),
        "b2": a["L0_ffn_b2"].reshape(EXPERTS, KT, P).transpose(0, 2, 1),
    }
    nc = bacc.Bacc("TRN2", target_bir_lowering=False, num_devices=1)
    io, feeds = {}, {}
    for name, array in arrays.items():
        feeds[f"in_{name}"] = np.ascontiguousarray(array)
        io[name] = nc.dram_tensor(f"in_{name}", array.shape, mybir.dt.from_np(array.dtype), kind="ExternalInput").ap()
    io["out_T"] = nc.dram_tensor("out_T", (DIM, TOKENS), F32, kind="ExternalOutput").ap()
    build(nc, io)
    result = run_bass_kernel_spmd(nc, [feeds], core_ids=[0])
    return np.ascontiguousarray(result.results[0]["out_T"].T).reshape(BATCH, SEQ, DIM)
```
